# Optimizing a Trainium2 kernel written in Bass

```python
import numpy as np
import jax
import jax.numpy as jnp

def _softmax(x, axis=-1):
    return jax.nn.softmax(x, axis=axis)

def _gelu(x):
    return jax.nn.gelu(x, approximate=True)

def _silu(x):
    return jax.nn.silu(x)

def _sigmoid(x):
    return jax.nn.sigmoid(x)

def _layernorm(x, axis=-1, eps=1e-05):
    m = jnp.mean(x, axis=axis, keepdims=True)
    v = jnp.var(x, axis=axis, keepdims=True)
    return (x - m) / jnp.sqrt(v + eps)

def _scatter_add(tgt, idx, src, axis=0):
    return tgt.at[idx].add(src)

def _segment_sum(src, seg, n):
    return jax.ops.segment_sum(src, seg, n)
kernel_name = 'mk_adj_ffn_d2_adj_r2_3a65e1'

def setup_inputs(seed: int=0):
    np.random.seed(seed)
    _w = jnp.asarray

    def _rec_inputs():
        import jax
        import jax.numpy as jnp
        _gk = jax.random.key(seed)
        x = -0.0005207 + 1.001 * jax.random.normal(jax.random.fold_in(_gk, 1), (4096, 128), jnp.float32)
        _a = jax.random.bernoulli(jax.random.fold_in(_gk, 2), 0.000488281, (4096, 4096))
        _a = jnp.logical_or(_a, jnp.eye(4096, dtype=bool))
        _af = _a.astype(jnp.float32)
        adj = _af
        return (x, adj)
    x, adj = _rec_inputs()

    def _L0_gnn_setup():
        import jax, jax.numpy as jnp
        import numpy as np
        N = 4096
        F = 128
        NEG_INF = -9000000000000000.0
        ALPHA = 0.2
        THRESH = 1e-06
        key = jax.random.key(seed)
        k1, k2, k3, k4 = jax.random.split(key, 4)
        x = jax.random.normal(k1, (N, F), jnp.float32)
        h0 = jax.random.normal(k2, (N, F), jnp.float32)
        limit = float(np.sqrt(6.0 / (2 * F + 1)) * 1.414)
        a = jax.random.uniform(k3, (2 * F, 1), jnp.float32, -limit, limit)
        temp = jnp.zeros((5,), jnp.float32)
        adj = jax.random.bernoulli(k4, 0.005, (N, N)).astype(jnp.float32)
        adj = jnp.maximum(adj, jnp.eye(N, dtype=jnp.float32))
        return {'x': x, 'h0': h0, 'a': a, 'temp': temp, 'adj': adj, 'l': 1}
    _L0_gnn_all = _L0_gnn_setup()
    _L0_gnn_in = {k: v for k, v in _L0_gnn_all.items() if k in ('h0', 'a', 'temp')}
    del _L0_gnn_all

    def _L0_ffn_setup():
        import jax, jax.numpy as jnp
        import numpy as np
        TOP_K = 2
        key = jax.random.key(seed)
        ks = jax.random.split(key, 4)
        B, L, D, H, E = (8, 2048, 128, 512, 8)
        s = 0.02
        return {'x': jax.random.normal(ks[0], (B, L, D), jnp.float32), 'Wg': jax.random.normal(ks[1], (D, E), jnp.float32) * s, 'bg': jnp.zeros((E,), jnp.float32), 'W1': jax.random.normal(ks[2], (E, D, H), jnp.float32) * s, 'b1': jnp.zeros((E, H), jnp.float32), 'W2': jax.random.normal(ks[3], (E, H, D), jnp.float32) * s, 'b2': jnp.zeros((E, D), jnp.float32)}
    _L0_ffn_all = _L0_ffn_setup()
    _L0_ffn_in = {k: v for k, v in _L0_ffn_all.items() if k in ('Wg', 'bg', 'W1', 'b1', 'W2', 'b2')}
    del _L0_ffn_all

    def _L1_gnn_setup():
        import jax, jax.numpy as jnp
        import numpy as np
        N = 4096
        F_IN = 128
        F_OUT = 128
        key = jax.random.key(seed)
        k_x, k_adj, k_kernel, k_bias, k_beta = jax.random.split(key, 5)
        x = jax.random.normal(k_x, (N, F_IN), dtype=jnp.float32)
        adj = jax.random.uniform(k_adj, (N, N), dtype=jnp.float32)
        limit = float(np.sqrt(6.0 / (F_IN + F_OUT)))
        kernel = jax.random.uniform(k_kernel, (F_IN, F_OUT), dtype=jnp.float32, minval=-limit, maxval=limit)
        bias = 0.01 * jax.random.normal(k_bias, (F_OUT,), dtype=jnp.float32)
        beta = 0.01 * jax.random.normal(k_beta, (N,), dtype=jnp.float32)
        return {'x': x, 'adj': adj, 'kernel': kernel, 'bias': bias, 'beta': beta}
    _L1_gnn_all = _L1_gnn_setup()
    _L1_gnn_in = {k: v for k, v in _L1_gnn_all.items() if k in ('kernel', 'bias', 'beta')}
    del _L1_gnn_all

    def _L1_ffn_setup():
        import jax, jax.numpy as jnp
        import numpy as np
        B, S, D, F, E, K = (8, 1024, 128, 512, 8, 2)
        key = jax.random.key(seed)
        ks = jax.random.split(key, 10)
        s = 0.02
        return {'x': jax.random.normal(ks[0], (B, S, D), dtype=jnp.float32), 'Wr': jax.random.normal(ks[1], (D, E), dtype=jnp.float32) * s, 'W1s': jax.random.normal(ks[2], (D, F), dtype=jnp.float32) * s, 'b1s': jnp.zeros((F,), dtype=jnp.float32), 'W2s': jax.random.normal(ks[3], (F, D), dtype=jnp.float32) * s, 'b2s': jnp.zeros((D,), dtype=jnp.float32), 'W1p': jax.random.normal(ks[4], (E, D, F), dtype=jnp.float32) * s, 'b1p': jnp.zeros((E, F), dtype=jnp.float32), 'W2p': jax.random.normal(ks[5], (E, F, D), dtype=jnp.float32) * s, 'b2p': jnp.zeros((E, D), dtype=jnp.float32)}
    _L1_ffn_all = _L1_ffn_setup()
    _L1_ffn_in = {k: v for k, v in _L1_ffn_all.items() if k in ('Wr', 'W1s', 'b1s', 'W2s', 'b2s', 'W1p', 'b1p', 'W2p', 'b2p')}
    del _L1_ffn_all
    return {'x': x, 'adj': adj, 'L0_gnn_h0': _L0_gnn_in['h0'], 'L0_gnn_a': _L0_gnn_in['a'], 'L0_gnn_temp': _L0_gnn_in['temp'], 'L0_ffn_Wg': _L0_ffn_in['Wg'], 'L0_ffn_bg': _L0_ffn_in['bg'], 'L0_ffn_W1': _L0_ffn_in['W1'], 'L0_ffn_b1': _L0_ffn_in['b1'], 'L0_ffn_W2': _L0_ffn_in['W2'], 'L0_ffn_b2': _L0_ffn_in['b2'], 'L1_gnn_kernel': _L1_gnn_in['kernel'], 'L1_gnn_bias': _L1_gnn_in['bias'], 'L1_gnn_beta': _L1_gnn_in['beta'], 'L1_ffn_Wr': _L1_ffn_in['Wr'], 'L1_ffn_W1s': _L1_ffn_in['W1s'], 'L1_ffn_b1s': _L1_ffn_in['b1s'], 'L1_ffn_W2s': _L1_ffn_in['W2s'], 'L1_ffn_b2s': _L1_ffn_in['b2s'], 'L1_ffn_W1p': _L1_ffn_in['W1p'], 'L1_ffn_b1p': _L1_ffn_in['b1p'], 'L1_ffn_W2p': _L1_ffn_in['W2p'], 'L1_ffn_b2p': _L1_ffn_in['b2p']}

def reference(x, adj, L0_gnn_h0, L0_gnn_a, L0_gnn_temp, L0_ffn_Wg, L0_ffn_bg, L0_ffn_W1, L0_ffn_b1, L0_ffn_W2, L0_ffn_b2, L1_gnn_kernel, L1_gnn_bias, L1_gnn_beta, L1_ffn_Wr, L1_ffn_W1s, L1_ffn_b1s, L1_ffn_W2s, L1_ffn_b2s, L1_ffn_W1p, L1_ffn_b1p, L1_ffn_W2p, L1_ffn_b2p):
    import jax
    import jax.numpy as jnp

    def _L0_gnn_ref(x, h0, a, temp, adj, l):
        import jax, jax.numpy as jnp
        import numpy as np
        N = 4096
        F = 128
        NEG_INF = -9000000000000000.0
        ALPHA = 0.2
        THRESH = 1e-06
        Fdim = x.shape[1]
        feat_1 = x @ a[:Fdim]
        feat_2 = x @ a[Fdim:]
        e = jax.nn.leaky_relu(feat_1 + feat_2.T, ALPHA)
        att = jnp.where(adj > 0, e, NEG_INF)
        U = jax.nn.softmax(att, axis=1)
        P = 0.5 * U
        prop_u = U @ x
        rowsum = jnp.sum(U * P, axis=1)
        coe = jax.nn.sigmoid(temp)
        xi = x * rowsum[:, None]
        feat_odd = prop_u - xi
        feat_even = x + prop_u - xi
        feat = coe[2] * feat_odd + (1.0 - coe[2]) * feat_even
        sgn = jnp.sign(feat)
        mod = jnp.abs(feat)
        mod = jnp.where(mod > THRESH, mod - THRESH, 0.0)
        feat = mod * sgn
        pu = U @ feat
        feat_odd2 = feat - coe[3] * pu
        feat_even2 = pu + feat_odd2 * rowsum[:, None]
        feat_odd2 = coe[0] * feat_odd2 + (1.0 - coe[0]) * h0
        out = coe[1] * feat_even2 + (1.0 - coe[1]) * feat_odd2
        return out

    def _L0_ffn_ref(x, Wg, bg, W1, b1, W2, b2):
        import jax, jax.numpy as jnp
        import numpy as np
        TOP_K = 2
        B, L, D = x.shape
        E = W1.shape[0]
        xf = x.reshape(-1, D)
        gate_logits = xf @ Wg + bg
        top_w, top_i = jax.lax.top_k(gate_logits, TOP_K)
        top_w = jax.nn.softmax(top_w, axis=-1)
        w_dense = jnp.sum(jax.nn.one_hot(top_i, E, dtype=xf.dtype) * top_w[..., None], axis=1)
        out = jnp.zeros_like(xf)
        for e in range(E):
            h = jax.nn.gelu(xf @ W1[e] + b1[e], approximate=False)
            out = out + w_dense[:, e:e + 1] * (h @ W2[e] + b2[e])
        return out.reshape(B, L, D)

    def _L1_gnn_ref(x, adj, kernel, bias, beta):
        import jax, jax.numpy as jnp
        import numpy as np
        N = 4096
        F_IN = 128
        F_OUT = 128
        scale = jnp.reciprocal(jnp.sum(adj, axis=1) + beta)
        agg = adj @ x + beta[:, None] * x
        return scale[:, None] * agg @ kernel + bias

    def _L1_ffn_ref(x, Wr, W1s, b1s, W2s, b2s, W1p, b1p, W2p, b2p):
        import jax, jax.numpy as jnp
        import numpy as np
        B, S, D, F, E, K = (8, 1024, 128, 512, 8, 2)
        gelu = lambda t: jax.nn.gelu(t, approximate=False)
        shared = gelu(x @ W1s + b1s) @ W2s + b2s
        rw = jax.nn.softmax(x @ Wr, axis=-1)
        topw, topi = jax.lax.top_k(rw, K)
        topw = topw / jnp.sum(topw, axis=-1, keepdims=True)
        mask = jnp.sum(jax.nn.one_hot(topi, E, dtype=topw.dtype) * topw[..., None], axis=-2)
        h = gelu(jnp.einsum('bsd,edf->bsef', x, W1p) + b1p)
        priv = jnp.einsum('bsef,efd->bsed', h, W2p) + b2p
        routed = jnp.einsum('bsed,bse->bsd', priv, mask)
        return shared + routed
    x = x + _L0_gnn_ref(_layernorm(x, axis=-1), L0_gnn_h0, L0_gnn_a, L0_gnn_temp, adj, 1)
    x = x + _L0_ffn_ref(_layernorm(x, axis=-1)[None], L0_ffn_Wg, L0_ffn_bg, L0_ffn_W1, L0_ffn_b1, L0_ffn_W2, L0_ffn_b2)[0]
    x = x + _L1_gnn_ref(_layernorm(x, axis=-1), adj, L1_gnn_kernel, L1_gnn_bias, L1_gnn_beta)
    x = x + _L1_ffn_ref(_layernorm(x, axis=-1)[None], L1_ffn_Wr, L1_ffn_W1s, L1_ffn_b1s, L1_ffn_W2s, L1_ffn_b2s, L1_ffn_W1p, L1_ffn_b1p, L1_ffn_W2p, L1_ffn_b2p)[0]
    return x

_drawn_inputs = setup_inputs


def setup_inputs(seed=0):
    import zlib

    import numpy as np

    out = dict(_drawn_inputs(seed))
    spreads = {'L0_gnn_temp': (0.0, 0.8),
     'L0_ffn_bg': (0.0, 0.303),
     'L0_ffn_b1': (0.0, 0.705),
     'L0_ffn_b2': (0.0, 0.1),
     'L1_ffn_b1s': (0.0, 0.622),
     'L1_ffn_b2s': (0.0, 0.1),
     'L1_ffn_b1p': (0.0, 0.8),
     'L1_ffn_b2p': (0.0, 0.1)}
    factors = {'L1_gnn_bias': 8.0, 'L1_gnn_beta': 32.51, 'L1_ffn_W1p': 2.703}
    for name, (base, spread) in spreads.items():
        noise = np.random.default_rng([zlib.crc32(name.encode()), seed]).standard_normal(out[name].shape)
        drawn = base * np.exp(spread * noise) if base else spread * noise
        out[name] = jnp.asarray(drawn.astype(out[name].dtype))
    for name, factor in factors.items():
        out[name] = (out[name] * factor).astype(out[name].dtype)
    return out
```

```python
from contextlib import ExitStack

import concourse.bass as bass
from concourse import mybir

F32 = mybir.dt.float32
F16 = mybir.dt.float16
BF16 = mybir.dt.bfloat16
ALU = mybir.AluOpType
ACT = mybir.ActivationFunctionType
AX = mybir.AxisListType.X
RMAX = bass.bass_isa.ReduceOp.max

P = 128
N = 4096
NT = N // P
TPG = 4
GW = TPG * P
NG = NT // TPG
HC = 4
CJ = 4
NQ = NT // CJ
NC = NG * NQ
SC = 1024.0
HS = 256.0
EPS = 1e-5
THRESH = 1e-6
ALPHA = 0.2
BIG = 1e30


class Ticks:

    def __init__(self, eng, sem):
        self.eng, self.sem, self.base, self.it, self.per, self.k = eng, sem, 0, None, 0, 0

    def loop(self, it, per):
        self.base, self.it, self.per, self.k = self.base + self.k, it, per, 0

    def end(self, trips):
        assert self.k == self.per, (self.k, self.per)
        self.base, self.it, self.k = self.base + trips * self.per, None, 0

    def tick(self, ins):
        ins.then_inc(self.sem, 1)
        self.k += 1

    def wait(self):
        v = self.base + self.k
        self.eng.wait_ge(self.sem, v if self.it is None else self.it * self.per + v)

    def link(self, ins):
        self.tick(ins)
        self.wait()


class Core:

    def __init__(self, nc, ctx):
        self.nc, self.ctx = nc, ctx
        self.x = self.sb(ctx, "x", [P, NT, P], F32)
        self.id16 = self.sb(ctx, "id16", [P, P], F16)
        self.id32 = self.sb(ctx, "id32", [P, P], F32)
        self.stats = self.sb(ctx, "stats", [P, NT, 6], F32)
        self.mean = self.sb(ctx, "mean", [P, NT], F32)
        self.rstd = self.sb(ctx, "rstd", [P, NT], F32)
        self.rtmp = self.sb(ctx, "rtmp", [P, NT], F32)
        self.veps = self.sb(ctx, "veps", [P, NT], F32)
        self.V = Ticks(nc.vector, self.sem("vector_chain"))
        self.A = Ticks(nc.scalar, self.sem("scalar_chain"))
        self.G = Ticks(nc.gpsimd, self.sem("gpsimd_chain"))
        self.s_rec = self.sem("variance_reciprocal")
        self.s_root = self.sem("rstd_root")
        self.norms = 0

    def sb(self, ctx, name, shape, dt):
        return ctx.enter_context(self.nc.sbuf_tensor(name, shape, dt))

    def ps(self, ctx, name, shape, dt):
        return ctx.enter_context(self.nc.psum_tensor(name, shape, dt))

    def sem(self, name):
        return self.ctx.enter_context(self.nc.semaphore(name))

    def stats_of_group(self, g):
        nc = self.nc
        for k in range(TPG):
            ins = nc.vector.bn_stats(self.stats[:, g * TPG + k, :], self.x[:, g * TPG + k, :])
        self.V.tick(ins)

    def rstd_vector(self, scale):
        nc, V = self.nc, self.V
        self.norms += 1
        me, se, mo, so = (self.stats[:, :, i] for i in (1, 2, 4, 5))
        V.tick(nc.vector.tensor_tensor(self.mean[:, :], me, mo, ALU.add))
        V.link(nc.vector.tensor_tensor(self.rtmp[:, :], me, mo, ALU.subtract))
        V.tick(nc.vector.scalar_tensor_tensor(out=self.rtmp[:, :], in0=self.rtmp[:, :], scalar=0.25, in1=self.rtmp[:, :],
                                              op0=ALU.mult, op1=ALU.mult))
        V.link(nc.vector.tensor_tensor(self.veps[:, :], se, so, ALU.add))
        V.tick(nc.vector.tensor_scalar(self.mean[:, :], self.mean[:, :], 0.5, None, ALU.mult))
        V.link(nc.vector.tensor_scalar(self.veps[:, :], self.veps[:, :], 1.0 / P, EPS, ALU.mult, ALU.add))
        V.link(nc.vector.tensor_tensor(self.veps[:, :], self.veps[:, :], self.rtmp[:, :], ALU.add))
        nc.vector.reciprocal(self.rtmp[:, :], self.veps[:, :]).then_inc(self.s_rec, 1)
        nc.vector.wait_ge(self.s_root, self.norms)
        V.link(nc.vector.tensor_tensor(self.rtmp[:, :], self.rstd[:, :], self.rstd[:, :], ALU.mult))
        V.link(nc.vector.tensor_tensor(self.rtmp[:, :], self.rtmp[:, :], self.veps[:, :], ALU.mult))
        V.link(nc.vector.tensor_scalar(self.rtmp[:, :], self.rtmp[:, :], -0.5 * scale, 1.5 * scale, ALU.mult, ALU.add))
        V.link(nc.vector.tensor_tensor(self.rstd[:, :], self.rstd[:, :], self.rtmp[:, :], ALU.mult))

    def rstd_scalar(self, n):
        self.nc.scalar.wait_ge(self.s_rec, n)
        self.nc.scalar.activation(self.rstd[:, :], self.rtmp[:, :], ACT.Sqrt).then_inc(self.s_root, 1)

    def normalise_group(self, out, g):
        for k in range(TPG):
            t = g * TPG + k
            ins = self.nc.vector.tensor_scalar(out[:, t, :], self.x[:, t, :], self.mean[:, bass.ds(t, 1)],
                                               self.rstd[:, bass.ds(t, 1)], ALU.subtract, ALU.mult)
        return ins


def tiles(t, g):
    return t[:, bass.ds(g * TPG, TPG)]


def over_columns(t, width):
    return t.unsqueeze(2).to_broadcast([P, t.shape[1], width])


def attention(core, io, f1_row):
    nc, x, V, G, sem = core.nc, core.x, core.V, core.G, core.sem
    RING = 4
    AHEAD = RING - 1
    AHEAD_S = AHEAD + 2
    M_START = 2 * NQ
    STEEP = 2.0 ** 100
    W = (P + 2, P)
    with ExitStack() as c:
        def sb(name, shape, dt=F32):
            return core.sb(c, name, shape, dt)

        xn = sb("xn", [P, NT, P])
        feat = sb("feat", [P, NT, P])
        rb = [sb(f"rb{k}", [P, NT, 2, W[k]], F16) for k in range(2)]
        rd = [sb(f"rd{k}", [P, NT, 2, W[k]], F16) for k in range(2)]
        adj = sb("adj", [P, 2, CJ, GW])
        edge = sb("edge", [P, 2, CJ, GW], BF16)
        f1g = sb("f1g", [P, 2, GW])
        pos = sb("pos", [P, 2, CJ, GW], BF16)
        m1 = sb("m1", [P, RING, CJ, GW], BF16)
        m2 = sb("m2", [P, RING, CJ, GW], BF16)
        acc_a = sb("acc_a", [P, TPG, 2 * W[0]])
        acc_c = sb("acc_c", [P, TPG, 2 * W[0]])
        num = sb("num", [P, TPG, W[0]])
        vb = sb("vb", [P, TPG, P])
        vd = sb("vd", [P, TPG, P])
        a_bc = sb("a_bc", [P, 2, P])
        temp = sb("temp", [P, 5])
        coe = sb("coe", [P, 5])
        om = sb("om", [P, 5])
        f1, f2, steep, z, ca, cc, wb, wd, wb2, wd2, den, rden, rows, kx, kf, kp, sq = (
            sb(f"col_{n}", [P, NT]) for n in ("f1", "f2", "steep", "z", "ca", "cc", "wb", "wd", "wb2", "wd2",
                                             "den", "rden", "rows", "kx", "kf", "kp", "sq"))
        fmax = sb("fmax", [P, 1])
        fall = sb("fall", [P, 1])
        nfall = sb("nfall", [P, 2])
        cf = sb("cf", [P, 2])
        f1t = sb("f1t", [NT, P])
        bank = [core.ps(c, f"bank{b}", [P, 512], F32) for b in range(2 * TPG)]

        s_x, s_par, s_h0 = sem("x_loaded"), sem("a_and_temp_loaded"), sem("h0_loaded")
        s_id = sem("identities_ready")
        s_f1, s_f1T, s_f1s, s_f1d = sem("f1_ready"), sem("f1_transposed"), sem("f1_rows_copied"), sem("f1_in_dram")
        s_fmax, s_fall, s_z = sem("f2_max_of_partitions"), sem("f2_max"), sem("exponents_ready")
        s_exp = sem("exponentials_ready")
        s_w = sem("b_and_d_ready")
        s_vb, s_vd, s_hb, s_hd = sem("b_rows"), sem("d_rows"), sem("b_rows_hi"), sem("d_rows_hi")
        s_rb, s_rd = sem("b_operands_ready"), sem("d_operands_ready")
        s_adj = [sem(f"adj_loaded{b}") for b in range(2)]
        s_f1g = [sem(f"f1_group_loaded{b}") for b in range(2)]
        s_edge = sem("edges_ready")
        s_pos = sem("pos_ready")
        s_m1, s_m2p, s_m2v = sem("mask1_ready"), sem("mask2_by_gpsimd"), sem("mask2_by_vector")
        s_pe = sem("mask_slots_free")
        s_ea, s_ec = sem("a_banks_copied"), sem("c_banks_copied")
        s_feat = sem("feat_ready")

        with nc.Block() as block:

            @block.sync
            def _(sp):
                sp.dma_start(x[:, :, :], io["x"]).then_inc(s_x, 16)
                sp.dma_start(a_bc[:, :, :], io["L0_gnn_a"].partition_broadcast(P)).then_inc(s_par, 16)
                sp.dma_start(temp[:, :], io["L0_gnn_temp"].partition_broadcast(P)).then_inc(s_par, 16)
                sp.dma_start(feat[:, :, :], io["L0_gnn_h0"]).then_inc(s_h0, 16)
                sp.wait_ge(s_f1s, 1)
                sp.dma_start(f1_row.rearrange("g (t p) -> (g t) p", p=P), f1t[:, :]).then_inc(s_f1d, 16)
                sp.wait_ge(s_f1d, 16)
                for k in range(2):
                    with sp.Fori(0, NG // 2) as g2:
                        for b in range(2):
                            g = g2 * 2 + (k * NG + b)
                            sp.wait_ge(s_m1, (g + 1) * NQ)
                            sp.dma_start(f1g[:, b, :], f1_row[bass.ds(g2 * 2 + b, 1), :].squeeze(0)
                                         .partition_broadcast(P)).then_inc(s_f1g[b], 16)
                            for q in range(NQ):
                                sp.wait_ge(s_edge, g * NQ + (q + 1))
                                sp.dma_start(adj[:, q % 2, :, :], io["adj"][bass.ds((g2 * 2 + b) * NQ + q, 1)].squeeze(0)
                                             ).then_inc(s_adj[q % 2], 16)

            @block.gpsimd
            def _(pool):
                for m in (core.id16, core.id32):
                    G.link(nc.gpsimd.memset(m[:, :], 0.0))
                    nc.gpsimd.affine_select(out=m[:, :], in_=m[:, :], compare_op=ALU.not_equal, fill=1.0, base=0,
                                            pattern=[[-1, P]], channel_multiplier=1).then_inc(s_id, 1)
                pool.sem_inc(s_m2p, M_START)
                pool.wait_ge(s_fmax, 1)
                nc.gpsimd.partition_all_reduce(fall[:, :], fmax[:, :], P, RMAX).then_inc(s_fall, 1)
                with pool.Fori(0, 2 * NC // RING) as n4:
                    for r in range(RING):
                        pool.wait_ge(s_m1, n4 * RING + (M_START + r + 1))
                        nc.gpsimd.tensor_tensor(m2[:, r, 1:CJ, :], edge[:, r % 2, 1:CJ, :], m1[:, r, 1:CJ, :],
                                                ALU.subtract).then_inc(s_m2p, 1)

            @block.scalar
            def _(act):
                act.sem_inc(s_ea, TPG)
                act.wait_ge(s_par, 32)
                nc.scalar.activation(coe[:, :], temp[:, :], ACT.Exp, scale=-1.0).then_inc(s_exp, 1)
                core.rstd_scalar(1)
                act.wait_ge(s_z, 1)
                nc.scalar.activation(wb[:, :], f2[:, :], ACT.Exp, bias=nfall[:, 0:1], scale=1.0).then_inc(s_exp, 1)
                nc.scalar.activation(wd[:, :], f2[:, :], ACT.Exp, bias=nfall[:, 1:2], scale=ALPHA).then_inc(s_exp, 1)
                nc.scalar.activation(ca[:, :], ca[:, :], ACT.Exp).then_inc(s_exp, 1)
                nc.scalar.activation(cc[:, :], cc[:, :], ACT.Exp).then_inc(s_exp, 1)

                def hi_b(k, g):
                    act.wait_ge(s_vb, g + (k * NG + 1))
                    nc.scalar.activation(tiles(rb[k], g)[:, :, 0, 0:P], vb[:, :, :], ACT.Copy).then_inc(s_hb, 1)

                def d_rows(k, g):
                    if k == 1:
                        act.wait_ge(s_feat, g + 1)
                    act.wait_ge(s_rd, g + (k * NG + 1))
                    for i in range(TPG):
                        t = g * TPG + i
                        ins = nc.scalar.activation(vd[:, i, :], (feat if k else xn)[:, t, :], ACT.Copy,
                                                   scale=wd[:, bass.ds(t, 1)])
                    ins.then_inc(s_vd, 1)
                    act.wait_ge(s_vd, g + (k * NG + 1))
                    nc.scalar.activation(tiles(rd[k], g)[:, :, 0, 0:P], vd[:, :, :], ACT.Copy).then_inc(s_hd, 1)

                def compare(g, b, q0, q1):
                    for q in range(q0, q1):
                        act.wait_ge(s_m1, g * NQ + (M_START + q - 1))
                        if q == 0:
                            act.wait_ge(s_f1g[b], (g + (2 - b)) * 8)
                        for i in range(CJ):
                            jt = q * CJ + i
                            ins = nc.scalar.activation(pos[:, q % 2, i, :], f1g[:, b, :], ACT.Sigmoid,
                                                       bias=steep[:, jt:jt + 1], scale=STEEP)
                        ins.then_inc(s_pos, 1)

                def copy_out(k, g):
                    act.wait_ge(s_pe, g * NQ + (k * NC + RING + NQ))
                    act.wait_ge(s_feat, g + k * NG)
                    for t in range(TPG):
                        nc.scalar.activation(acc_a[:, t, 0:2 * W[k]], bank[2 * t][:, 0:2 * W[k]], ACT.Copy,
                                             scale=ca[:, bass.ds(g * TPG + t, 1)]).then_inc(s_ea, 1)

                act.wait_ge(s_w, 1)
                with act.Fori(0, NG) as g:
                    d_rows(0, g)
                    hi_b(0, g)
                compare(0, 0, 0, NQ)
                compare(1, 1, 0, AHEAD_S)
                for k in range(2):
                    with act.Fori(0, NG // 2 - k) as g2:
                        for b in range(2):
                            g = g2 * 2 + b
                            copy_out(k, g)
                            if k == 0:
                                d_rows(1, g)
                                hi_b(1, g)
                            compare(g + (k * NG + 1), 1 - b, AHEAD_S, NQ)
                            compare(g + (k * NG + 2), b, 0, AHEAD_S)
                copy_out(1, NG - 2)
                compare(2 * NG - 1, 1, AHEAD_S, NQ)
                copy_out(1, NG - 1)

            @block.tensor
            def _(pe):
                pe.sem_inc(s_pe, RING)
                pe.wait_ge(s_id, 2)
                pe.wait_ge(s_f1, 1)
                nc.tensor.transpose(bank[0][0:NT, 0:P], f1[:, :], core.id32[:, :]).then_inc(s_f1T, 1)
                for k in range(2):
                    pe.wait_ge(s_rb, (k + 1) * (NG + 1) - k)
                    pe.wait_ge(s_rd, (k + 1) * NG)
                    with pe.Fori(0, NG) as g:
                        for jt in range(NT):
                            q = jt // CJ
                            if jt % CJ == 0:
                                pe.wait_ge(s_m2p, g * NQ + (k * NC + M_START + q + 1))
                                pe.wait_ge(s_m2v, g * NQ + (k * NC + M_START + q + 1))
                            for t in range(TPG):
                                for m, r, o in ((m1, rb, 0), (m2, rd, 1)):
                                    if jt == 0:
                                        pe.wait_ge((s_ea, s_ec)[o], g * TPG + (k * NT + t + 1))
                                    mm = nc.tensor.matmul(bank[2 * t + o][:, 0:2 * W[k]], m[:, q % RING, jt % CJ, t * P:(t + 1) * P],
                                                          r[k][:, jt, :, :].rearrange("p h w -> p (h w)"),
                                                          start=(jt == 0), stop=(jt == NT - 1))
                            if jt % CJ == CJ - 1:
                                mm.then_inc(s_pe, 1)

            @block.vector
            def _(dve):
                dve.sem_inc(s_m1, M_START)
                dve.sem_inc(s_m2v, M_START)
                dve.sem_inc(s_edge, 2)
                dve.sem_inc(s_rd, 1)
                dve.sem_inc(s_ec, TPG)
                dve.wait_ge(s_x, 16)
                with dve.Fori(0, NG) as g:
                    V.loop(g, 1)
                    core.stats_of_group(g)
                V.end(NG)
                V.wait()
                core.rstd_vector(1.0)
                with dve.Fori(0, NG) as g:
                    V.loop(g, 1)
                    V.tick(core.normalise_group(xn, g))
                V.end(NG)
                V.wait()
                dve.wait_ge(s_par, 32)
                with dve.Fori(0, NG) as g:
                    V.loop(g, 4)
                    for h, f in ((0, f1), (1, f2)):
                        V.link(nc.vector.tensor_tensor(vb[:, :, :], tiles(xn, g), a_bc[:, h:h + 1, :].to_broadcast([P, TPG, P]),
                                                       ALU.mult))
                        V.link(nc.vector.tensor_reduce(tiles(f, g), vb[:, :, :], AX, ALU.add))
                V.end(NG)
                dve.sem_inc(s_f1, 1)
                nc.vector.tensor_reduce(fmax[:, :], f2[:, :], AX, ALU.max).then_inc(s_fmax, 1)
                V.tick(nc.vector.tensor_scalar(steep[:, :], f2[:, :], STEEP, None, ALU.mult))
                dve.wait_ge(s_exp, 1)
                V.link(nc.vector.tensor_scalar(coe[:, :], coe[:, :], 1.0, None, ALU.add))
                V.link(nc.vector.reciprocal(coe[:, :], coe[:, :]))
                V.link(nc.vector.tensor_scalar(om[:, :], coe[:, :], -1.0, 1.0, ALU.mult, ALU.add))
                V.tick(nc.vector.tensor_tensor(cf[:, 0:1], om[:, 1:2], coe[:, 0:1], ALU.mult))
                V.link(nc.vector.tensor_tensor(cf[:, 1:2], om[:, 1:2], om[:, 0:1], ALU.mult))
                dve.wait_ge(s_f1T, 1)
                nc.vector.tensor_copy(f1t[:, :], bank[0][0:NT, 0:P]).then_inc(s_f1s, 1)
                dve.wait_ge(s_fall, 1)
                V.tick(nc.vector.tensor_scalar(nfall[:, 0:1], fall[:, :], -1.0, None, ALU.mult))
                V.tick(nc.vector.tensor_scalar(nfall[:, 1:2], fall[:, :], -ALPHA, None, ALU.mult))
                V.link(nc.vector.tensor_scalar(z[:, :], f1[:, :], fall[:, 0:1], None, ALU.add))
                V.link(nc.vector.scalar_tensor_tensor(out=kx[:, :], in0=z[:, :], scalar=ALPHA, in1=z[:, :],
                                                      op0=ALU.mult, op1=ALU.max))
                V.tick(nc.vector.tensor_tensor(ca[:, :], z[:, :], kx[:, :], ALU.subtract))
                V.link(nc.vector.scalar_tensor_tensor(out=cc[:, :], in0=z[:, :], scalar=ALPHA, in1=kx[:, :],
                                                      op0=ALU.mult, op1=ALU.subtract))
                dve.sem_inc(s_z, 1)
                dve.wait_ge(s_h0, 16)
                V.tick(nc.vector.scalar_tensor_tensor(out=x[:, :, :], in0=feat[:, :, :], scalar=cf[:, 1:2], in1=x[:, :, :],
                                                      op0=ALU.mult, op1=ALU.add))
                dve.wait_ge(s_exp, 5)
                V.tick(nc.vector.scalar_tensor_tensor(out=wb2[:, :], in0=wb[:, :], scalar=SC, in1=wb[:, :], op0=ALU.mult, op1=ALU.mult))
                V.link(nc.vector.scalar_tensor_tensor(out=wd2[:, :], in0=wd[:, :], scalar=SC, in1=wd[:, :], op0=ALU.mult, op1=ALU.mult))
                V.tick(nc.vector.tensor_scalar(wb[:, :], wb[:, :], SC, None, ALU.mult))
                V.link(nc.vector.tensor_scalar(wd[:, :], wd[:, :], SC, None, ALU.mult))
                dve.sem_inc(s_w, 1)
                for r, w, w2 in ((rb[0], wb, wb2), (rd[0], wd, wd2)):
                    V.tick(nc.vector.tensor_copy(r[:, :, 0, P], w[:, :]))
                    V.link(nc.vector.tensor_copy(r[:, :, 0, P + 1], w2[:, :]))
                    V.tick(nc.vector.tensor_tensor(r[:, :, 1, P], w[:, :], r[:, :, 0, P], ALU.subtract))
                    V.link(nc.vector.tensor_tensor(r[:, :, 1, P + 1], w2[:, :], r[:, :, 0, P + 1], ALU.subtract))
                dve.sem_inc(s_rb, 1)

                def b_rows(k, g):
                    dve.wait_ge(s_rb, g + (k * NG + 1))
                    nc.vector.tensor_tensor(vb[:, :, :], tiles(feat if k else xn, g), over_columns(tiles(wb, g), P),
                                            ALU.mult).then_inc(s_vb, 1)

                def lo_rows(k, g):
                    for v, r, s_v, s_hi, s_r in ((vd, rd, s_vd, s_hd, s_rd), (vb, rb, s_vb, s_hb, s_rb)):
                        dve.wait_ge(s_v, g + (k * NG + 1))
                        dve.wait_ge(s_hi, g + (k * NG + 1))
                        r = tiles(r[k], g)
                        nc.vector.tensor_tensor(r[:, :, 1, 0:P], v[:, :, :], r[:, :, 0, 0:P], ALU.subtract).then_inc(s_r, 1)

                with dve.Fori(0, NG) as g:
                    b_rows(0, g)
                    lo_rows(0, g)

                def edges(g, q):
                    dve.wait_ge(s_adj[q % 2], g * (NQ // 2 * 16) + (q // 2 + 1) * 16)
                    dve.wait_ge(s_m2p, g * NQ + (M_START + q - 1))
                    dve.wait_ge(s_m2v, g * NQ + (M_START + q - 1))
                    nc.vector.tensor_scalar(edge[:, q % 2], adj[:, q % 2], 0.0, None, ALU.is_gt).then_inc(s_edge, 1)

                def masks(g, q0, q1, more=True):
                    for q in range(q0, q1):
                        if q + 1 < NQ:
                            edges(g, q + 1)
                        elif more:
                            edges(g + 1, 0)
                        n = g * NQ + (q + 1)
                        dve.wait_ge(s_edge, n + 2)
                        dve.wait_ge(s_pos, n)
                        dve.wait_ge(s_pe, n)
                        r = q % RING
                        nc.vector.tensor_tensor(m1[:, r], edge[:, q % 2], pos[:, q % 2], ALU.mult).then_inc(s_m1, 1)
                        dve.wait_ge(s_m1, n + M_START)
                        nc.vector.tensor_tensor(m2[:, r, 0, :], edge[:, q % 2, 0, :], m1[:, r, 0, :], ALU.subtract).then_inc(s_m2v, 1)

                def sums(k, g):
                    w = W[k]
                    dve.wait_ge(s_pe, g * NQ + (k * NC + RING + NQ))
                    for t in range(TPG):
                        nc.vector.tensor_scalar(acc_c[:, t, 0:2 * w], bank[2 * t + 1][:, 0:2 * w],
                                                cc[:, bass.ds(g * TPG + t, 1)], None, ALU.mult).then_inc(s_ec, 1)
                    dve.wait_ge(s_ec, g * TPG + (k * NT + 2 * TPG))
                    dve.wait_ge(s_ea, g * TPG + (k * NT + 2 * TPG))
                    if k == 0:
                        s, d = tiles(sq, g), tiles(den, g)
                        V.tick(nc.vector.tensor_tensor(s, acc_a[:, :, w - 1], acc_a[:, :, 2 * w - 1], ALU.add))
                        V.link(nc.vector.tensor_tensor(d, acc_c[:, :, w - 1], acc_c[:, :, 2 * w - 1], ALU.add))
                        V.tick(nc.vector.tensor_tensor(s, s, tiles(ca, g), ALU.mult))
                        V.link(nc.vector.tensor_tensor(d, d, tiles(cc, g), ALU.mult))
                        V.tick(nc.vector.tensor_tensor(s, s, d, ALU.add))
                    V.link(nc.vector.tensor_tensor(acc_c[:, :, 0:2 * w], acc_c[:, :, 0:2 * w], acc_a[:, :, 0:2 * w], ALU.add))
                    V.link(nc.vector.tensor_tensor(num[:, :, 0:w], acc_c[:, :, 0:w], acc_c[:, :, w:2 * w], ALU.add))

                def first_post(g):
                    sums(0, g)
                    V.link(nc.vector.reciprocal(tiles(rden, g), num[:, :, P]))
                    V.link(nc.vector.tensor_tensor(tiles(den, g), tiles(rden, g), tiles(rden, g), ALU.mult))
                    V.link(nc.vector.scalar_tensor_tensor(out=tiles(rows, g), in0=tiles(den, g), scalar=0.5 * SC,
                                                          in1=tiles(sq, g), op0=ALU.mult, op1=ALU.mult))
                    V.link(nc.vector.tensor_scalar(tiles(kx, g), tiles(rows, g), -1.0, om[:, 2:3], ALU.mult, ALU.add))
                    for k in range(TPG):
                        t = g * TPG + k
                        ins = nc.vector.tensor_scalar(feat[:, t, :], xn[:, t, :], kx[:, bass.ds(t, 1)], None, ALU.mult)
                    V.link(ins)
                    for k in range(TPG):
                        t = g * TPG + k
                        ins = nc.vector.scalar_tensor_tensor(out=feat[:, t, :], in0=num[:, k, 0:P], scalar=rden[:, bass.ds(t, 1)],
                                                             in1=feat[:, t, :], op0=ALU.mult, op1=ALU.add)
                    V.link(ins)
                    dve.wait_ge(s_rb, g + (NG + 1))
                    V.link(nc.vector.tensor_scalar(vb[:, :, :], tiles(feat, g), THRESH, -THRESH, ALU.min, ALU.max))
                    nc.vector.tensor_tensor(tiles(feat, g), tiles(feat, g), vb[:, :, :], ALU.subtract).then_inc(s_feat, 1)
                    dve.wait_ge(s_feat, g + 1)
                    b_rows(1, g)

                def second_post(g):
                    sums(1, g)
                    for k in range(TPG):
                        t = g * TPG + k
                        ins = nc.vector.scalar_tensor_tensor(out=x[:, t, :], in0=num[:, k, 0:P], scalar=kp[:, bass.ds(t, 1)],
                                                             in1=x[:, t, :], op0=ALU.mult, op1=ALU.add)
                    ins.then_inc(s_feat, 1)
                    dve.wait_ge(s_feat, g + (NG + 1))
                    for k in range(TPG):
                        t = g * TPG + k
                        ins = nc.vector.scalar_tensor_tensor(out=x[:, t, :], in0=feat[:, t, :], scalar=kf[:, bass.ds(t, 1)],
                                                             in1=x[:, t, :], op0=ALU.mult, op1=ALU.add)
                    V.link(ins)
                    core.stats_of_group(g)

                FIRST_TICKS, SECOND_TICKS = 14, 4
                edges(0, 0)
                masks(0, 0, NQ)
                masks(1, 0, AHEAD)
                with dve.Fori(0, NG // 2) as g2:
                    V.loop(g2, 2 * FIRST_TICKS)
                    for b in range(2):
                        g = g2 * 2 + b
                        first_post(g)
                        masks(g + 1, AHEAD, AHEAD + 1)
                        lo_rows(1, g)
                        masks(g + 1, AHEAD + 1, NQ)
                        masks(g + 2, 0, AHEAD)
                V.end(NG // 2)
                V.link(nc.vector.tensor_scalar(kf[:, :], rows[:, :], coe[:, 1:2], cf[:, 0:1], ALU.mult, ALU.add))
                V.link(nc.vector.tensor_scalar(kp[:, :], kf[:, :], coe[:, 3:4], None, ALU.mult))
                V.link(nc.vector.tensor_scalar(kp[:, :], kp[:, :], -1.0, coe[:, 1:2], ALU.mult, ALU.add))
                V.link(nc.vector.tensor_tensor(kp[:, :], kp[:, :], rden[:, :], ALU.mult))
                with dve.Fori(0, NG // 2 - 1) as g2:
                    V.loop(g2, 2 * SECOND_TICKS)
                    for b in range(2):
                        g = g2 * 2 + b
                        second_post(g)
                        masks(g + (NG + 1), AHEAD, NQ)
                        masks(g + (NG + 2), 0, AHEAD)
                V.end(NG // 2 - 1)
                second_post(NG - 2)
                masks(2 * NG - 1, AHEAD, NQ, more=False)
                second_post(NG - 1)
                V.wait()


def split_tensors(core, c, tag):
    xs = core.sb(c, f"xs{tag}", [P, NT, P], F32)
    xh = core.sb(c, f"xh{tag}", [P, 2, NT, P], F16)
    xt = core.sb(c, f"xt{tag}", [P, 2, N], F16)
    turn = core.ps(c, f"turn{tag}", [P, 2, GW], F16)
    sems = [core.sem(f"{n}{tag}") for n in ("xs_ready", "xs_hi_ready", "xs_lo_ready", "xs_turned", "xt_ready")]
    return xs, xh, xt, turn, sems


def split_vector(core, s):
    xs, xh, xt, turn, (s_n, s_h, s_l, s_t, s_c) = s
    nc, V = core.nc, core.V
    core.rstd_vector(SC)
    with nc.vector.Fori(0, NG) as g:
        core.normalise_group(xs, g).then_inc(s_n, 1)
    with nc.vector.Fori(0, NG) as g:
        nc.vector.wait_ge(s_n, g + 1)
        nc.vector.wait_ge(s_h, g + 1)
        nc.vector.tensor_tensor(tiles(xh[:, 1], g), tiles(xs, g), tiles(xh[:, 0], g), ALU.subtract).then_inc(s_l, 1)


def split_scalar(core, s, n):
    xs, xh, xt, turn, (s_n, s_h, s_l, s_t, s_c) = s
    nc = core.nc
    core.rstd_scalar(n)
    with nc.scalar.Fori(0, NG) as g:
        nc.scalar.wait_ge(s_n, g + 1)
        nc.scalar.activation(tiles(xh[:, 0], g), tiles(xs, g), ACT.Copy).then_inc(s_h, 1)
    with nc.scalar.Fori(0, NG) as g:
        nc.scalar.wait_ge(s_t, g + 1)
        nc.scalar.activation(xt[:, :, bass.ds(g * GW, GW)], turn[:, :, :], ACT.Copy).then_inc(s_c, 1)


def split_tensor(core, s):
    xs, xh, xt, turn, (s_n, s_h, s_l, s_t, s_c) = s
    nc = core.nc

    def turn_group(g):
        nc.tensor.wait_ge(s_l, g + 1)
        for h in range(2):
            for k in range(TPG):
                mm = nc.tensor.transpose(turn[:, h, k * P:(k + 1) * P], xh[:, h, g * TPG + k, :], core.id16[:, :])
        mm.then_inc(s_t, 1)

    for g in range(NG):
        if g:
            nc.tensor.wait_ge(s_c, g)
        turn_group(g)
    nc.tensor.wait_ge(s_c, NG)


def experts(core, io, tag, E, routed, wg_d, bg_d, w1_d, b1_d, w2_d, b2_d, out_d):
    nc, x, V, sem = core.nc, core.x, core.V, core.sem
    R = routed
    norm = core.norms + 1
    with ExitStack() as c:
        def sb(name, shape, dt=F32):
            return core.sb(c, f"{name}{tag}", shape, dt)

        s = split_tensors(core, c, tag)
        xs, xh, xt, turn, (s_n, s_h, s_l, s_t, s_c) = s
        wg = sb("wg", [P, R])
        wgs = sb("wgs", [P, 2, R], F16)
        bg = sb("bg", [P, R])
        b1 = sb("b1", [P, E, HC])
        b2 = sb("b2", [E, P])
        w1f = sb("w1f", [P, HC * P])
        w2f = sb("w2f", [P, HC * P])
        w1 = sb("w1", [P, 2, 2, HC, P], F16)
        w2 = sb("w2", [P, 2, 2, HC, P], F16)
        lg = sb("lg", [P, NT, R])
        t1 = sb("t1", [P, NT, R])
        oh = sb("oh", [P, 2, NT, R])
        best = sb("best", [P, 2, NT])
        pick = sb("pick", [P, NT])
        ex = sb("ex", [P, NT])
        wt = sb("wt", [P, 2, NT])
        order = sb("order", [P, R])
        wtok = sb("wtok", [P, NT, E])
        wsc = sb("wsc", [P, NT, E])
        wT = sb("wT", [E, GW])
        h32 = sb("h32", [P, HC, GW])
        hh = sb("hh", [P, HC, GW], F16)
        hl = sb("hl", [P, HC, GW], F16)
        hbank = [core.ps(c, f"hid{tag}_{k}", [P, GW], F32) for k in range(HC)]
        ybank = [core.ps(c, f"y{tag}_{k}", [P, TPG, P], F32) for k in range(2)]
        lbank = core.ps(c, f"logits{tag}", [P, 512], F32)

        s_wg = sem(f"gate_loaded{tag}")
        s_b = sem(f"biases_loaded{tag}")
        s_w = sem(f"weights_loaded{tag}")
        s_ws = sem(f"weights_split{tag}")
        s_wgs = sem(f"gate_split{tag}")
        s_lg = sem(f"logits_summed{tag}")
        s_ord = sem(f"order_ready{tag}")
        s_d, s_ex = sem(f"logit_gap{tag}"), sem(f"gap_exp{tag}")
        s_wt = sem(f"token_weights{tag}")
        s_wT, s_wTc = sem(f"token_weights_turned{tag}"), sem(f"token_weights_copied{tag}")
        s_bias, s_biasd = sem(f"bias_sums{tag}"), sem(f"bias_added{tag}")
        s_h1 = sem(f"hidden_summed{tag}")
        s_ge = sem(f"gelu_done{tag}")
        s_hh, s_hl = sem(f"hidden_hi{tag}"), sem(f"hidden_lo{tag}")
        s_y = sem(f"hidden_used{tag}")
        s_add = sem(f"expert_added{tag}")
        s_out = sem(f"stored{tag}")

        with nc.Block() as block:

            @block.sync
            def _(sp):
                sp.dma_start(wg[:, :], wg_d).then_inc(s_wg, 16)
                if bg_d is not None:
                    sp.dma_start(bg[:, :], bg_d.partition_broadcast(P)).then_inc(s_wg, 16)
                sp.dma_start(b1[:, :, :], b1_d).then_inc(s_b, 16)
                sp.dma_start(b2[:, :], b2_d).then_inc(s_b, 16)
                with sp.Fori(0, E) as e:
                    sp.wait_ge(s_ws, e + 1)
                    sp.dma_start(w1f[:, :], w1_d[bass.ds(e, 1)].squeeze(0)).then_inc(s_w, 16)
                    sp.dma_start(w2f[:, :], w2_d[bass.ds(e, 1)].squeeze(0)).then_inc(s_w, 16)
                if out_d is not None:
                    with sp.Fori(0, NG) as g:
                        sp.wait_ge(s_add, g + (2 + (E - 1) * NG + 1))
                        sp.dma_start(tiles(out_d, g), tiles(x, g)).then_inc(s_out, 16)
                    sp.wait_ge(s_out, 16 * NG)

            @block.gpsimd
            def _(pool):
                for k in range(R):
                    ins = nc.gpsimd.memset(order[:, k:k + 1], float(R - k))
                ins.then_inc(s_ord, 1)

            @block.scalar
            def _(act):
                split_scalar(core, s, norm)
                act.wait_ge(s_d, 1)
                nc.scalar.activation(ex[:, :], ex[:, :], ACT.Exp).then_inc(s_ex, 1)
                act.sem_inc(s_ge, HC)
                with act.Fori(0, NG) as g:
                    act.wait_ge(s_wT, g + 1)
                    nc.scalar.activation(wT[:, :], lbank[0:E, 0:GW], ACT.Copy).then_inc(s_wTc, 1)
                act.wait_ge(s_b, 32)
                with act.Fori(0, E) as e:
                    with act.Fori(0, NG) as g:
                        n = e * (NG * HC) + g * HC
                        for k in range(HC):
                            act.wait_ge(s_h1, n + (k + 1))
                            act.wait_ge(s_hh, n + (k + 1))
                            act.wait_ge(s_hl, n + (k + 1))
                            nc.scalar.activation(h32[:, k, :], hbank[k][:, :], ACT.Gelu, bias=b1[:, e, k:k + 1],
                                                 scale=1.0 / (SC * SC)).then_inc(s_ge, 1)

            @block.vector
            def _(dve):
                dve.sem_inc(s_ws, 1)
                dve.sem_inc(s_hh, HC)
                dve.sem_inc(s_hl, HC)
                dve.sem_inc(s_add, 2)
                dve.sem_inc(s_biasd, 1)
                dve.wait_ge(s_wg, 16 if bg_d is None else 32)
                V.link(nc.vector.tensor_scalar(wgs[:, 0, :], wg[:, :], SC, None, ALU.mult))
                nc.vector.scalar_tensor_tensor(out=wgs[:, 1, :], in0=wg[:, :], scalar=SC, in1=wgs[:, 0, :],
                                               op0=ALU.mult, op1=ALU.subtract).then_inc(s_wgs, 1)

                def split_weights(e, b):
                    dve.wait_ge(s_w, e * 32 + 32)
                    for f, w in ((w1f, w1), (w2f, w2)):
                        v = [w[:, b, h].rearrange("p c n -> p (c n)") for h in range(2)]
                        V.link(nc.vector.tensor_scalar(v[0], f[:, :], SC, None, ALU.mult))
                        ins = nc.vector.scalar_tensor_tensor(out=v[1], in0=f[:, :], scalar=SC, in1=v[0],
                                                             op0=ALU.mult, op1=ALU.subtract)
                        if f is w1f:
                            V.tick(ins)
                    ins.then_inc(s_ws, 1)

                split_vector(core, s)
                dve.wait_ge(s_lg, 1)
                dve.wait_ge(s_ord, 1)
                lview = lbank[:, 0:NT * R].rearrange("p (t r) -> p t r", r=R)
                V.link(nc.vector.tensor_scalar(lg[:, :, :], lview, 1.0 / (SC * SC), None, ALU.mult))
                if bg_d is not None:
                    V.link(nc.vector.tensor_tensor(lg[:, :, :], lg[:, :, :], bg[:, None, :].to_broadcast([P, NT, R]), ALU.add))
                obc = order[:, None, :].to_broadcast([P, NT, R])
                for k in range(2):
                    V.link(nc.vector.tensor_reduce(best[:, k, :], lg[:, :, :], AX, ALU.max))
                    V.link(nc.vector.tensor_tensor(t1[:, :, :], lg[:, :, :], over_columns(best[:, k, :], R), ALU.is_equal))
                    V.link(nc.vector.tensor_tensor(t1[:, :, :], t1[:, :, :], obc, ALU.mult))
                    V.link(nc.vector.tensor_reduce(pick[:, :], t1[:, :, :], AX, ALU.max))
                    V.link(nc.vector.tensor_tensor(oh[:, k], obc, over_columns(pick[:, :], R), ALU.is_equal))
                    if k == 0:
                        V.link(nc.vector.scalar_tensor_tensor(out=lg[:, :, :], in0=oh[:, 0], scalar=-BIG, in1=lg[:, :, :],
                                                              op0=ALU.mult, op1=ALU.add))
                nc.vector.tensor_tensor(ex[:, :], best[:, 1, :], best[:, 0, :], ALU.subtract).then_inc(s_d, 1)
                split_weights(0, 0)
                dve.wait_ge(s_ex, 1)
                V.link(nc.vector.tensor_scalar(wt[:, 0, :], ex[:, :], 1.0, None, ALU.add))
                V.link(nc.vector.reciprocal(wt[:, 0, :], wt[:, 0, :]))
                V.link(nc.vector.tensor_tensor(wt[:, 1, :], wt[:, 0, :], ex[:, :], ALU.mult))
                V.tick(nc.vector.tensor_tensor(oh[:, 0], oh[:, 0], over_columns(wt[:, 0, :], R), ALU.mult))
                V.link(nc.vector.tensor_tensor(oh[:, 1], oh[:, 1], over_columns(wt[:, 1, :], R), ALU.mult))
                V.link(nc.vector.tensor_tensor(wtok[:, :, 0:R], oh[:, 0], oh[:, 1], ALU.add))
                if E > R:
                    V.link(nc.vector.memset(wtok[:, :, R:E], 1.0))
                nc.vector.tensor_scalar(wsc[:, :, :], wtok[:, :, :], 1.0 / (SC * HS), None, ALU.mult).then_inc(s_wt, 1)
                with dve.Fori(0, NG) as g:
                    dve.wait_ge(s_bias, g + 1)
                    nc.vector.tensor_tensor(tiles(x, g), ybank[0][:, :, :], tiles(x, g), ALU.add).then_inc(s_biasd, 1)
                dve.wait_ge(s_biasd, 1 + NG)
                dve.wait_ge(s_wt, 1)

                def turns(e, g, b):
                    n = e * (NG * HC) + g * HC
                    for k in range(HC):
                        dve.wait_ge(s_ge, n + (HC + k + 1))
                        dve.wait_ge(s_y, n + (k + 1))
                        nc.vector.tensor_scalar(hh[:, k, :], h32[:, k, :], HS, None, ALU.mult).then_inc(s_hh, 1)
                        dve.wait_ge(s_hh, n + (HC + k + 1))
                        nc.vector.scalar_tensor_tensor(out=hl[:, k, :], in0=h32[:, k, :], scalar=HS, in1=hh[:, k, :],
                                                       op0=ALU.mult, op1=ALU.subtract).then_inc(s_hl, 1)
                    dve.wait_ge(s_y, n + 2 * HC)
                    dve.wait_ge(s_add, e * NG + g + 2)
                    for k in range(TPG):
                        t = g * TPG + k
                        ins = nc.vector.scalar_tensor_tensor(out=x[:, t, :], in0=ybank[b][:, k, :], scalar=wsc[:, t, bass.ds(e, 1)],
                                                             in1=x[:, t, :], op0=ALU.mult, op1=ALU.add)
                    ins.then_inc(s_add, 1)

                def expert(e, b, last):
                    with dve.Fori(0, NG // 2 - 1) as g2:
                        for gb in range(2):
                            turns(e, g2 * 2 + gb, gb)
                    if not last:
                        split_weights(e + 1, 1 - b)
                    for gb in range(2):
                        turns(e, NG - 2 + gb, gb)

                EL = E - 1 if E % 2 else E - 2
                with dve.Fori(0, EL // 2) as e2:
                    V.loop(e2, 6)
                    for b in range(2):
                        expert(e2 * 2 + b, b, False)
                V.end(EL // 2)
                for e in range(EL, E):
                    expert(e, e % 2, e == E - 1)
                dve.wait_ge(s_add, 2 + E * NG)
                if out_d is None:
                    with dve.Fori(0, NG) as g:
                        V.loop(g, 1)
                        core.stats_of_group(g)
                    V.end(NG)
                V.wait()

            @block.tensor
            def _(pe):
                pe.sem_inc(s_y, HC)
                split_tensor(core, s)
                pe.wait_ge(s_wgs, 1)
                for t in range(NT):
                    for n, (h, w) in enumerate(((0, 0), (0, 1), (1, 0))):
                        mm = nc.tensor.matmul(lbank[:, t * R:(t + 1) * R], xt[:, h, t * P:(t + 1) * P], wgs[:, w, :],
                                              start=(n == 0), stop=(n == 2))
                mm.then_inc(s_lg, 1)
                pe.wait_ge(s_wt, 1)
                pe.wait_ge(s_b, 32)
                for g in range(NG):
                    for k in range(TPG):
                        mm = nc.tensor.transpose(lbank[0:E, k * P:(k + 1) * P], wtok[:, g * TPG + k, :], core.id32[:, :])
                    mm.then_inc(s_wT, 1)
                    pe.wait_ge(s_wTc, g + 1)
                    pe.wait_ge(s_biasd, g + 1)
                    for k in range(TPG):
                        mm = nc.tensor.matmul(ybank[0][:, k, :], wT[:, k * P:(k + 1) * P], b2[:, :], start=True, stop=True)
                    mm.then_inc(s_bias, 1)
                pe.wait_ge(s_biasd, 1 + NG)

                def first(e, g, b, k):
                    pe.wait_ge(s_ge, e * (NG * HC) + g * HC + (k + 1))
                    for n, (h, w) in enumerate(((0, 0), (1, 0), (0, 1))):
                        mm = nc.tensor.matmul(hbank[k][:, :], w1[:, b, w, k, :], xt[:, h, bass.ds(g * GW, GW)],
                                              start=(n == 0), stop=(n == 2))
                    mm.then_inc(s_h1, 1)

                def second(e, g, b, gb, k):
                    n = e * (NG * HC) + g * HC
                    pe.wait_ge(s_hl, n + (HC + k + 1))
                    if k == 0:
                        pe.wait_ge(s_add, e * NG + g + 1)
                    for t in range(TPG):
                        for i, (h, w) in enumerate(((hh, 0), (hh, 1), (hl, 0))):
                            mm = nc.tensor.matmul(ybank[gb][:, t, :], h[:, k, t * P:(t + 1) * P], w2[:, b, w, k, :],
                                                  start=(k == 0 and t == 0 and i == 0),
                                                  stop=(k == HC - 1 and t == TPG - 1 and i == 2), skip_group_check=True)
                    mm.then_inc(s_y, 1)

                LA = 2

                def turn(e, g, b, gb, follow):
                    for k in range(HC):
                        if k + LA < HC:
                            first(e, g, b, k + LA)
                        elif follow == "group":
                            first(e, g + 1, b, k + LA - HC)
                        elif follow == "expert":
                            if k + LA == HC:
                                pe.wait_ge(s_ws, e + 3)
                            first(e + 1, 0, 1 - b, k + LA - HC)
                        second(e, g, b, gb, k)

                def expert(e, b, last):
                    with pe.Fori(0, NG // 2 - 1) as g2:
                        for gb in range(2):
                            turn(e, g2 * 2 + gb, b, gb, "group")
                    turn(e, NG - 2, b, 0, "group")
                    turn(e, NG - 1, b, 1, None if last else "expert")

                pe.wait_ge(s_ws, 2)
                for k in range(LA):
                    first(0, 0, 0, k)
                EL = E - 1 if E % 2 else E - 2
                with pe.Fori(0, EL // 2) as e2:
                    for b in range(2):
                        expert(e2 * 2 + b, b, False)
                for e in range(EL, E):
                    expert(e, e % 2, e == E - 1)


def aggregate(core, io):
    nc, x, V, sem = core.nc, core.x, core.V, core.sem
    W = P + 1
    norm = core.norms + 1
    with ExitStack() as c:
        def sb(name, shape, dt=F32):
            return core.sb(c, name, shape, dt)

        s = split_tensors(core, c, "g")
        xs, xh, xt, turn, (s_n, s_h, s_l, s_t, s_c) = s
        kf = sb("kernf", [P, P])
        ks = sb("kerns", [P, 2, P], F16)
        ys = sb("ys", [P, NT, P])
        ry = sb("ry", [P, NT, 2, W], F16)
        bias = sb("bias", [P, P])
        beta = sb("beta", [P, NT])
        adj = sb("adjg", [P, 2, CJ, GW])
        ah = sb("ah", [P, 2, CJ, GW], F16)
        al = sb("al", [P, 2, CJ, GW], F16)
        acc = sb("accg", [P, TPG, 2 * W])
        num = sb("numg", [P, TPG, W])
        sc = sb("scg", [P, TPG])
        bank = [core.ps(c, f"agg{b}", [P, 512], F32) for b in range(7)]
        s_par = sem("kernel_loaded")
        s_ks = sem("kernel_split")
        s_one = sem("ones_ready")
        s_y = sem("y_summed")
        s_yc = sem("y_copied")
        s_yh, s_yl = sem("y_hi"), sem("y_lo")
        s_adj = [sem(f"adjg_loaded{b}") for b in range(2)]
        s_ah, s_al = sem("adj_hi"), sem("adj_lo")
        s_pe = sem("adj_parts_used")
        s_acc = sem("sums_copied")
        s_done = sem("group_done")
        with nc.Block() as block:

            @block.sync
            def _(sp):
                sp.dma_start(kf[:, :], io["L1_gnn_kernel"]).then_inc(s_par, 16)
                sp.dma_start(bias[:, :], io["L1_gnn_bias"].partition_broadcast(P)).then_inc(s_par, 16)
                sp.dma_start(beta[:, :], io["L1_gnn_beta"]).then_inc(s_par, 16)
                with sp.Fori(0, NC // 2) as n2:
                    for b in range(2):
                        n = n2 * 2 + b
                        sp.wait_ge(s_al, n + 1)
                        sp.dma_start(adj[:, b, :, :], io["adj"][bass.ds(n, 1)].squeeze(0)).then_inc(s_adj[b], 16)

            @block.gpsimd
            def _(pool):
                nc.gpsimd.memset(ry[:, :, 0, P:W], 1.0)
                nc.gpsimd.memset(ry[:, :, 1, P:W], 0.0).then_inc(s_one, 1)

            @block.scalar
            def _(act):
                split_scalar(core, s, norm)
                with act.Fori(0, NG) as g:
                    act.wait_ge(s_y, g + 1)
                    nc.scalar.activation(tiles(ys, g), bank[0][:, :].rearrange("p (t f) -> p t f", f=P), ACT.Copy,
                                         scale=1.0 / SC).then_inc(s_yc, 1)
                    act.wait_ge(s_yc, g + 1)
                    nc.scalar.activation(tiles(ry, g)[:, :, 0, 0:P], tiles(ys, g), ACT.Copy).then_inc(s_yh, 1)

                def parts(g, q0, q1):
                    for q in range(q0, q1):
                        act.wait_ge(s_adj[q % 2], g * (NQ // 2 * 16) + (q // 2 + 1) * 16)
                        act.wait_ge(s_pe, g * NQ + (q + 1))
                        nc.scalar.activation(ah[:, q % 2], adj[:, q % 2], ACT.Copy).then_inc(s_ah, 1)

                def copy_out(g):
                    act.wait_ge(s_pe, g * NQ + (2 + NQ))
                    act.wait_ge(s_done, g + 1)
                    for t in range(TPG):
                        ins = nc.scalar.activation(acc[:, t, :], bank[t][:, 0:2 * W], ACT.Copy)
                    ins.then_inc(s_acc, 1)

                parts(0, 0, 1)
                with act.Fori(0, NG - 1) as g:
                    parts(g, 1, NQ)
                    parts(g + 1, 0, 1)
                    copy_out(g)
                parts(NG - 1, 1, NQ)
                copy_out(NG - 1)

            @block.vector
            def _(dve):
                dve.sem_inc(s_al, 2)
                dve.sem_inc(s_done, 1)
                dve.wait_ge(s_par, 48)
                V.link(nc.vector.tensor_scalar(ks[:, 0, :], kf[:, :], SC, None, ALU.mult))
                nc.vector.scalar_tensor_tensor(out=ks[:, 1, :], in0=kf[:, :], scalar=SC, in1=ks[:, 0, :],
                                               op0=ALU.mult, op1=ALU.subtract).then_inc(s_ks, 1)
                split_vector(core, s)
                with dve.Fori(0, NG) as g:
                    dve.wait_ge(s_yh, g + 1)
                    r = tiles(ry, g)
                    nc.vector.tensor_tensor(r[:, :, 1, 0:P], tiles(ys, g), r[:, :, 0, 0:P], ALU.subtract).then_inc(s_yl, 1)

                def parts(g, q0, q1):
                    for q in range(q0, q1):
                        dve.wait_ge(s_ah, g * NQ + (q + 1))
                        nc.vector.tensor_tensor(al[:, q % 2], adj[:, q % 2], ah[:, q % 2], ALU.subtract).then_inc(s_al, 1)

                def post(g):
                    dve.wait_ge(s_acc, g + 1)
                    V.link(nc.vector.tensor_tensor(num[:, :, :], acc[:, :, 0:W], acc[:, :, W:2 * W], ALU.add))
                    V.link(nc.vector.tensor_tensor(sc[:, :], num[:, :, P], tiles(beta, g), ALU.add))
                    V.link(nc.vector.reciprocal(sc[:, :], sc[:, :]))
                    V.tick(nc.vector.tensor_scalar(sc[:, :], sc[:, :], 1.0 / SC, None, ALU.mult))
                    for k in range(TPG):
                        t = g * TPG + k
                        ins = nc.vector.scalar_tensor_tensor(out=num[:, k, 0:P], in0=ys[:, t, :], scalar=beta[:, bass.ds(t, 1)],
                                                             in1=num[:, k, 0:P], op0=ALU.mult, op1=ALU.add)
                    V.link(ins)
                    for k in range(TPG):
                        t = g * TPG + k
                        ins = nc.vector.scalar_tensor_tensor(out=x[:, t, :], in0=num[:, k, 0:P], scalar=sc[:, k:k + 1],
                                                             in1=x[:, t, :], op0=ALU.mult, op1=ALU.add)
                    V.link(ins)
                    V.link(nc.vector.tensor_tensor(tiles(x, g), tiles(x, g), bias[:, None, :].to_broadcast([P, TPG, P]), ALU.add))
                    core.stats_of_group(g)

                parts(0, 0, 1)
                with dve.Fori(0, NG - 1) as g:
                    V.loop(g, 8)
                    parts(g, 1, NQ)
                    parts(g + 1, 0, 1)
                    post(g)
                    dve.sem_inc(s_done, 1)
                V.end(NG - 1)
                parts(NG - 1, 1, NQ)
                post(NG - 1)
                V.wait()

            @block.tensor
            def _(pe):
                pe.sem_inc(s_pe, 2)
                split_tensor(core, s)
                pe.wait_ge(s_ks, 1)
                with pe.Fori(0, NG) as g:
                    pe.wait_ge(s_yc, g)
                    for k in range(TPG):
                        for i, (h, w) in enumerate(((0, 0), (0, 1), (1, 0))):
                            mm = nc.tensor.matmul(bank[0][:, k * P:(k + 1) * P], xt[:, h, bass.ds(g * GW + k * P, P)],
                                                  ks[:, w, :], start=(i == 0), stop=(i == 2))
                    mm.then_inc(s_y, 1)
                pe.wait_ge(s_yl, NG)
                pe.wait_ge(s_one, 1)
                with pe.Fori(0, NG) as g:
                    pe.wait_ge(s_acc, g)
                    for jt in range(NT):
                        q = jt // CJ
                        if jt % CJ == 0:
                            pe.wait_ge(s_al, g * NQ + (q + 3))
                        for t in range(TPG):
                            for part in range(2):
                                mm = nc.tensor.matmul(
                                    bank[t][:, 0:W if part else 2 * W],
                                    (ah, al)[part][:, q % 2, jt % CJ, t * P:(t + 1) * P],
                                    ry[:, jt, 0, :] if part else ry[:, jt, :, :].rearrange("p h w -> p (h w)"),
                                    start=(jt == 0 and part == 0), stop=(jt == NT - 1 and part == 1), skip_group_check=True)
                        if jt % CJ == CJ - 1:
                            mm.then_inc(s_pe, 1)


NAMES = ["x", "adj", "L0_gnn_h0", "L0_gnn_a", "L0_gnn_temp", "L0_ffn_Wg", "L0_ffn_bg", "L0_ffn_W1", "L0_ffn_b1",
         "L0_ffn_W2", "L0_ffn_b2", "L1_gnn_kernel", "L1_gnn_bias", "L1_gnn_beta", "L1_ffn_Wr", "L1_ffn_W1", "L1_ffn_b1",
         "L1_ffn_W2", "L1_ffn_b2"]


def build(nc, io, out):
    f1_row = nc.dram_tensor("f1_row", [NG, GW], F32).ap()
    with ExitStack() as ctx:
        core = Core(nc, ctx)
        attention(core, io, f1_row)
        experts(core, io, "a", 8, 8, io["L0_ffn_Wg"], io["L0_ffn_bg"], io["L0_ffn_W1"], io["L0_ffn_b1"],
                io["L0_ffn_W2"], io["L0_ffn_b2"], None)
        aggregate(core, io)
        experts(core, io, "b", 9, 8, io["L1_ffn_Wr"], None, io["L1_ffn_W1"], io["L1_ffn_b1"],
                io["L1_ffn_W2"], io["L1_ffn_b2"], out)


def kernel(**inputs):
    import numpy as np
    import concourse.bacc as bacc
    from concourse import mybir as mb
    from concourse.bass_utils import run_bass_kernel_spmd

    v = {n: np.asarray(a) for n, a in inputs.items()}

    def by_tile(a):
        return a.reshape(NT, P, P).transpose(1, 0, 2)

    def hidden_bias(a):
        return a.reshape(-1, HC, P).transpose(2, 0, 1)

    def second_weight(a):
        return a.reshape(-1, HC, P, P).transpose(0, 2, 1, 3).reshape(-1, P, HC * P)

    laid = {
        "x": by_tile(v["x"]),
        "adj": v["adj"].reshape(NG, GW, NQ, CJ, P).transpose(0, 2, 4, 3, 1).reshape(NC, P, CJ, GW),
        "L0_gnn_h0": by_tile(v["L0_gnn_h0"]),
        "L0_gnn_a": v["L0_gnn_a"].reshape(2, P),
        "L0_gnn_temp": v["L0_gnn_temp"],
        "L0_ffn_Wg": v["L0_ffn_Wg"], "L0_ffn_bg": v["L0_ffn_bg"],
        "L0_ffn_W1": v["L0_ffn_W1"], "L0_ffn_b1": hidden_bias(v["L0_ffn_b1"]),
        "L0_ffn_W2": second_weight(v["L0_ffn_W2"]), "L0_ffn_b2": v["L0_ffn_b2"],
        "L1_gnn_kernel": v["L1_gnn_kernel"], "L1_gnn_bias": v["L1_gnn_bias"],
        "L1_gnn_beta": v["L1_gnn_beta"].reshape(NT, P).T,
        "L1_ffn_Wr": v["L1_ffn_Wr"],
        "L1_ffn_W1": np.concatenate([v["L1_ffn_W1p"], v["L1_ffn_W1s"][None]]),
        "L1_ffn_b1": hidden_bias(np.concatenate([v["L1_ffn_b1p"], v["L1_ffn_b1s"][None]])),
        "L1_ffn_W2": second_weight(np.concatenate([v["L1_ffn_W2p"], v["L1_ffn_W2s"][None]])),
        "L1_ffn_b2": np.concatenate([v["L1_ffn_b2p"], v["L1_ffn_b2s"][None]]),
    }
    nc = bacc.Bacc("TRN2", target_bir_lowering=False, num_devices=1)
    arrays, io = {}, {}
    for name in NAMES:
        a = np.ascontiguousarray(laid[name])
        arrays[f"in_{name}"] = a
        io[name] = nc.dram_tensor(f"in_{name}", a.shape, mb.dt.from_np(a.dtype), kind="ExternalInput").ap()
    out = nc.dram_tensor("out_0", (P, NT, P), mb.dt.float32, kind="ExternalOutput").ap()
    build(nc, io, out)
    r = run_bass_kernel_spmd(nc, [arrays], core_ids=[0])
    return np.ascontiguousarray(r.results[0]["out_0"].transpose(1, 0, 2)).reshape(N, P)
```

```python
from contextlib import ExitStack

import concourse.bass as bass
from concourse import mybir

F32 = mybir.dt.float32
F16 = mybir.dt.float16
BF16 = mybir.dt.bfloat16
ALU = mybir.AluOpType
ACT = mybir.ActivationFunctionType
AX = mybir.AxisListType.X
RMAX = bass.bass_isa.ReduceOp.max

P = 128
N = 4096
NT = N // P
TPG = 4
GW = TPG * P
NG = NT // TPG
HC = 4
CJ = 4
NQ = NT // CJ
NC = NG * NQ
SC = 1024.0
HS = 256.0
EPS = 1e-5
THRESH = 1e-6
ALPHA = 0.2
BIG = 1e30
R = 8
HALVES = 2
HNT = NT // HALVES
SNT = -(-(2 * HNT + R - 1) // TPG) * TPG
SNG = SNT // TPG
SLOTS = SNT * P


class Ticks:

    def __init__(self, eng, sem):
        self.eng, self.sem, self.base, self.it, self.per, self.k = eng, sem, 0, None, 0, 0

    def loop(self, it, per):
        self.base, self.it, self.per, self.k = self.base + self.k, it, per, 0

    def end(self, trips):
        assert self.k == self.per, (self.k, self.per)
        self.base, self.it, self.k = self.base + trips * self.per, None, 0

    def tick(self, ins):
        ins.then_inc(self.sem, 1)
        self.k += 1

    def wait(self):
        v = self.base + self.k
        self.eng.wait_ge(self.sem, v if self.it is None else self.it * self.per + v)

    def link(self, ins):
        self.tick(ins)
        self.wait()


class Core:

    def __init__(self, nc, ctx):
        self.nc, self.ctx = nc, ctx
        self.x = self.sb(ctx, "x", [P, NT, P], F32)
        self.id16 = self.sb(ctx, "id16", [P, P], F16)
        self.id32 = self.sb(ctx, "id32", [P, P], F32)
        self.stats = self.sb(ctx, "stats", [P, NT, 6], F32)
        self.mean = self.sb(ctx, "mean", [P, NT], F32)
        self.rstd = self.sb(ctx, "rstd", [P, NT], F32)
        self.rtmp = self.sb(ctx, "rtmp", [P, NT], F32)
        self.veps = self.sb(ctx, "veps", [P, NT], F32)
        self.V = Ticks(nc.vector, self.sem("vector_chain"))
        self.A = Ticks(nc.scalar, self.sem("scalar_chain"))
        self.G = Ticks(nc.gpsimd, self.sem("gpsimd_chain"))
        self.s_zero = self.sem("slots_cleared")
        self.s_rec = self.sem("variance_reciprocal")
        self.s_root = self.sem("rstd_root")
        self.norms = 0

    def sb(self, ctx, name, shape, dt):
        return ctx.enter_context(self.nc.sbuf_tensor(name, shape, dt))

    def ps(self, ctx, name, shape, dt):
        return ctx.enter_context(self.nc.psum_tensor(name, shape, dt))

    def sem(self, name):
        return self.ctx.enter_context(self.nc.semaphore(name))

    def stats_of_group(self, g):
        nc = self.nc
        for k in range(TPG):
            ins = nc.vector.bn_stats(self.stats[:, g * TPG + k, :], self.x[:, g * TPG + k, :])
        self.V.tick(ins)

    def rstd_vector(self, scale):
        nc, V = self.nc, self.V
        self.norms += 1
        me, se, mo, so = (self.stats[:, :, i] for i in (1, 2, 4, 5))
        V.tick(nc.vector.tensor_tensor(self.mean[:, :], me, mo, ALU.add))
        V.link(nc.vector.tensor_tensor(self.rtmp[:, :], me, mo, ALU.subtract))
        V.tick(nc.vector.scalar_tensor_tensor(out=self.rtmp[:, :], in0=self.rtmp[:, :], scalar=0.25, in1=self.rtmp[:, :],
                                              op0=ALU.mult, op1=ALU.mult))
        V.link(nc.vector.tensor_tensor(self.veps[:, :], se, so, ALU.add))
        V.tick(nc.vector.tensor_scalar(self.mean[:, :], self.mean[:, :], 0.5, None, ALU.mult))
        V.link(nc.vector.tensor_scalar(self.veps[:, :], self.veps[:, :], 1.0 / P, EPS, ALU.mult, ALU.add))
        V.link(nc.vector.tensor_tensor(self.veps[:, :], self.veps[:, :], self.rtmp[:, :], ALU.add))
        nc.vector.reciprocal(self.rtmp[:, :], self.veps[:, :]).then_inc(self.s_rec, 1)
        nc.vector.wait_ge(self.s_root, self.norms)
        V.link(nc.vector.tensor_tensor(self.rtmp[:, :], self.rstd[:, :], self.rstd[:, :], ALU.mult))
        V.link(nc.vector.tensor_tensor(self.rtmp[:, :], self.rtmp[:, :], self.veps[:, :], ALU.mult))
        V.link(nc.vector.tensor_scalar(self.rtmp[:, :], self.rtmp[:, :], -0.5 * scale, 1.5 * scale, ALU.mult, ALU.add))
        V.link(nc.vector.tensor_tensor(self.rstd[:, :], self.rstd[:, :], self.rtmp[:, :], ALU.mult))

    def rstd_scalar(self, n):
        self.nc.scalar.wait_ge(self.s_rec, n)
        self.nc.scalar.activation(self.rstd[:, :], self.rtmp[:, :], ACT.Sqrt).then_inc(self.s_root, 1)

    def normalise_group(self, out, g):
        for k in range(TPG):
            t = g * TPG + k
            ins = self.nc.vector.tensor_scalar(out[:, t, :], self.x[:, t, :], self.mean[:, bass.ds(t, 1)],
                                               self.rstd[:, bass.ds(t, 1)], ALU.subtract, ALU.mult)
        return ins


def tiles(t, g):
    return t[:, bass.ds(g * TPG, TPG)]


def over_columns(t, width):
    return t.unsqueeze(2).to_broadcast([P, t.shape[1], width])


def attention(core, io, f1_row, x_rows):
    nc, x, V, G, sem = core.nc, core.x, core.V, core.G, core.sem
    RING = 4
    AHEAD = RING - 1
    AHEAD_S = AHEAD + 2
    M_START = 2 * NQ
    STEEP = 2.0 ** 100
    W = (P + 2, P)
    with ExitStack() as c:
        def sb(name, shape, dt=F32):
            return core.sb(c, name, shape, dt)

        xn = sb("xn", [P, NT, P])
        feat = sb("feat", [P, NT, P])
        rb = [sb(f"rb{k}", [P, NT, 2, W[k]], F16) for k in range(2)]
        rd = [sb(f"rd{k}", [P, NT, 2, W[k]], F16) for k in range(2)]
        adj = sb("adj", [P, 2, CJ, GW])
        edge = sb("edge", [P, RING, CJ, GW], BF16)
        f1g = sb("f1g", [P, 2, GW])
        pos = sb("pos", [P, 2, CJ, GW], BF16)
        m1 = sb("m1", [P, RING, CJ, GW], BF16)
        m2 = sb("m2", [P, RING, CJ, GW], BF16)
        acc_a = sb("acc_a", [P, TPG, 2 * W[0]])
        acc_c = sb("acc_c", [P, TPG, 2 * W[0]])
        num = sb("num", [P, TPG, W[0]])
        vb = sb("vb", [P, TPG, P])
        vd = sb("vd", [P, TPG, P])
        a_bc = acc_c[:, 0:2, 0:P]
        f1t = acc_a[0:NT, 0, 0:P]
        temp = sb("temp", [P, 5])
        coe = sb("coe", [P, 5])
        om = sb("om", [P, 5])
        f1, f2, steep, z, ca, cc, wb, wd, wb2, wd2, den, rden, rows, kx, kf, kp, sq = (
            sb(f"col_{n}", [P, NT]) for n in ("f1", "f2", "steep", "z", "ca", "cc", "wb", "wd", "wb2", "wd2",
                                             "den", "rden", "rows", "kx", "kf", "kp", "sq"))
        fmax = sb("fmax", [P, 1])
        fall = sb("fall", [P, 1])
        nfall = sb("nfall", [P, 2])
        cf = sb("cf", [P, 2])
        zero = sb("zero", [P, 2 * P], F16)
        bank = [core.ps(c, f"bank{b}", [P, 512], F32) for b in range(2 * TPG)]

        s_x, s_par, s_h0 = sem("x_loaded"), sem("a_and_temp_loaded"), sem("h0_loaded")
        s_id = sem("identities_ready")
        s_z0 = sem("zeros_ready")
        s_f1, s_f1T, s_f1s, s_f1d = sem("f1_ready"), sem("f1_transposed"), sem("f1_rows_copied"), sem("f1_in_dram")
        s_fmax, s_fall, s_z = sem("f2_max_of_partitions"), sem("f2_max"), sem("exponents_ready")
        s_exp = sem("exponentials_ready")
        s_w = sem("b_and_d_ready")
        s_vb, s_vd, s_hb, s_hd = sem("b_rows"), sem("d_rows"), sem("b_rows_hi"), sem("d_rows_hi")
        s_rb, s_rd = sem("b_operands_ready"), sem("d_operands_ready")
        s_adj = [sem(f"adj_loaded{b}") for b in range(2)]
        s_f1g = [sem(f"f1_group_loaded{b}") for b in range(2)]
        s_edge = sem("edges_ready")
        s_pos = sem("pos_ready")
        s_m1, s_m2p, s_m2v = sem("mask1_ready"), sem("mask2_by_gpsimd"), sem("mask2_by_vector")
        s_pe = sem("mask_slots_free")
        s_ea, s_ec = sem("a_banks_copied"), sem("c_banks_copied")
        s_feat = sem("feat_ready")

        with nc.Block() as block:

            @block.sync
            def _(sp):
                sp.dma_start(x[:, :, :], io["x"]).then_inc(s_x, 16)
                sp.dma_start(a_bc, io["L0_gnn_a"].partition_broadcast(P)).then_inc(s_par, 16)
                sp.dma_start(temp[:, :], io["L0_gnn_temp"].partition_broadcast(P)).then_inc(s_par, 16)
                sp.dma_start(feat[:, :, :], io["L0_gnn_h0"]).then_inc(s_h0, 16)
                sp.wait_ge(s_z0, 1)
                for rows in x_rows:
                    sp.dma_start(rows.rearrange("(t p) f -> p t f", p=P),
                                 zero[:, None, :].to_broadcast([P, SNT, 2 * P])).then_inc(core.s_zero, 16)
                sp.wait_ge(s_f1s, 1)
                sp.dma_start(f1_row.rearrange("g (t p) -> (g t) p", p=P), f1t).then_inc(s_f1d, 16)
                sp.wait_ge(s_f1d, 16)
                for k in range(2):
                    with sp.Fori(0, NG // 2) as g2:
                        for b in range(2):
                            g = g2 * 2 + (k * NG + b)
                            sp.wait_ge(s_m1, (g + 1) * NQ)
                            sp.dma_start(f1g[:, b, :], f1_row[bass.ds(g2 * 2 + b, 1), :].squeeze(0)
                                         .partition_broadcast(P)).then_inc(s_f1g[b], 16)
                            for q in range(NQ):
                                sp.wait_ge(s_edge, g * NQ + (q + 1))
                                sp.dma_start(adj[:, q % 2, :, :], io["adj"][bass.ds((g2 * 2 + b) * NQ + q, 1)].squeeze(0)
                                             ).then_inc(s_adj[q % 2], 16)

            @block.gpsimd
            def _(pool):
                nc.gpsimd.memset(zero[:, :], 0.0).then_inc(s_z0, 1)
                for m in (core.id16, core.id32):
                    G.link(nc.gpsimd.memset(m[:, :], 0.0))
                    nc.gpsimd.affine_select(out=m[:, :], in_=m[:, :], compare_op=ALU.not_equal, fill=1.0, base=0,
                                            pattern=[[-1, P]], channel_multiplier=1).then_inc(s_id, 1)
                pool.sem_inc(s_m2p, M_START)
                pool.wait_ge(s_fmax, 1)
                nc.gpsimd.partition_all_reduce(fall[:, :], fmax[:, :], P, RMAX).then_inc(s_fall, 1)
                with pool.Fori(0, 2 * NC // RING) as n4:
                    for r in range(RING):
                        pool.wait_ge(s_m1, n4 * RING + (M_START + r + 1))
                        nc.gpsimd.tensor_tensor(m2[:, r, 1:CJ, :], edge[:, r, 1:CJ, :], m1[:, r, 1:CJ, :],
                                                ALU.subtract).then_inc(s_m2p, 1)

            @block.scalar
            def _(act):
                act.sem_inc(s_ea, TPG)
                act.wait_ge(s_par, 32)
                nc.scalar.activation(coe[:, :], temp[:, :], ACT.Exp, scale=-1.0).then_inc(s_exp, 1)
                core.rstd_scalar(1)
                act.wait_ge(s_z, 1)
                nc.scalar.activation(wb[:, :], f2[:, :], ACT.Exp, bias=nfall[:, 0:1], scale=1.0).then_inc(s_exp, 1)
                nc.scalar.activation(wd[:, :], f2[:, :], ACT.Exp, bias=nfall[:, 1:2], scale=ALPHA).then_inc(s_exp, 1)
                nc.scalar.activation(ca[:, :], ca[:, :], ACT.Exp).then_inc(s_exp, 1)
                nc.scalar.activation(cc[:, :], cc[:, :], ACT.Exp).then_inc(s_exp, 1)

                def hi_b(k, g):
                    act.wait_ge(s_vb, g + (k * NG + 1))
                    nc.scalar.activation(tiles(rb[k], g)[:, :, 0, 0:P], vb[:, :, :], ACT.Copy).then_inc(s_hb, 1)

                def d_rows(k, g):
                    if k == 1:
                        act.wait_ge(s_feat, g + 1)
                    act.wait_ge(s_rd, g + (k * NG + 1))
                    for i in range(TPG):
                        t = g * TPG + i
                        ins = nc.scalar.activation(vd[:, i, :], (feat if k else xn)[:, t, :], ACT.Copy,
                                                   scale=wd[:, bass.ds(t, 1)])
                    ins.then_inc(s_vd, 1)
                    act.wait_ge(s_vd, g + (k * NG + 1))
                    nc.scalar.activation(tiles(rd[k], g)[:, :, 0, 0:P], vd[:, :, :], ACT.Copy).then_inc(s_hd, 1)

                def compare(g, b, q0, q1):
                    for q in range(q0, q1):
                        act.wait_ge(s_m1, g * NQ + (M_START + q - 1))
                        if q == 0:
                            act.wait_ge(s_f1g[b], (g + (2 - b)) * 8)
                        for i in range(CJ):
                            jt = q * CJ + i
                            ins = nc.scalar.activation(pos[:, q % 2, i, :], f1g[:, b, :], ACT.Sigmoid,
                                                       bias=steep[:, jt:jt + 1], scale=STEEP)
                        ins.then_inc(s_pos, 1)

                def copy_out(k, g):
                    act.wait_ge(s_pe, g * NQ + (k * NC + RING + NQ))
                    act.wait_ge(s_feat, g + k * NG)
                    for t in range(TPG):
                        nc.scalar.activation(acc_a[:, t, 0:2 * W[k]], bank[2 * t][:, 0:2 * W[k]], ACT.Copy,
                                             scale=ca[:, bass.ds(g * TPG + t, 1)]).then_inc(s_ea, 1)

                act.wait_ge(s_w, 1)
                with act.Fori(0, NG) as g:
                    d_rows(0, g)
                    hi_b(0, g)
                compare(0, 0, 0, NQ)
                compare(1, 1, 0, AHEAD_S)
                for k in range(2):
                    with act.Fori(0, NG // 2 - k) as g2:
                        for b in range(2):
                            g = g2 * 2 + b
                            copy_out(k, g)
                            if k == 0:
                                d_rows(1, g)
                                hi_b(1, g)
                            compare(g + (k * NG + 1), 1 - b, AHEAD_S, NQ)
                            compare(g + (k * NG + 2), b, 0, AHEAD_S)
                copy_out(1, NG - 2)
                compare(2 * NG - 1, 1, AHEAD_S, NQ)
                copy_out(1, NG - 1)

            @block.tensor
            def _(pe):
                pe.sem_inc(s_pe, RING)
                pe.wait_ge(s_id, 2)
                pe.wait_ge(s_f1, 1)
                nc.tensor.transpose(bank[0][0:NT, 0:P], f1[:, :], core.id32[:, :]).then_inc(s_f1T, 1)
                for k in range(2):
                    pe.wait_ge(s_rb, (k + 1) * (NG + 1) - k)
                    pe.wait_ge(s_rd, (k + 1) * NG)
                    with pe.Fori(0, NG) as g:
                        for jt in range(NT):
                            q = jt // CJ
                            if jt % CJ == 0:
                                pe.wait_ge(s_m2p, g * NQ + (k * NC + M_START + q + 1))
                                pe.wait_ge(s_m2v, g * NQ + (k * NC + M_START + q + 1))
                            for t in range(TPG):
                                for m, r, o in ((m1, rb, 0), (m2, rd, 1)):
                                    if jt == 0:
                                        pe.wait_ge((s_ea, s_ec)[o], g * TPG + (k * NT + t + 1))
                                    mm = nc.tensor.matmul(bank[2 * t + o][:, 0:2 * W[k]], m[:, q % RING, jt % CJ, t * P:(t + 1) * P],
                                                          r[k][:, jt, :, :].rearrange("p h w -> p (h w)"),
                                                          start=(jt == 0), stop=(jt == NT - 1))
                            if jt % CJ == CJ - 1:
                                mm.then_inc(s_pe, 1)

            @block.vector
            def _(dve):
                dve.sem_inc(s_m1, M_START)
                dve.sem_inc(s_m2v, M_START)
                dve.sem_inc(s_edge, 2)
                dve.sem_inc(s_rd, 1)
                dve.sem_inc(s_ec, TPG)
                dve.wait_ge(s_x, 16)
                with dve.Fori(0, NG) as g:
                    V.loop(g, 1)
                    core.stats_of_group(g)
                V.end(NG)
                V.wait()
                core.rstd_vector(1.0)
                with dve.Fori(0, NG) as g:
                    V.loop(g, 1)
                    V.tick(core.normalise_group(xn, g))
                V.end(NG)
                V.wait()
                dve.wait_ge(s_par, 32)
                with dve.Fori(0, NG) as g:
                    V.loop(g, 4)
                    for h, f in ((0, f1), (1, f2)):
                        V.link(nc.vector.tensor_tensor(vb[:, :, :], tiles(xn, g), a_bc[:, h:h + 1, :].to_broadcast([P, TPG, P]),
                                                       ALU.mult))
                        V.link(nc.vector.tensor_reduce(tiles(f, g), vb[:, :, :], AX, ALU.add))
                V.end(NG)
                dve.sem_inc(s_f1, 1)
                nc.vector.tensor_reduce(fmax[:, :], f2[:, :], AX, ALU.max).then_inc(s_fmax, 1)
                V.tick(nc.vector.tensor_scalar(steep[:, :], f2[:, :], STEEP, None, ALU.mult))
                dve.wait_ge(s_exp, 1)
                V.link(nc.vector.tensor_scalar(coe[:, :], coe[:, :], 1.0, None, ALU.add))
                V.link(nc.vector.reciprocal(coe[:, :], coe[:, :]))
                V.link(nc.vector.tensor_scalar(om[:, :], coe[:, :], -1.0, 1.0, ALU.mult, ALU.add))
                V.tick(nc.vector.tensor_tensor(cf[:, 0:1], om[:, 1:2], coe[:, 0:1], ALU.mult))
                V.link(nc.vector.tensor_tensor(cf[:, 1:2], om[:, 1:2], om[:, 0:1], ALU.mult))
                dve.wait_ge(s_f1T, 1)
                nc.vector.tensor_copy(f1t, bank[0][0:NT, 0:P]).then_inc(s_f1s, 1)
                dve.wait_ge(s_fall, 1)
                V.tick(nc.vector.tensor_scalar(nfall[:, 0:1], fall[:, :], -1.0, None, ALU.mult))
                V.tick(nc.vector.tensor_scalar(nfall[:, 1:2], fall[:, :], -ALPHA, None, ALU.mult))
                V.link(nc.vector.tensor_scalar(z[:, :], f1[:, :], fall[:, 0:1], None, ALU.add))
                V.link(nc.vector.scalar_tensor_tensor(out=kx[:, :], in0=z[:, :], scalar=ALPHA, in1=z[:, :],
                                                      op0=ALU.mult, op1=ALU.max))
                V.tick(nc.vector.tensor_tensor(ca[:, :], z[:, :], kx[:, :], ALU.subtract))
                V.link(nc.vector.scalar_tensor_tensor(out=cc[:, :], in0=z[:, :], scalar=ALPHA, in1=kx[:, :],
                                                      op0=ALU.mult, op1=ALU.subtract))
                dve.sem_inc(s_z, 1)
                dve.wait_ge(s_h0, 16)
                V.tick(nc.vector.scalar_tensor_tensor(out=x[:, :, :], in0=feat[:, :, :], scalar=cf[:, 1:2], in1=x[:, :, :],
                                                      op0=ALU.mult, op1=ALU.add))
                dve.wait_ge(s_exp, 5)
                V.tick(nc.vector.scalar_tensor_tensor(out=wb2[:, :], in0=wb[:, :], scalar=SC, in1=wb[:, :], op0=ALU.mult, op1=ALU.mult))
                V.link(nc.vector.scalar_tensor_tensor(out=wd2[:, :], in0=wd[:, :], scalar=SC, in1=wd[:, :], op0=ALU.mult, op1=ALU.mult))
                V.tick(nc.vector.tensor_scalar(wb[:, :], wb[:, :], SC, None, ALU.mult))
                V.link(nc.vector.tensor_scalar(wd[:, :], wd[:, :], SC, None, ALU.mult))
                dve.sem_inc(s_w, 1)
                for r, w, w2 in ((rb[0], wb, wb2), (rd[0], wd, wd2)):
                    V.tick(nc.vector.tensor_copy(r[:, :, 0, P], w[:, :]))
                    V.link(nc.vector.tensor_copy(r[:, :, 0, P + 1], w2[:, :]))
                    V.tick(nc.vector.tensor_tensor(r[:, :, 1, P], w[:, :], r[:, :, 0, P], ALU.subtract))
                    V.link(nc.vector.tensor_tensor(r[:, :, 1, P + 1], w2[:, :], r[:, :, 0, P + 1], ALU.subtract))
                dve.sem_inc(s_rb, 1)

                def b_rows(k, g):
                    dve.wait_ge(s_rb, g + (k * NG + 1))
                    nc.vector.tensor_tensor(vb[:, :, :], tiles(feat if k else xn, g), over_columns(tiles(wb, g), P),
                                            ALU.mult).then_inc(s_vb, 1)

                def lo_rows(k, g):
                    for v, r, s_v, s_hi, s_r in ((vd, rd, s_vd, s_hd, s_rd), (vb, rb, s_vb, s_hb, s_rb)):
                        dve.wait_ge(s_v, g + (k * NG + 1))
                        dve.wait_ge(s_hi, g + (k * NG + 1))
                        r = tiles(r[k], g)
                        nc.vector.tensor_tensor(r[:, :, 1, 0:P], v[:, :, :], r[:, :, 0, 0:P], ALU.subtract).then_inc(s_r, 1)

                with dve.Fori(0, NG) as g:
                    b_rows(0, g)
                    lo_rows(0, g)

                def edges(g, q):
                    dve.wait_ge(s_adj[q % 2], g * (NQ // 2 * 16) + (q // 2 + 1) * 16)
                    dve.wait_ge(s_m2p, g * NQ + (M_START + q + 1 - RING))
                    dve.wait_ge(s_m2v, g * NQ + (M_START + q + 1 - RING))
                    nc.vector.tensor_scalar(edge[:, q % RING], adj[:, q % 2], 0.0, None, ALU.is_gt).then_inc(s_edge, 1)

                def masks(g, q0, q1, more=True):
                    for q in range(q0, q1):
                        if q + 1 < NQ:
                            edges(g, q + 1)
                        elif more:
                            edges(g + 1, 0)
                        n = g * NQ + (q + 1)
                        dve.wait_ge(s_edge, n + 2)
                        dve.wait_ge(s_pos, n)
                        dve.wait_ge(s_pe, n)
                        r = q % RING
                        nc.vector.tensor_tensor(m1[:, r], edge[:, r], pos[:, q % 2], ALU.mult).then_inc(s_m1, 1)
                        dve.wait_ge(s_m1, n + M_START)
                        nc.vector.tensor_tensor(m2[:, r, 0, :], edge[:, r, 0, :], m1[:, r, 0, :], ALU.subtract).then_inc(s_m2v, 1)

                def sums(k, g):
                    w = W[k]
                    dve.wait_ge(s_pe, g * NQ + (k * NC + RING + NQ))
                    for t in range(TPG):
                        nc.vector.tensor_scalar(acc_c[:, t, 0:2 * w], bank[2 * t + 1][:, 0:2 * w],
                                                cc[:, bass.ds(g * TPG + t, 1)], None, ALU.mult).then_inc(s_ec, 1)
                    dve.wait_ge(s_ec, g * TPG + (k * NT + 2 * TPG))
                    dve.wait_ge(s_ea, g * TPG + (k * NT + 2 * TPG))
                    if k == 0:
                        s, d = tiles(sq, g), tiles(den, g)
                        V.tick(nc.vector.tensor_tensor(s, acc_a[:, :, w - 1], acc_a[:, :, 2 * w - 1], ALU.add))
                        V.link(nc.vector.tensor_tensor(d, acc_c[:, :, w - 1], acc_c[:, :, 2 * w - 1], ALU.add))
                        V.tick(nc.vector.tensor_tensor(s, s, tiles(ca, g), ALU.mult))
                        V.link(nc.vector.tensor_tensor(d, d, tiles(cc, g), ALU.mult))
                        V.tick(nc.vector.tensor_tensor(s, s, d, ALU.add))
                    V.link(nc.vector.tensor_tensor(acc_c[:, :, 0:2 * w], acc_c[:, :, 0:2 * w], acc_a[:, :, 0:2 * w], ALU.add))
                    V.link(nc.vector.tensor_tensor(num[:, :, 0:w], acc_c[:, :, 0:w], acc_c[:, :, w:2 * w], ALU.add))

                def first_post(g):
                    sums(0, g)
                    V.link(nc.vector.reciprocal(tiles(rden, g), num[:, :, P]))
                    V.link(nc.vector.tensor_tensor(tiles(den, g), tiles(rden, g), tiles(rden, g), ALU.mult))
                    V.link(nc.vector.scalar_tensor_tensor(out=tiles(rows, g), in0=tiles(den, g), scalar=0.5 * SC,
                                                          in1=tiles(sq, g), op0=ALU.mult, op1=ALU.mult))
                    V.link(nc.vector.tensor_scalar(tiles(kx, g), tiles(rows, g), -1.0, om[:, 2:3], ALU.mult, ALU.add))
                    for k in range(TPG):
                        t = g * TPG + k
                        ins = nc.vector.tensor_scalar(feat[:, t, :], xn[:, t, :], kx[:, bass.ds(t, 1)], None, ALU.mult)
                    V.link(ins)
                    for k in range(TPG):
                        t = g * TPG + k
                        ins = nc.vector.scalar_tensor_tensor(out=feat[:, t, :], in0=num[:, k, 0:P], scalar=rden[:, bass.ds(t, 1)],
                                                             in1=feat[:, t, :], op0=ALU.mult, op1=ALU.add)
                    V.link(ins)
                    dve.wait_ge(s_rb, g + (NG + 1))
                    V.link(nc.vector.tensor_scalar(vb[:, :, :], tiles(feat, g), THRESH, -THRESH, ALU.min, ALU.max))
                    nc.vector.tensor_tensor(tiles(feat, g), tiles(feat, g), vb[:, :, :], ALU.subtract).then_inc(s_feat, 1)
                    dve.wait_ge(s_feat, g + 1)
                    b_rows(1, g)

                def second_post(g):
                    sums(1, g)
                    for k in range(TPG):
                        t = g * TPG + k
                        ins = nc.vector.scalar_tensor_tensor(out=x[:, t, :], in0=num[:, k, 0:P], scalar=kp[:, bass.ds(t, 1)],
                                                             in1=x[:, t, :], op0=ALU.mult, op1=ALU.add)
                    ins.then_inc(s_feat, 1)
                    dve.wait_ge(s_feat, g + (NG + 1))
                    for k in range(TPG):
                        t = g * TPG + k
                        ins = nc.vector.scalar_tensor_tensor(out=x[:, t, :], in0=feat[:, t, :], scalar=kf[:, bass.ds(t, 1)],
                                                             in1=x[:, t, :], op0=ALU.mult, op1=ALU.add)
                    V.link(ins)
                    core.stats_of_group(g)

                FIRST_TICKS, SECOND_TICKS = 14, 4
                edges(0, 0)
                masks(0, 0, NQ)
                masks(1, 0, AHEAD)
                with dve.Fori(0, NG // 2) as g2:
                    V.loop(g2, 2 * FIRST_TICKS)
                    for b in range(2):
                        g = g2 * 2 + b
                        first_post(g)
                        masks(g + 1, AHEAD, AHEAD + 1)
                        lo_rows(1, g)
                        masks(g + 1, AHEAD + 1, NQ)
                        masks(g + 2, 0, AHEAD)
                V.end(NG // 2)
                V.link(nc.vector.tensor_scalar(kf[:, :], rows[:, :], coe[:, 1:2], cf[:, 0:1], ALU.mult, ALU.add))
                V.link(nc.vector.tensor_scalar(kp[:, :], kf[:, :], coe[:, 3:4], None, ALU.mult))
                V.link(nc.vector.tensor_scalar(kp[:, :], kp[:, :], -1.0, coe[:, 1:2], ALU.mult, ALU.add))
                V.link(nc.vector.tensor_tensor(kp[:, :], kp[:, :], rden[:, :], ALU.mult))
                with dve.Fori(0, NG // 2 - 1) as g2:
                    V.loop(g2, 2 * SECOND_TICKS)
                    for b in range(2):
                        g = g2 * 2 + b
                        second_post(g)
                        masks(g + (NG + 1), AHEAD, NQ)
                        masks(g + (NG + 2), 0, AHEAD)
                V.end(NG // 2 - 1)
                second_post(NG - 2)
                masks(2 * NG - 1, AHEAD, NQ, more=False)
                second_post(NG - 1)
                V.wait()


def split_tensors(core, c, tag):
    xs = core.sb(c, f"xs{tag}", [P, NT, P], F32)
    xh = core.sb(c, f"xh{tag}", [P, NT, 2, P], F16)
    xt = core.sb(c, f"xt{tag}", [P, 2, N], F16)
    turn = core.ps(c, f"turn{tag}", [P, 2, GW], F16)
    sems = [core.sem(f"{n}{tag}") for n in ("xs_ready", "xs_hi_ready", "xs_lo_ready", "xs_turned", "xt_ready")]
    return xs, xh, xt, turn, sems


def split_vector(core, s, then=None):
    xs, xh, xt, turn, (s_n, s_h, s_l, s_t, s_c) = s
    nc = core.nc
    core.rstd_vector(SC)
    core.normalise_group(xs, 0).then_inc(s_n, 1)
    for g in range(NG):
        if g + 1 < NG:
            core.normalise_group(xs, g + 1).then_inc(s_n, 1)
        nc.vector.wait_ge(s_n, g + 1)
        nc.vector.wait_ge(s_h, g + 1)
        nc.vector.tensor_tensor(tiles(xh, g)[:, :, 1, :], tiles(xs, g), tiles(xh, g)[:, :, 0, :], ALU.subtract).then_inc(s_l, 1)
        if then and g:
            then(g - 1)
    if then:
        then(NG - 1)


def split_scalar(core, s, n, spare, then=None):
    xs, xh, xt, turn, (s_n, s_h, s_l, s_t, s_c) = s
    nc = core.nc
    core.rstd_scalar(n)

    def hi(g):
        nc.scalar.wait_ge(s_n, g + 1)
        nc.scalar.activation(tiles(xh, g)[:, :, 0, :], tiles(xs, g), ACT.Copy).then_inc(s_h, 1)

    hi(0)
    for g in range(NG):
        if g + 1 < NG:
            hi(g + 1)
        for h in range(2):
            nc.scalar.wait_ge(s_t, 2 * g + h + 1)
            nc.scalar.activation(xt[:, h, g * GW:(g + 1) * GW], (turn[:, 0, :], spare)[h], ACT.Copy).then_inc(s_c, 1)
        if then and g:
            then(g - 1)
    if then:
        then(NG - 1)


def split_tensor(core, s, spare, then):
    xs, xh, xt, turn, (s_n, s_h, s_l, s_t, s_c) = s
    nc = core.nc

    def turn_group(g):
        for h in range(2):
            nc.tensor.wait_ge((s_h, s_l)[h], g + 1)
            if g:
                nc.tensor.wait_ge(s_c, 2 * g - 1 + h)
            for k in range(TPG):
                mm = nc.tensor.transpose((turn[:, 0, :], spare)[h][:, k * P:(k + 1) * P], xh[:, g * TPG + k, h, :], core.id16[:, :])
            mm.then_inc(s_t, 1)

    turn_group(0)
    for g in range(NG):
        if g + 1 < NG:
            turn_group(g + 1)
        nc.tensor.wait_ge(s_c, 2 * g + 2)
        then(g)


def experts(core, tag, S, wg_d, bg_d, w1_d, b1_d, w2_d, b2_d, x_rows, y_rows, out_d):
    nc, x, V, G, sem = core.nc, core.x, core.V, core.G, core.sem
    E = S + R
    norm = core.norms + 1
    RING = 4
    LA = 2
    DU, DG = S * NT, S * NG
    SG = HALVES * SNG
    EARLY = 5
    with ExitStack() as c:
        def sb(name, shape, dt=F32):
            return core.sb(c, f"{name}{tag}", shape, dt)

        s = split_tensors(core, c, tag)
        xs, xh, xt, turn, (s_n, s_h, s_l, s_t, s_c) = s
        wg = sb("wg", [P, R])
        wgs = sb("wgs", [P, 2, R], F16)
        bg = sb("bg", [P, R])
        wf = sb("wf", [P, 2, 2, HC * P])
        w1 = sb("w1", [P, 2, E, HC, P], F16)
        w2 = sb("w2", [P, 2, E, HC, P], F16)
        b1f = sb("b1f", [2 * HC, E, P])
        b1h = sb("b1h", [2 * HC, E, P], F16)
        b1s = sb("b1s", [2 * HC, E, P], F16)
        b2f = sb("b2f", [2, E, P])
        b2h = sb("b2h", [2, E, P], F16)
        b2s = sb("b2s", [2, E, P], F16)
        pick1 = sb("pick1", [2 * HC, HC, P], F16)
        pick2 = sb("pick2", [2, P], F16)
        low1 = sb("low1", [2 * HC, 1])
        low2 = sb("low2", [2, 1])
        lg = sb("lg", [P, NT, R])
        t1 = sb("t1", [P, NT, R])
        oh = sb("oh", [P, 2, NT, R])
        both = sb("both", [P, NT, R], F16)
        best = sb("best", [P, 2, NT])
        pick = sb("pick", [P, NT])
        ex = sb("ex", [P, NT])
        wt = sb("wt", [P, 2, NT])
        order = sb("order", [P, R])
        below = sb("below", [P, P], F16)
        ones = sb("ones", [P, P], F16)
        before = sb("before", [P, R, R])
        countn = sb("countn", [P, SNT], mybir.dt.int32)
        count = sb("count", [P, SNT])
        run = [sb(f"run{k}", [P, HALVES, HNT, R]) for k in range(2)]
        cnt = sb("cnt", [P, HALVES, HNT, R])
        tot = sb("tot", [P, HALVES, R])
        more = sb("more", [P, HALVES, R, HNT])
        nt = sb("nt", [P, HALVES, R])
        prod = sb("prod", [P, HALVES, R, R])
        off = sb("off", [P, HALVES, R])
        base = sb("base", [P, HALVES, R])
        past = sb("past", [P, HALVES, SNT, R])
        owner = sb("owner", [P, HALVES, SNT])
        own = sb("own", [P, HALVES * SNT], mybir.dt.int32)
        slotf = sb("slotf", [P, 2, NT])
        slot = sb("slot", [P, 2, NT], mybir.dt.uint32)
        xg = sb("xg", [P, 2, TPG, 2 * P], F16)
        xgt = sb("xgt", [P, 2, 2, GW], F16)
        h32 = sb("h32", [P, RING, GW])
        hh = sb("hh", [P, RING, GW], F16)
        hl = sb("hl", [P, RING, GW], F16)
        yo = sb("yo", [P, 2, TPG, P])
        got = sb("got", [P, NT, 2, P])
        hbank = [core.ps(c, f"hid{tag}_{k}", [P, GW], F32) for k in range(RING)]
        ybank = [core.ps(c, f"y{tag}_{k}", [P, TPG, P], F32) for k in range(2)]
        lbank = core.ps(c, f"logits{tag}", [P, 2, NT * R], F32)
        spare = hbank[RING - 1][:, :].bitcast(F16)[:, 0:GW]

        s_wg = sem(f"gate_loaded{tag}")
        s_b = sem(f"biases_loaded{tag}")
        s_bs = sem(f"biases_split{tag}")
        s_w = [sem(f"weights_loaded{tag}{b}") for b in range(2)]
        s_ws = sem(f"weights_split{tag}")
        s_wgs = sem(f"gate_split{tag}")
        s_lg = sem(f"logits_summed{tag}")
        s_const = sem(f"constants_ready{tag}")
        s_d, s_ex = sem(f"logit_gap{tag}"), sem(f"gap_exp{tag}")
        s_both, s_rank = sem(f"choices_ready{tag}"), sem(f"ranks_summed{tag}")
        s_slot, s_own = sem(f"slots_ready{tag}"), sem(f"owners_ready{tag}")
        s_sc = [sem(f"half_scattered{tag}{h}") for h in range(HALVES)]
        s_xg = [sem(f"slot_rows_loaded{tag}{b}") for b in range(2)]
        s_xgt = sem(f"slot_rows_turned{tag}")
        s_xgc = sem(f"turned_copied{tag}")
        s_h1 = sem(f"hidden_summed{tag}")
        s_ge = sem(f"gelu_done{tag}")
        s_hh, s_hl = sem(f"hidden_hi{tag}"), sem(f"hidden_lo{tag}")
        s_y = sem(f"unit_done{tag}")
        s_add = sem(f"dense_added{tag}")
        s_yo = sem(f"y_copied{tag}")
        s_st = [sem(f"y_stored{tag}{b}") for b in range(2)]
        s_got = [sem(f"y_gathered{tag}{g}") for g in range(NG)]
        s_res = sem(f"group_done{tag}")
        s_out = sem(f"stored{tag}")

        with nc.Block() as block:

            @block.sync
            def _(sp):
                sp.sem_inc(s_st[0], 16)
                sp.sem_inc(s_st[1], 16)
                sp.dma_start(wg[:, :], wg_d).then_inc(s_wg, 16)
                if bg_d is not None:
                    sp.dma_start(bg[:, :], bg_d.partition_broadcast(P)).then_inc(s_wg, 16)
                for h in range(2):
                    sp.dma_start(b1f[h * HC:(h + 1) * HC, :, :], b1_d).then_inc(s_b, 16)
                    sp.dma_start(b2f[h:h + 1, :, :], b2_d[None, :, :]).then_inc(s_b, 16)
                for e in range(E):
                    sp.wait_ge(s_ws, e + 1)
                    sp.dma_start(wf[:, e % 2, 0, :], w1_d[e]).then_inc(s_w[e % 2], 16)
                    sp.dma_start(wf[:, e % 2, 1, :], w2_d[e]).then_inc(s_w[e % 2], 16)

                def of_group(rows, g):
                    return rows.rearrange("(g t p) f -> g p t f", p=P, t=TPG)[bass.ds(g, 1)].squeeze(0)

                def load(h, g, b):
                    sp.wait_ge(s_xgt, g + (h * SNG + 1))
                    sp.dma_start(xg[:, b, :, :], of_group(x_rows[h], g)).then_inc(s_xg[b], 16)

                def store(h, g, b):
                    sp.wait_ge(s_yo, g + (h * SNG + 3))
                    sp.dma_start(of_group(y_rows[h], g), yo[:, b, :, :]).then_inc(s_st[b], 16)

                for h in range(HALVES):
                    sp.wait_ge(s_sc[h], 2 * HNT * 16)
                    load(h, 0, 0)
                    load(h, 1, 1)
                    if h:
                        store(h - 1, SNG - 2, 0)
                        store(h - 1, SNG - 1, 1)
                    with sp.Fori(0, SNG // 2 - 1) as g2:
                        for b in range(2):
                            load(h, g2 * 2 + (b + 2), b)
                            store(h, g2 * 2 + b, b)
                store(HALVES - 1, SNG - 2, 0)
                store(HALVES - 1, SNG - 1, 1)
                if out_d is not None:
                    for g in range(NG):
                        sp.wait_ge(s_res, g + 1)
                        sp.dma_start(tiles(out_d, g), tiles(x, g)).then_inc(s_out, 16)
                    sp.wait_ge(s_out, 16 * NG)

            @block.gpsimd
            def _(pool):
                for k in range(R):
                    nc.gpsimd.memset(order[:, k:k + 1], float(R - k))
                G.link(nc.gpsimd.memset(ones[:, :], 1.0))
                nc.gpsimd.affine_select(out=below[:, :], in_=ones[:, :], compare_op=ALU.is_gt, fill=0.0, base=0,
                                        pattern=[[1, P]], channel_multiplier=-1)
                G.link(nc.gpsimd.memset(before[:, :, :], 1.0))
                nc.gpsimd.affine_select(out=before[:, :, :], in_=before[:, :, :], compare_op=ALU.is_gt, fill=0.0, base=0,
                                        pattern=[[1, R], [-1, R]], channel_multiplier=0)
                G.link(nc.gpsimd.iota(countn[:, :], [[1, SNT]], base=0, channel_multiplier=0))
                nc.gpsimd.tensor_copy(count[:, :], countn[:, :]).then_inc(s_const, 1)
                G.tick(nc.gpsimd.memset(pick2[:, :], HS))
                G.tick(nc.gpsimd.memset(low1[:, :], 1.0))
                G.tick(nc.gpsimd.memset(low2[:, :], 1.0))
                G.link(nc.gpsimd.memset(pick1[:, :, :], 0.0))
                nc.gpsimd.affine_select(out=low1[:, :], in_=low1[:, :], compare_op=ALU.is_ge, fill=0.0, base=-HC,
                                        pattern=[[0, 1]], channel_multiplier=1)
                nc.gpsimd.affine_select(out=low2[:, :], in_=low2[:, :], compare_op=ALU.is_ge, fill=0.0, base=-1,
                                        pattern=[[0, 1]], channel_multiplier=1)
                for h in range(2):
                    ins = nc.gpsimd.affine_select(out=pick1[:, :, :], in_=pick1[:, :, :], compare_op=ALU.not_equal, fill=SC,
                                                  base=-h * HC, pattern=[[-1, HC], [0, P]], channel_multiplier=1)
                    if h == 0:
                        G.link(ins)
                ins.then_inc(s_const, 1)
                pool.wait_ge(core.s_zero, 16 * HALVES)
                pool.wait_ge(s_l, NG)
                pool.wait_ge(s_slot, 1)
                for h in range(HALVES):
                    for t in range(h * HNT, (h + 1) * HNT):
                        for k in range(2):
                            nc.gpsimd.indirect_dma_start(
                                x_rows[h], bass.IndirectOffsetOnAxis(slot[:, k, t:t + 1], 0),
                                xh[:, t, :, :].rearrange("p h f -> p (h f)"), None).then_inc(s_sc[h], 16)
                for h in range(HALVES):
                    for b in range(2):
                        pool.wait_ge(s_st[b], 16 + (h + 1) * (SNG // 2 * 16))
                    for t in range(h * HNT, (h + 1) * HNT):
                        for k in range(2):
                            nc.gpsimd.indirect_dma_start(
                                got[:, t, k, :], None, y_rows[h],
                                bass.IndirectOffsetOnAxis(slot[:, k, t:t + 1], 0)).then_inc(s_got[t // TPG], 16)

            @block.scalar
            def _(act):
                act.sem_inc(s_ge, RING)
                act.sem_inc(s_yo, 2)
                split_scalar(core, s, norm, spare)
                act.wait_ge(s_d, 1)
                nc.scalar.activation(ex[:, :], ex[:, :], ACT.Exp).then_inc(s_ex, 1)

                def gelu(u, r):
                    act.wait_ge(s_h1, u + 1)
                    act.wait_ge(s_hl, u + 1)
                    nc.scalar.activation(h32[:, r, :], hbank[r][:, :], ACT.Gelu, scale=1.0 / (SC * SC)).then_inc(s_ge, 1)

                def copy_y(g, b):
                    act.wait_ge(s_y, g * TPG + (DU + RING + TPG))
                    act.wait_ge(s_st[b], (g + (2 - b)) * 8)
                    nc.scalar.copy(yo[:, b, :, :], ybank[b][:, :, :]).then_inc(s_yo, 1)

                if S:
                    with act.Fori(0, DU // RING) as g:
                        for r in range(RING):
                            gelu(g * RING + r, r)
                for r in range(LA):
                    gelu(DU + r, r)
                with act.Fori(0, SG // 2 - 1) as g2:
                    for b in range(2):
                        for j in range(TPG):
                            gelu(g2 * (2 * TPG) + (DU + b * TPG + j + LA), (j + LA) % RING)
                        copy_y(g2 * 2 + b, b)
                for j in range(LA, 2 * TPG):
                    gelu(DU + (SG - 2) * TPG + j, j % RING)
                    if j == TPG + LA - 1:
                        copy_y(SG - 2, 0)
                copy_y(SG - 1, 1)

            @block.vector
            def _(dve):
                dve.sem_inc(s_ws, 2)
                dve.sem_inc(s_hl, RING)
                dve.sem_inc(s_add, 2)
                dve.sem_inc(s_xgc, 1)
                dve.wait_ge(s_wg, 16 if bg_d is None else 32)
                V.link(nc.vector.tensor_scalar(wgs[:, 0, :], wg[:, :], SC, None, ALU.mult))
                nc.vector.scalar_tensor_tensor(out=wgs[:, 1, :], in0=wg[:, :], scalar=SC, in1=wgs[:, 0, :],
                                               op0=ALU.mult, op1=ALU.subtract).then_inc(s_wgs, 1)

                def split_weights(e):
                    dve.wait_ge(s_w[e % 2], (e // 2 + 1) * 32)
                    for m, w in enumerate((w1, w2)):
                        v = [w[:, h, e].rearrange("p c n -> p (c n)") for h in range(2)]
                        V.link(nc.vector.tensor_scalar(v[0], wf[:, e % 2, m, :], SC, None, ALU.mult))
                        ins = nc.vector.scalar_tensor_tensor(out=v[1], in0=wf[:, e % 2, m, :], scalar=SC, in1=v[0],
                                                             op0=ALU.mult, op1=ALU.subtract)
                        if m == 0:
                            V.tick(ins)
                    ins.then_inc(s_ws, 1)

                split_vector(core, s)
                dve.wait_ge(s_b, 64)
                dve.wait_ge(s_const, 2)
                for f, h, o, low in ((b1f, b1h, b1s, low1), (b2f, b2h, b2s, low2)):
                    f, h, o = (v[:, :, :].rearrange("p e n -> p (e n)") for v in (f, h, o))
                    V.link(nc.vector.tensor_scalar(f, f, SC, None, ALU.mult))
                    V.link(nc.vector.tensor_copy(h, f))
                    V.link(nc.vector.tensor_scalar(h, h, low[:, 0:1], None, ALU.mult))
                    V.link(nc.vector.tensor_tensor(o, f, h, ALU.subtract))
                dve.sem_inc(s_bs, 1)
                for e in range(EARLY):
                    split_weights(e)
                dve.wait_ge(s_lg, NG)
                lview = lbank[:, 0, :].rearrange("p (t r) -> p t r", r=R)
                V.link(nc.vector.tensor_scalar(lg[:, :, :], lview, 1.0 / (SC * SC), None, ALU.mult))
                if bg_d is not None:
                    V.link(nc.vector.tensor_tensor(lg[:, :, :], lg[:, :, :], bg[:, None, :].to_broadcast([P, NT, R]), ALU.add))
                obc = order[:, None, :].to_broadcast([P, NT, R])
                for k in range(2):
                    V.link(nc.vector.tensor_reduce(best[:, k, :], lg[:, :, :], AX, ALU.max))
                    V.link(nc.vector.tensor_tensor(t1[:, :, :], lg[:, :, :], over_columns(best[:, k, :], R), ALU.is_equal))
                    V.link(nc.vector.tensor_tensor(t1[:, :, :], t1[:, :, :], obc, ALU.mult))
                    V.link(nc.vector.tensor_reduce(pick[:, :], t1[:, :, :], AX, ALU.max))
                    V.link(nc.vector.tensor_tensor(oh[:, k], obc, over_columns(pick[:, :], R), ALU.is_equal))
                    if k == 0:
                        V.link(nc.vector.scalar_tensor_tensor(out=lg[:, :, :], in0=oh[:, 0], scalar=-BIG, in1=lg[:, :, :],
                                                              op0=ALU.mult, op1=ALU.add))
                nc.vector.tensor_tensor(both[:, :, :], oh[:, 0], oh[:, 1], ALU.add).then_inc(s_both, 1)
                nc.vector.tensor_tensor(ex[:, :], best[:, 1, :], best[:, 0, :], ALU.subtract).then_inc(s_d, 1)
                dve.wait_ge(s_rank, 1)
                rank = lbank[:, 0, :].rearrange("p (h t r) -> p h t r", h=HALVES, r=R)
                V.link(nc.vector.tensor_copy(cnt[:, :, :, :], lbank[:, 1, :].rearrange("p (h t r) -> p h t r", h=HALVES, r=R)))
                a, step, k = cnt, 1, 0
                while step < HNT:
                    V.tick(nc.vector.tensor_copy(run[k][:, :, 0:step, :], a[:, :, 0:step, :]))
                    V.link(nc.vector.tensor_tensor(run[k][:, :, step:, :], a[:, :, step:, :], a[:, :, 0:HNT - step, :], ALU.add))
                    a, step, k = run[k], 2 * step, 1 - k
                V.tick(nc.vector.tensor_tensor(cnt[:, :, :, :], a[:, :, :, :], cnt[:, :, :, :], ALU.subtract))
                V.link(nc.vector.tensor_scalar(tot[:, :, :], a[:, :, HNT - 1, :], 1.0 / P, None, ALU.mult))
                V.link(nc.vector.tensor_tensor(more[:, :, :, :], tot[:, :, :].unsqueeze(3).to_broadcast([P, HALVES, R, HNT]),
                                               count[:, None, None, 0:HNT].to_broadcast([P, HALVES, R, HNT]), ALU.is_gt))
                V.link(nc.vector.tensor_reduce(nt[:, :, :], more[:, :, :, :], AX, ALU.add))
                V.link(nc.vector.tensor_tensor(prod[:, :, :, :], nt[:, :, None, :].to_broadcast([P, HALVES, R, R]),
                                               before[:, None, :, :].to_broadcast([P, HALVES, R, R]), ALU.mult))
                V.link(nc.vector.tensor_reduce(off[:, :, :], prod[:, :, :, :], AX, ALU.add))
                V.tick(nc.vector.tensor_scalar(base[:, :, :], off[:, :, :], float(P), None, ALU.mult))
                V.link(nc.vector.tensor_tensor(cnt[:, :, :, :], cnt[:, :, :, :], rank, ALU.add))
                V.link(nc.vector.tensor_tensor(cnt[:, :, :, :], cnt[:, :, :, :],
                                               base[:, :, None, :].to_broadcast([P, HALVES, HNT, R]), ALU.add))
                for k in range(2):
                    V.link(nc.vector.tensor_tensor(t1[:, :, :], oh[:, k], cnt[:, :, :, :].rearrange("p h t r -> p (h t) r"), ALU.mult))
                    V.link(nc.vector.tensor_reduce(slotf[:, k, :], t1[:, :, :], AX, ALU.add))
                nc.vector.tensor_copy(slot[:, :, :], slotf[:, :, :]).then_inc(s_slot, 1)
                V.link(nc.vector.tensor_tensor(off[:, :, :], off[:, :, :], nt[:, :, :], ALU.add))
                V.link(nc.vector.tensor_tensor(past[:, :, :, :], off[:, :, None, :].to_broadcast([P, HALVES, SNT, R]),
                                               count[:, None, :, None].to_broadcast([P, HALVES, SNT, R]), ALU.is_le))
                V.link(nc.vector.tensor_reduce(owner[:, :, :], past[:, :, :, :], AX, ALU.add))
                V.link(nc.vector.tensor_scalar(owner[:, :, :], owner[:, :, :], float(R - 1), float(S), ALU.min, ALU.add))
                nc.vector.tensor_copy(own[:, :], owner[:, :, :].rearrange("p h s -> p (h s)")).then_inc(s_own, 1)
                dve.wait_ge(s_ex, 1)
                V.link(nc.vector.tensor_scalar(wt[:, 0, :], ex[:, :], 1.0, None, ALU.add))
                V.link(nc.vector.reciprocal(wt[:, 0, :], wt[:, 0, :]))
                V.link(nc.vector.tensor_scalar(wt[:, 0, :], wt[:, 0, :], 1.0 / (SC * HS), None, ALU.mult))
                V.link(nc.vector.tensor_tensor(wt[:, 1, :], wt[:, 0, :], ex[:, :], ALU.mult))
                for e in range(EARLY, E):
                    split_weights(e)

                def parts(u, r):
                    dve.wait_ge(s_ge, u + (RING + 1))
                    dve.wait_ge(s_y, u + 1)
                    nc.vector.tensor_scalar(hh[:, r, :], h32[:, r, :], HS, None, ALU.mult).then_inc(s_hh, 1)
                    dve.wait_ge(s_hh, u + 1)
                    nc.vector.scalar_tensor_tensor(out=hl[:, r, :], in0=h32[:, r, :], scalar=HS, in1=hh[:, r, :],
                                                   op0=ALU.mult, op1=ALU.subtract).then_inc(s_hl, 1)

                def copy_turned(g, b):
                    dve.wait_ge(s_xgt, g + 3)
                    nc.vector.tensor_copy(xgt[:, b, :, :], turn[:, :, :]).then_inc(s_xgc, 1)

                def add_dense(g, b):
                    dve.wait_ge(s_y, g * TPG + (RING + TPG))
                    nc.vector.scalar_tensor_tensor(out=tiles(x, g), in0=ybank[b][:, :, :], scalar=1.0 / (SC * HS),
                                                   in1=tiles(x, g), op0=ALU.mult, op1=ALU.add).then_inc(s_add, 1)

                if S:
                    for r in range(LA):
                        parts(r, r)
                    with dve.Fori(0, DG // 2 - 1) as g2:
                        for b in range(2):
                            for j in range(TPG):
                                parts(g2 * (2 * TPG) + (b * TPG + j + LA), (j + LA) % RING)
                            add_dense(g2 * 2 + b, b)
                    for j in range(LA, 2 * TPG):
                        parts(DU - 2 * TPG + j, j % RING)
                        if j == TPG + LA - 1:
                            add_dense(DG - 2, 0)
                    add_dense(DG - 1, 1)
                copy_turned(0, 0)
                parts(DU, 0)
                with dve.Fori(0, SG // 2 - 1) as g2:
                    for b in range(2):
                        u = g2 * (2 * TPG) + (DU + b * TPG)
                        parts(u + 1, 1)
                        dve.wait_ge(s_h1, u + 1)
                        copy_turned(g2 * 2 + (b + 1), 1 - b)
                        for j in range(2, TPG + 1):
                            parts(u + j, j % RING)
                u = DU + (SG - 2) * TPG
                parts(u + 1, 1)
                dve.wait_ge(s_h1, u + 1)
                copy_turned(SG - 1, 1)
                for j in range(2, 2 * TPG):
                    parts(u + j, j % RING)
                dve.wait_ge(s_add, 2 + DG)
                for g in range(NG):
                    dve.wait_ge(s_got[g], 2 * TPG * 16)
                    for k in range(2):
                        for t in range(g * TPG, (g + 1) * TPG):
                            ins = nc.vector.scalar_tensor_tensor(out=x[:, t, :], in0=got[:, t, k, :], scalar=wt[:, k, t:t + 1],
                                                                 in1=x[:, t, :], op0=ALU.mult, op1=ALU.add)
                        if k == 0 or out_d is None:
                            V.link(ins)
                        else:
                            ins.then_inc(s_res, 1)
                    if out_d is None:
                        core.stats_of_group(g)
                V.wait()

            @block.tensor
            def _(pe):
                pe.sem_inc(s_y, RING)
                pe.sem_inc(s_xgt, 2)
                pe.wait_ge(s_wgs, 1)

                def logits(g):
                    for t in range(g * TPG, (g + 1) * TPG):
                        for n, (h, w) in enumerate(((0, 0), (0, 1), (1, 0))):
                            mm = nc.tensor.matmul(lbank[:, 0, t * R:(t + 1) * R], xt[:, h, t * P:(t + 1) * P], wgs[:, w, :],
                                                  start=(n == 0), stop=(n == 2))
                    mm.then_inc(s_lg, 1)

                split_tensor(core, s, spare, logits)
                pe.wait_ge(s_both, 1)
                pe.wait_ge(s_const, 1)
                for i, m in enumerate((below, ones)):
                    mm = nc.tensor.matmul(lbank[:, i, :], m[:, :], both[:, :, :].rearrange("p t r -> p (t r)"), start=True, stop=True)
                mm.then_inc(s_rank, 1)

                def first(u, r, rows, e):
                    pe.wait_ge(s_ge, u + 1)
                    nc.tensor.matmul(hbank[r][:, :], b1s[:, bass.ds(e, 1), :].squeeze(1), pick1[:, :, :].rearrange("p c n -> p (c n)"),
                                     start=True, stop=False, skip_group_check=True)
                    for k in range(HC):
                        for n, (h, w) in enumerate(((0, 0), (1, 0), (0, 1))):
                            mm = nc.tensor.matmul(hbank[r][:, k * P:(k + 1) * P], w1[:, w, bass.ds(e, 1), k, :].squeeze(1), rows[h],
                                                  start=False, stop=(n == 2 and k == HC - 1), skip_group_check=True)
                    mm.then_inc(s_h1, 1)

                def second(u, j, e, b):
                    pe.wait_ge(s_hl, u + (RING + 1))
                    nc.tensor.matmul(ybank[b][:, j, :], pick2[:, :], b2s[:, bass.ds(e, 1), :].squeeze(1),
                                     start=(j == 0), stop=False, skip_group_check=True)
                    for k in range(HC):
                        for i, (h, w) in enumerate(((hh, 0), (hh, 1), (hl, 0))):
                            mm = nc.tensor.matmul(ybank[b][:, j, :], h[:, j, k * P:(k + 1) * P], w2[:, w, bass.ds(e, 1), k, :].squeeze(1),
                                                  start=False, stop=(j == TPG - 1 and k == HC - 1 and i == 2), skip_group_check=True)
                    mm.then_inc(s_y, 1)

                def transpose_rows(g, b):
                    pe.wait_ge(s_xg[b], (g + (2 - b)) * 8)
                    pe.wait_ge(s_xgc, g + 1)
                    for h in range(2):
                        for j in range(TPG):
                            mm = nc.tensor.transpose(turn[:, h, j * P:(j + 1) * P], xg[:, b, j, h * P:(h + 1) * P], core.id16[:, :])
                    mm.then_inc(s_xgt, 1)

                pe.wait_ge(s_bs, 1)
                if S:
                    pe.wait_ge(s_ws, 2 + S)

                    def dense_rows(t):
                        return [xt[:, h, bass.ds(t * P, P)] for h in range(2)]

                    def dense_pair(g2, last):
                        for b in range(2):
                            for j in range(TPG):
                                u = g2 * (2 * TPG) + (b * TPG + j)
                                if b * TPG + j + LA < 2 * TPG or not last:
                                    first(u + LA, (j + LA) % RING, dense_rows(u + LA), 0)
                                if j == 0:
                                    pe.wait_ge(s_add, g2 * 2 + (b + 1))
                                second(u, j, 0, b)

                    for u in range(LA):
                        first(u, u, dense_rows(u), 0)
                    with pe.Fori(0, DG // 2 - 1) as g2:
                        dense_pair(g2, False)
                    dense_pair(DG // 2 - 1, True)
                    pe.wait_ge(s_add, 2 + DG)

                def slot_rows(b, j):
                    return [xgt[:, b, h, j * P:(j + 1) * P] for h in range(2)]

                def load_owners(u, n):
                    return nc.values_load_multi_w_load_instructions(
                        own[0:1, bass.ds(u, n)], engines=(mybir.EngineType.PE,), min_val=S, max_val=E - 1,
                        skip_runtime_bounds_check_because="the number of an expert")[1]

                def slot_pair(g2, e, last):
                    for b in range(2):
                        for j in range(TPG):
                            i = b * TPG + j
                            u = g2 * (2 * TPG) + (DU + i)
                            if j == 0 and not (last and b):
                                transpose_rows(g2 * 2 + (b + 1), 1 - b)
                            if i + LA < 2 * TPG or not last:
                                if j + LA == TPG:
                                    pe.wait_ge(s_xgc, g2 * 2 + (b + 3))
                                first(u + LA, (j + LA) % RING, slot_rows((b + (j + LA) // TPG) % 2, (j + LA) % TPG), e[i + LA])
                            if j == 0:
                                pe.wait_ge(s_yo, g2 * 2 + (b + 1))
                            second(u, j, e[i], b)

                transpose_rows(0, 0)
                pe.wait_ge(s_ws, 2 + E)
                pe.wait_ge(s_own, 1)
                pe.wait_ge(s_xgc, 2)
                e = load_owners(0, LA)
                for u in range(LA):
                    first(DU + u, u, slot_rows(0, u), e[u])
                with pe.Fori(0, SG // 2 - 1) as g2:
                    slot_pair(g2, load_owners(g2 * (2 * TPG), 2 * TPG + LA), False)
                slot_pair(SG // 2 - 1, load_owners((SG - 2) * TPG, 2 * TPG), True)


def aggregate(core, io):
    nc, x, V, sem = core.nc, core.x, core.V, core.sem
    W = P + 1
    norm = core.norms + 1
    RING = 4
    AHEAD = RING - 1
    with ExitStack() as c:
        def sb(name, shape, dt=F32):
            return core.sb(c, name, shape, dt)

        s = split_tensors(core, c, "g")
        xs, xh, xt, turn, (s_n, s_h, s_l, s_t, s_c) = s
        kf = sb("kernf", [P, P])
        ks = sb("kerns", [P, 2, P], F16)
        ys = sb("ys", [P, NT, P])
        ry = sb("ry", [P, NT, 2, W], F16)
        bias = sb("bias", [P, P])
        beta = sb("beta", [P, NT])
        adj = sb("adjg", [P, NQ, CJ, GW])
        ah = sb("ah", [P, RING, CJ, GW], F16)
        al = sb("al", [P, RING, CJ, GW], F16)
        acc = sb("accg", [P, TPG, 2 * W])
        num = sb("numg", [P, TPG, W])
        sc = sb("scg", [P, TPG])
        bank = [core.ps(c, f"agg{b}", [P, 512], F32) for b in range(TPG + 1)]
        spare = bank[TPG][:, :].bitcast(F16)[:, 0:GW]
        s_par = sem("kernel_loaded")
        s_ks = sem("kernel_split")
        s_one = sem("ones_ready")
        s_xb = sem("bias_added")
        s_y = sem("y_summed")
        s_yc = sem("y_copied")
        s_yh, s_yl = sem("y_hi"), sem("y_lo")
        s_adj = [sem(f"adjg_loaded{q}") for q in range(NQ)]
        s_ah, s_al = sem("adj_hi"), sem("adj_lo")
        s_pe = sem("adj_parts_used")
        s_acc = sem("sums_copied")
        s_done = sem("group_done")
        with nc.Block() as block:

            @block.sync
            def _(sp):
                sp.dma_start(kf[:, :], io["L1_gnn_kernel"]).then_inc(s_par, 16)
                sp.dma_start(bias[:, :], io["L1_gnn_bias"].partition_broadcast(P)).then_inc(s_par, 16)
                sp.dma_start(beta[:, :], io["L1_gnn_beta"]).then_inc(s_par, 16)
                with sp.Fori(0, NG) as g:
                    for q in range(NQ):
                        n = g * NQ + q
                        sp.wait_ge(s_al, n + 1)
                        sp.dma_start(adj[:, q, :, :], io["adj"][bass.ds(n, 1)].squeeze(0)).then_inc(s_adj[q], 16)

            @block.gpsimd
            def _(pool):
                nc.gpsimd.memset(ry[:, :, 0, P:W], 1.0)
                nc.gpsimd.memset(ry[:, :, 1, P:W], 0.0).then_inc(s_one, 1)
                pool.wait_ge(s_par, 48)
                pool.wait_ge(s_n, NG)
                for g in range(NG):
                    nc.gpsimd.tensor_tensor(tiles(x, g), tiles(x, g), bias[:, None, :].to_broadcast([P, TPG, P]),
                                            ALU.add).then_inc(s_xb, 1)

            @block.scalar
            def _(act):

                def copy_y(g):
                    act.wait_ge(s_y, g + 1)
                    yb = bank[g % 4][:, :].rearrange("p (t f) -> p t f", f=P)
                    nc.scalar.activation(tiles(ry, g)[:, :, 0, 0:P], yb, ACT.Copy, scale=1.0 / SC).then_inc(s_yh, 1)
                    nc.scalar.activation(tiles(ys, g), yb, ACT.Copy, scale=1.0 / SC).then_inc(s_yc, 1)

                act.sem_inc(s_acc, 1)
                split_scalar(core, s, norm, spare, copy_y)

                def parts(g, q0, q1):
                    for q in range(q0, q1):
                        act.wait_ge(s_adj[q], g * 16 + 16)
                        act.wait_ge(s_pe, g * NQ + (q + 1))
                        nc.scalar.activation(ah[:, q % RING], adj[:, q], ACT.Copy).then_inc(s_ah, 1)

                def copy_out(g):
                    act.wait_ge(s_pe, g * NQ + (RING + NQ))
                    act.wait_ge(s_done, g + 1)
                    for t in range(TPG):
                        ins = nc.scalar.activation(acc[:, t, :], bank[t][:, 0:2 * W], ACT.Copy)
                    ins.then_inc(s_acc, 1)

                parts(0, 0, AHEAD)
                with act.Fori(0, NG - 1) as g:
                    parts(g, AHEAD, NQ)
                    parts(g + 1, 0, AHEAD)
                    copy_out(g)
                parts(NG - 1, AHEAD, NQ)
                copy_out(NG - 1)

            @block.vector
            def _(dve):
                dve.sem_inc(s_al, NQ)
                dve.sem_inc(s_done, 1)
                dve.wait_ge(s_par, 48)
                V.link(nc.vector.tensor_scalar(ks[:, 0, :], kf[:, :], SC, None, ALU.mult))
                nc.vector.scalar_tensor_tensor(out=ks[:, 1, :], in0=kf[:, :], scalar=SC, in1=ks[:, 0, :],
                                               op0=ALU.mult, op1=ALU.subtract).then_inc(s_ks, 1)

                def lo_y(g):
                    dve.wait_ge(s_yh, g + 1)
                    dve.wait_ge(s_yc, g + 1)
                    r = tiles(ry, g)
                    nc.vector.tensor_tensor(r[:, :, 1, 0:P], tiles(ys, g), r[:, :, 0, 0:P], ALU.subtract).then_inc(s_yl, 1)

                split_vector(core, s, lo_y)

                def parts(g, q0, q1):
                    for q in range(q0, q1):
                        dve.wait_ge(s_ah, g * NQ + (q + 1))
                        nc.vector.tensor_tensor(al[:, q % RING], adj[:, q], ah[:, q % RING], ALU.subtract).then_inc(s_al, 1)

                def post(g):
                    dve.wait_ge(s_acc, g + 2)
                    V.link(nc.vector.tensor_tensor(num[:, :, :], acc[:, :, 0:W], acc[:, :, W:2 * W], ALU.add))
                    V.link(nc.vector.tensor_tensor(sc[:, :], num[:, :, P], tiles(beta, g), ALU.add))
                    V.link(nc.vector.reciprocal(sc[:, :], sc[:, :]))
                    V.tick(nc.vector.tensor_scalar(sc[:, :], sc[:, :], 1.0 / SC, None, ALU.mult))
                    for k in range(TPG):
                        t = g * TPG + k
                        ins = nc.vector.scalar_tensor_tensor(out=num[:, k, 0:P], in0=ys[:, t, :], scalar=beta[:, bass.ds(t, 1)],
                                                             in1=num[:, k, 0:P], op0=ALU.mult, op1=ALU.add)
                    V.link(ins)
                    for k in range(TPG):
                        t = g * TPG + k
                        ins = nc.vector.scalar_tensor_tensor(out=x[:, t, :], in0=num[:, k, 0:P], scalar=sc[:, k:k + 1],
                                                             in1=x[:, t, :], op0=ALU.mult, op1=ALU.add)
                    V.link(ins)
                    core.stats_of_group(g)

                parts(0, 0, AHEAD)
                dve.wait_ge(s_xb, NG)
                with dve.Fori(0, NG - 1) as g:
                    V.loop(g, 7)
                    parts(g, AHEAD, NQ)
                    parts(g + 1, 0, AHEAD)
                    post(g)
                    dve.sem_inc(s_done, 1)
                V.end(NG - 1)
                parts(NG - 1, AHEAD, NQ)
                post(NG - 1)
                V.wait()

            @block.tensor
            def _(pe):
                pe.sem_inc(s_pe, RING)
                pe.wait_ge(s_ks, 1)

                def sums_y(g):
                    if g >= 4:
                        pe.wait_ge(s_yc, g - 3)
                    for k in range(TPG):
                        for i, (h, w) in enumerate(((0, 0), (0, 1), (1, 0))):
                            mm = nc.tensor.matmul(bank[g % 4][:, k * P:(k + 1) * P], xt[:, h, g * GW + k * P:g * GW + (k + 1) * P],
                                                  ks[:, w, :], start=(i == 0), stop=(i == 2))
                    mm.then_inc(s_y, 1)

                split_tensor(core, s, spare, sums_y)
                pe.wait_ge(s_yl, NG)
                pe.wait_ge(s_one, 1)
                with pe.Fori(0, NG) as g:
                    pe.wait_ge(s_acc, g + 1)
                    for jt in range(NT):
                        q = jt // CJ
                        if jt % CJ == 0:
                            pe.wait_ge(s_al, g * NQ + (q + 1 + NQ))
                        for t in range(TPG):
                            for part in range(2):
                                mm = nc.tensor.matmul(
                                    bank[t][:, 0:W if part else 2 * W],
                                    (ah, al)[part][:, q % RING, jt % CJ, t * P:(t + 1) * P],
                                    ry[:, jt, 0, :] if part else ry[:, jt, :, :].rearrange("p h w -> p (h w)"),
                                    start=(jt == 0 and part == 0), stop=(jt == NT - 1 and part == 1), skip_group_check=True)
                        if jt % CJ == CJ - 1:
                            mm.then_inc(s_pe, 1)


NAMES = ["x", "adj", "L0_gnn_h0", "L0_gnn_a", "L0_gnn_temp", "L0_ffn_Wg", "L0_ffn_bg", "L0_ffn_W1", "L0_ffn_b1",
         "L0_ffn_W2", "L0_ffn_b2", "L1_gnn_kernel", "L1_gnn_bias", "L1_gnn_beta", "L1_ffn_Wr", "L1_ffn_W1", "L1_ffn_b1",
         "L1_ffn_W2", "L1_ffn_b2"]


def build(nc, io, out):
    f1_row = nc.dram_tensor("f1_row", [NG, GW], F32).ap()
    x_rows = [nc.dram_tensor(f"x_rows{h}", [SLOTS, 2 * P], F16).ap() for h in range(HALVES)]
    y_rows = [nc.dram_tensor(f"y_rows{h}", [SLOTS, P], F32).ap() for h in range(HALVES)]
    with ExitStack() as ctx:
        core = Core(nc, ctx)
        attention(core, io, f1_row, x_rows)
        experts(core, "a", 0, io["L0_ffn_Wg"], io["L0_ffn_bg"], io["L0_ffn_W1"], io["L0_ffn_b1"],
                io["L0_ffn_W2"], io["L0_ffn_b2"], x_rows, y_rows, None)
        aggregate(core, io)
        experts(core, "b", 1, io["L1_ffn_Wr"], None, io["L1_ffn_W1"], io["L1_ffn_b1"],
                io["L1_ffn_W2"], io["L1_ffn_b2"], x_rows, y_rows, out)


def kernel(**inputs):
    import numpy as np
    import concourse.bacc as bacc
    from concourse import mybir as mb
    from concourse.bass_utils import run_bass_kernel_spmd

    v = {n: np.asarray(a) for n, a in inputs.items()}

    def by_tile(a):
        return a.reshape(NT, P, P).transpose(1, 0, 2)

    def hidden_bias(a):
        return a.reshape(-1, HC, P).transpose(1, 0, 2)

    def second_weight(a):
        return a.reshape(-1, HC, P, P).transpose(0, 2, 1, 3).reshape(-1, P, HC * P)

    laid = {
        "x": by_tile(v["x"]),
        "adj": v["adj"].reshape(NG, GW, NQ, CJ, P).transpose(0, 2, 4, 3, 1).reshape(NC, P, CJ, GW),
        "L0_gnn_h0": by_tile(v["L0_gnn_h0"]),
        "L0_gnn_a": v["L0_gnn_a"].reshape(2, P),
        "L0_gnn_temp": v["L0_gnn_temp"],
        "L0_ffn_Wg": v["L0_ffn_Wg"], "L0_ffn_bg": v["L0_ffn_bg"],
        "L0_ffn_W1": v["L0_ffn_W1"], "L0_ffn_b1": hidden_bias(v["L0_ffn_b1"]),
        "L0_ffn_W2": second_weight(v["L0_ffn_W2"]), "L0_ffn_b2": v["L0_ffn_b2"],
        "L1_gnn_kernel": v["L1_gnn_kernel"], "L1_gnn_bias": v["L1_gnn_bias"],
        "L1_gnn_beta": v["L1_gnn_beta"].reshape(NT, P).T,
        "L1_ffn_Wr": v["L1_ffn_Wr"],
        "L1_ffn_W1": np.concatenate([v["L1_ffn_W1s"][None], v["L1_ffn_W1p"]]),
        "L1_ffn_b1": hidden_bias(np.concatenate([v["L1_ffn_b1s"][None], v["L1_ffn_b1p"]])),
        "L1_ffn_W2": second_weight(np.concatenate([v["L1_ffn_W2s"][None], v["L1_ffn_W2p"]])),
        "L1_ffn_b2": np.concatenate([v["L1_ffn_b2s"][None], v["L1_ffn_b2p"]]),
    }
    nc = bacc.Bacc("TRN2", target_bir_lowering=False, num_devices=1)
    arrays, io = {}, {}
    for name in NAMES:
        a = np.ascontiguousarray(laid[name])
        arrays[f"in_{name}"] = a
        io[name] = nc.dram_tensor(f"in_{name}", a.shape, mb.dt.from_np(a.dtype), kind="ExternalInput").ap()
    out = nc.dram_tensor("out_0", (P, NT, P), mb.dt.float32, kind="ExternalOutput").ap()
    build(nc, io, out)
    r = run_bass_kernel_spmd(nc, [arrays], core_ids=[0])
    return np.ascontiguousarray(r.results[0]["out_0"].transpose(1, 0, 2)).reshape(N, P)
```

```python
from contextlib import ExitStack

import concourse.bass as bass
from concourse import mybir

F32 = mybir.dt.float32
F16 = mybir.dt.float16
BF16 = mybir.dt.bfloat16
ALU = mybir.AluOpType
ACT = mybir.ActivationFunctionType
AX = mybir.AxisListType.X
RMAX = bass.bass_isa.ReduceOp.max

P = 128
N = 4096
NT = N // P
TPG = 4
GW = TPG * P
NG = NT // TPG
HC = 4
CJ = 4
NQ = NT // CJ
NC = NG * NQ
SC = 1024.0
HS = 256.0
EPS = 1e-5
THRESH = 1e-6
ALPHA = 0.2
BIG = 1e30
R = 8
HALVES = 2
HNT = NT // HALVES
UT = 2
UW = UT * P
SNU = -(-((2 * HNT * P + R * (UW - 1)) // UW) // (2 * TPG // UT)) * (2 * TPG // UT)
SNG = SNU * UT // TPG
SLOTS = SNU * UW


class Ticks:

    def __init__(self, eng, sem):
        self.eng, self.sem, self.base, self.it, self.per, self.k = eng, sem, 0, None, 0, 0

    def loop(self, it, per):
        self.base, self.it, self.per, self.k = self.base + self.k, it, per, 0

    def end(self, trips):
        assert self.k == self.per, (self.k, self.per)
        self.base, self.it, self.k = self.base + trips * self.per, None, 0

    def tick(self, ins):
        ins.then_inc(self.sem, 1)
        self.k += 1

    def wait(self):
        v = self.base + self.k
        self.eng.wait_ge(self.sem, v if self.it is None else self.it * self.per + v)

    def link(self, ins):
        self.tick(ins)
        self.wait()


class Core:

    def __init__(self, nc, ctx):
        self.nc, self.ctx = nc, ctx
        self.x = self.sb(ctx, "x", [P, NT, P], F32)
        self.id16 = self.sb(ctx, "id16", [P, P], F16)
        self.id32 = self.sb(ctx, "id32", [P, P], F32)
        self.stats = self.sb(ctx, "stats", [P, NT, 6], F32)
        self.mean = self.sb(ctx, "mean", [P, NT], F32)
        self.rstd = self.sb(ctx, "rstd", [P, NT], F32)
        self.rtmp = self.sb(ctx, "rtmp", [P, NT], F32)
        self.veps = self.sb(ctx, "veps", [P, NT], F32)
        self.V = Ticks(nc.vector, self.sem("vector_chain"))
        self.A = Ticks(nc.scalar, self.sem("scalar_chain"))
        self.G = Ticks(nc.gpsimd, self.sem("gpsimd_chain"))
        self.s_zero = self.sem("slots_cleared")
        self.s_rec = self.sem("variance_reciprocal")
        self.s_root = self.sem("rstd_root")
        self.norms = 0

    def sb(self, ctx, name, shape, dt):
        return ctx.enter_context(self.nc.sbuf_tensor(name, shape, dt))

    def ps(self, ctx, name, shape, dt):
        return ctx.enter_context(self.nc.psum_tensor(name, shape, dt))

    def sem(self, name):
        return self.ctx.enter_context(self.nc.semaphore(name))

    def stats_of_group(self, g):
        nc = self.nc
        for k in range(TPG):
            ins = nc.vector.bn_stats(self.stats[:, g * TPG + k, :], self.x[:, g * TPG + k, :])
        self.V.tick(ins)

    def rstd_vector(self, scale):
        nc, V = self.nc, self.V
        self.norms += 1
        me, se, mo, so = (self.stats[:, :, i] for i in (1, 2, 4, 5))
        V.tick(nc.vector.tensor_tensor(self.mean[:, :], me, mo, ALU.add))
        V.link(nc.vector.tensor_tensor(self.rtmp[:, :], me, mo, ALU.subtract))
        V.tick(nc.vector.scalar_tensor_tensor(out=self.rtmp[:, :], in0=self.rtmp[:, :], scalar=0.25, in1=self.rtmp[:, :],
                                              op0=ALU.mult, op1=ALU.mult))
        V.link(nc.vector.tensor_tensor(self.veps[:, :], se, so, ALU.add))
        V.tick(nc.vector.tensor_scalar(self.mean[:, :], self.mean[:, :], 0.5, None, ALU.mult))
        V.link(nc.vector.tensor_scalar(self.veps[:, :], self.veps[:, :], 1.0 / P, EPS, ALU.mult, ALU.add))
        V.link(nc.vector.tensor_tensor(self.veps[:, :], self.veps[:, :], self.rtmp[:, :], ALU.add))
        nc.vector.reciprocal(self.rtmp[:, :], self.veps[:, :]).then_inc(self.s_rec, 1)
        nc.vector.wait_ge(self.s_root, self.norms)
        V.link(nc.vector.tensor_tensor(self.rtmp[:, :], self.rstd[:, :], self.rstd[:, :], ALU.mult))
        V.link(nc.vector.tensor_tensor(self.rtmp[:, :], self.rtmp[:, :], self.veps[:, :], ALU.mult))
        V.link(nc.vector.tensor_scalar(self.rtmp[:, :], self.rtmp[:, :], -0.5 * scale, 1.5 * scale, ALU.mult, ALU.add))
        V.link(nc.vector.tensor_tensor(self.rstd[:, :], self.rstd[:, :], self.rtmp[:, :], ALU.mult))

    def rstd_scalar(self, n):
        self.nc.scalar.wait_ge(self.s_rec, n)
        self.nc.scalar.activation(self.rstd[:, :], self.rtmp[:, :], ACT.Sqrt).then_inc(self.s_root, 1)

    def normalise_group(self, out, g):
        for k in range(TPG):
            t = g * TPG + k
            ins = self.nc.vector.tensor_scalar(out[:, t, :], self.x[:, t, :], self.mean[:, bass.ds(t, 1)],
                                               self.rstd[:, bass.ds(t, 1)], ALU.subtract, ALU.mult)
        return ins


def tiles(t, g):
    return t[:, bass.ds(g * TPG, TPG)]


def over_columns(t, width):
    return t.unsqueeze(2).to_broadcast([P, t.shape[1], width])


def attention(core, io, f1_row, x_rows):
    nc, x, V, G, sem = core.nc, core.x, core.V, core.G, core.sem
    RING = 4
    AHEAD = RING - 1
    AHEAD_S = AHEAD + 1
    M_START = 2 * NQ
    STEEP = 2.0 ** 100
    W = (P + 2, P)
    with ExitStack() as c:
        def sb(name, shape, dt=F32):
            return core.sb(c, name, shape, dt)

        xn = sb("xn", [P, NT, P])
        feat = sb("feat", [P, NT, P])
        rb = [sb(f"rb{k}", [P, NT, 2, W[k]], F16) for k in range(2)]
        rd = [sb(f"rd{k}", [P, NT, 2, W[k]], F16) for k in range(2)]
        adj = sb("adj", [P, 2, CJ, GW])
        edge = sb("edge", [P, RING, CJ, GW], BF16)
        f1g = sb("f1g", [P, 2, GW])
        pos = sb("pos", [P, 2, CJ, GW], BF16)
        m1 = sb("m1", [P, RING, CJ, GW], BF16)
        m2 = sb("m2", [P, RING, CJ, GW], BF16)
        acc_a = sb("acc_a", [P, TPG, 2 * W[0]])
        acc_c = sb("acc_c", [P, TPG, 2 * W[0]])
        num = sb("num", [P, TPG, W[0]])
        vb = sb("vb", [P, TPG, P])
        vd = sb("vd", [P, TPG, P])
        vbs, vds = (vb[:, :, :], num[:, :, 0:P]), (vd[:, :, :], acc_c[:, :, 0:P])
        a2 = sb("a2", [P, 2])
        xnt = [t[:, :, 0:P] for t in (acc_a, acc_c)]
        f1t = acc_a[0:NT, 0, 0:P]
        temp = sb("temp", [P, 5])
        coe = sb("coe", [P, 5])
        om = sb("om", [P, 5])
        f1, f2, steep, z, ca, cc, wb, wd, wb2, wd2, den, rden, rows, kx, kf, kp, sq = (
            sb(f"col_{n}", [P, NT]) for n in ("f1", "f2", "steep", "z", "ca", "cc", "wb", "wd", "wb2", "wd2",
                                             "den", "rden", "rows", "kx", "kf", "kp", "sq"))
        sqd = sb("sqd", [P, TPG, 2])
        fmax = sb("fmax", [P, 1])
        fall = sb("fall", [P, 1])
        nfall = sb("nfall", [P, 2])
        cf = sb("cf", [P, 2])
        zero = sb("zero", [P, 2 * P], F16)
        banks = core.ps(c, "banks", [P, TPG, 2, 512], F32)
        bank = [banks[:, b // 2, b % 2, :] for b in range(2 * TPG)]

        s_x = [sem(f"x_loaded{i}") for i in range(NG // 2)]
        s_par, s_h0 = sem("a_and_temp_loaded"), sem("h0_loaded")
        s_cf, s_h0s, s_res = sem("h0_factor_ready"), sem("h0_scaled"), sem("h0_added")
        s_xn, s_xnT, s_xnc, s_fs = sem("xn_ready"), sem("xn_transposed"), sem("xn_transposed_copied"), sem("f_summed")
        s_id = sem("identities_ready")
        s_z0 = sem("zeros_ready")
        s_f1, s_f1T, s_f1s, s_f1d = sem("f1_ready"), sem("f1_transposed"), sem("f1_rows_copied"), sem("f1_in_dram")
        s_fmax, s_fall, s_z = sem("f2_max_of_partitions"), sem("f2_max"), sem("exponents_ready")
        s_exp = sem("exponentials_ready")
        s_w = sem("b_and_d_ready")
        s_vb, s_vd, s_hb, s_hd = sem("b_rows"), sem("d_rows"), sem("b_rows_hi"), sem("d_rows_hi")
        s_rb, s_rd = sem("b_operands_ready"), sem("d_operands_ready")
        s_adj = [sem(f"adj_loaded{b}") for b in range(2)]
        s_f1g = [sem(f"f1_group_loaded{b}") for b in range(2)]
        s_edge = sem("edges_ready")
        s_pos = sem("pos_ready")
        s_m1, s_m2p, s_m2v = sem("mask1_ready"), sem("mask2_by_gpsimd"), sem("mask2_by_vector")
        s_pe = sem("mask_slots_free")

        def vector_tiles(n):
            return n - -(-n // RING)

        s_ea, s_ec = sem("a_banks_copied"), sem("c_banks_copied")
        s_feat = sem("feat_ready")

        with nc.Block() as block:

            @block.sync
            def _(sp):
                for i in range(NG // 2):
                    part = slice(i * 2 * TPG, (i + 1) * 2 * TPG)
                    sp.dma_start(x[:, part, :], io["x"][:, part, :]).then_inc(s_x[i], 16)
                sp.dma_start(a2[:, :], io["L0_gnn_a"]).then_inc(s_par, 16)
                sp.dma_start(temp[:, :], io["L0_gnn_temp"].partition_broadcast(P)).then_inc(s_par, 16)
                sp.dma_start(feat[:, :, :], io["L0_gnn_h0"]).then_inc(s_h0, 16)
                sp.wait_ge(s_z0, 1)
                for rows in x_rows:
                    sp.dma_start(rows.rearrange("(t p) f -> p t f", p=P),
                                 zero[:, None, :].to_broadcast([P, SLOTS // P, 2 * P])).then_inc(core.s_zero, 16)
                sp.wait_ge(s_f1s, 1)
                sp.dma_start(f1_row.rearrange("g (t p) -> (g t) p", p=P), f1t).then_inc(s_f1d, 16)
                sp.wait_ge(s_f1d, 16)
                for k in range(2):
                    with sp.Fori(0, NG // 2) as g2:
                        for b in range(2):
                            g = g2 * 2 + (k * NG + b)
                            sp.wait_ge(s_m1, (g + 1) * NQ)
                            sp.dma_start(f1g[:, b, :], f1_row[bass.ds(g2 * 2 + b, 1), :].squeeze(0)
                                         .partition_broadcast(P)).then_inc(s_f1g[b], 16)
                            for q in range(NQ):
                                sp.wait_ge(s_edge, g * NQ + (q + 1))
                                sp.dma_start(adj[:, q % 2, :, :], io["adj"][bass.ds((g2 * 2 + b) * NQ + q, 1)].squeeze(0)
                                             ).then_inc(s_adj[q % 2], 16)

            @block.gpsimd
            def _(pool):
                nc.gpsimd.memset(zero[:, :], 0.0).then_inc(s_z0, 1)
                for m in (core.id16, core.id32):
                    G.link(nc.gpsimd.memset(m[:, :], 0.0))
                    nc.gpsimd.affine_select(out=m[:, :], in_=m[:, :], compare_op=ALU.not_equal, fill=1.0, base=0,
                                            pattern=[[-1, P]], channel_multiplier=1).then_inc(s_id, 1)
                pool.sem_inc(s_m2p, M_START)
                pool.wait_ge(s_xn, NG)
                pool.wait_ge(s_h0s, 1)
                for g in range(NG):
                    nc.gpsimd.tensor_tensor(tiles(x, g), tiles(x, g), tiles(feat, g), ALU.add).then_inc(s_res, 1)
                pool.wait_ge(s_fmax, 1)
                nc.gpsimd.partition_all_reduce(fall[:, :], fmax[:, :], P, RMAX).then_inc(s_fall, 1)
                pool.wait_ge(s_w, 1)
                def first_rows(g):
                    if g >= 2:
                        pool.wait_ge(s_rd, g)
                    nc.gpsimd.tensor_tensor(vds[g % 2], tiles(xn, g), over_columns(tiles(wd, g), P), ALU.mult).then_inc(s_vd, 1)

                def mask2(n4, r):
                    pool.wait_ge(s_m1, n4 * RING + (M_START + r + 1))
                    j = 1 if r else 0
                    nc.gpsimd.tensor_tensor(m2[:, r, j:CJ, :], edge[:, r, j:CJ, :], m1[:, r, j:CJ, :],
                                            ALU.subtract).then_inc(s_m2p, 1)

                first_rows(0)
                for q in range(NQ):
                    if q + 1 < NG:
                        first_rows(q + 1)
                    mask2(q // RING, q % RING)
                with pool.Fori(NQ // RING, 2 * NC // RING) as n4:
                    for r in range(RING):
                        mask2(n4, r)

            @block.scalar
            def _(act):
                act.sem_inc(s_ea, TPG)
                act.wait_ge(s_par, 32)
                nc.scalar.activation(coe[:, :], temp[:, :], ACT.Exp, scale=-1.0).then_inc(s_exp, 1)
                core.rstd_scalar(1)
                act.wait_ge(s_h0, 16)
                act.wait_ge(s_cf, 1)
                nc.scalar.activation(feat[:, :, :], feat[:, :, :], ACT.Copy, scale=cf[:, 1:2]).then_inc(s_h0s, 1)
                for g in range(NG):
                    act.wait_ge(s_xnT, g + 1)
                    if g >= 2:
                        act.wait_ge(s_fs, g - 1)
                    nc.scalar.copy(xnt[g % 2], bank[g % TPG].rearrange("p (t f) -> p t f", f=P)).then_inc(s_xnc, 1)
                act.wait_ge(s_z, 1)
                nc.scalar.activation(wb[:, :], f2[:, :], ACT.Exp, bias=nfall[:, 0:1], scale=1.0).then_inc(s_exp, 1)
                nc.scalar.activation(wd[:, :], f2[:, :], ACT.Exp, bias=nfall[:, 1:2], scale=ALPHA).then_inc(s_exp, 1)
                nc.scalar.activation(ca[:, :], ca[:, :], ACT.Exp).then_inc(s_exp, 1)
                nc.scalar.activation(cc[:, :], cc[:, :], ACT.Exp).then_inc(s_exp, 1)

                def second_rows(g):
                    act.wait_ge(s_feat, g + 2)
                    for v, w, r, s_v, s_hi, s_r in ((vd, wd, rd, s_vd, s_hd, s_rd), (vb, wb, rb, s_vb, s_hb, s_rb)):
                        act.wait_ge(s_r, g + (NG + 1))
                        for i in range(TPG):
                            t = g * TPG + i
                            ins = nc.scalar.activation(v[:, i, :], feat[:, t, :], ACT.Copy, scale=w[:, bass.ds(t, 1)])
                        ins.then_inc(s_v, 1)
                        act.wait_ge(s_v, g + (NG + 1))
                        nc.scalar.activation(tiles(r[1], g)[:, :, 0, 0:P], v[:, :, :], ACT.Copy).then_inc(s_hi, 1)

                def compare(g, b, q0, q1):
                    for q in range(q0, q1):
                        act.wait_ge(s_m1, g * NQ + (M_START + q - 1))
                        if q == 0:
                            act.wait_ge(s_f1g[b], (g + (2 - b)) * 8)
                        for i in range(CJ):
                            jt = q * CJ + i
                            ins = nc.scalar.activation(pos[:, q % 2, i, :], f1g[:, b, :], ACT.Sigmoid,
                                                       bias=steep[:, jt:jt + 1], scale=STEEP)
                        ins.then_inc(s_pos, 1)

                def copy_out(k, g):
                    act.wait_ge(s_pe, g * NQ + (k * NC + RING + NQ))
                    act.wait_ge(s_feat, g + (k * NG + 1))
                    for t in range(TPG):
                        nc.scalar.activation(acc_a[:, t, 0:2 * W[k]], bank[2 * t][:, 0:2 * W[k]], ACT.Copy,
                                             scale=ca[:, bass.ds(g * TPG + t, 1)]).then_inc(s_ea, 1)

                for g in range(NG):
                    for v, r, s_v, s_hi in ((vds, rd, s_vd, s_hd), (vbs, rb, s_vb, s_hb)):
                        act.wait_ge(s_v, g + 1)
                        nc.scalar.activation(tiles(r[0], g)[:, :, 0, 0:P], v[g % 2], ACT.Copy).then_inc(s_hi, 1)
                    compare(0, 0, g, g + 1)
                compare(1, 1, 0, AHEAD_S)
                for k in range(2):
                    with act.Fori(0, NG // 2 - k) as g2:
                        for b in range(2):
                            g = g2 * 2 + b
                            copy_out(k, g)
                            compare(g + (k * NG + 1), 1 - b, AHEAD_S, AHEAD_S + 3)
                            if k == 0:
                                second_rows(g)
                            compare(g + (k * NG + 1), 1 - b, AHEAD_S + 3, NQ)
                            compare(g + (k * NG + 2), b, 0, AHEAD_S)
                copy_out(1, NG - 2)
                compare(2 * NG - 1, 1, AHEAD_S, NQ)
                copy_out(1, NG - 1)

            @block.tensor
            def _(pe):
                pe.sem_inc(s_pe, RING)
                pe.wait_ge(s_id, 2)
                pe.wait_ge(s_par, 32)

                def transpose_group(g):
                    pe.wait_ge(s_xn, g + 1)
                    if g >= TPG:
                        pe.wait_ge(s_xnc, g - TPG + 1)
                    for k in range(TPG):
                        mm = nc.tensor.transpose(bank[g % TPG][:, k * P:(k + 1) * P], xn[:, g * TPG + k, :], core.id32[:, :])
                    mm.then_inc(s_xnT, 1)

                transpose_group(0)
                for g in range(NG):
                    if g + 1 < NG:
                        transpose_group(g + 1)
                    pe.wait_ge(s_xnc, g + 1)
                    for k in range(TPG):
                        t = g * TPG + k
                        mm = nc.tensor.matmul(bank[TPG][:, 2 * t:2 * t + 2], xnt[g % 2][:, k, :], a2[:, :], start=True, stop=True)
                    mm.then_inc(s_fs, 1)
                pe.wait_ge(s_f1, 1)
                nc.tensor.transpose(bank[0][0:NT, 0:P], f1[:, :], core.id32[:, :]).then_inc(s_f1T, 1)

                def group(k, g, by_chunk):
                    for q in range(NQ):
                        if by_chunk:
                            pe.wait_ge(s_rb, k * NG + (q + 2))
                            pe.wait_ge(s_rd, k * NG + (q + 2))
                        pe.wait_ge(s_m2p, g * NQ + (k * NC + M_START + q + 1))
                        pe.wait_ge(s_m2v, g * vector_tiles(NQ) + ((k * NG + 2) * vector_tiles(NQ) + vector_tiles(q + 1)))
                        steps = ([(j, t, o) for o in range(2) for t in range(TPG) for j in range(CJ)] if q == 0 else
                                 [(j, t, o) for j in range(CJ) for t in range(TPG) for o in range(2)])
                        for j, t, o in steps:
                            jt = q * CJ + j
                            m, r = ((m1, rb), (m2, rd))[o]
                            if jt == 0:
                                pe.wait_ge((s_ea, s_ec)[o], g * TPG + (k * NT + t + 1))
                            mm = nc.tensor.matmul(bank[2 * t + o][:, 0:2 * W[k]], m[:, q % RING, j, t * P:(t + 1) * P],
                                                  r[k][:, jt, :, :].rearrange("p h w -> p (h w)"),
                                                  start=(jt == 0), stop=(jt == NT - 1))
                        mm.then_inc(s_pe, 1)

                for k in range(2):
                    group(k, 0, True)
                    with pe.Fori(1, NG) as g:
                        group(k, g, False)

            @block.vector
            def _(dve):
                dve.sem_inc(s_m1, M_START)
                dve.sem_inc(s_m2v, 2 * vector_tiles(NQ))
                dve.sem_inc(s_edge, 2)
                dve.sem_inc(s_rd, 1)
                dve.sem_inc(s_feat, 1)
                dve.sem_inc(s_ec, TPG)
                for g in range(NG):
                    if g % 2 == 0:
                        dve.wait_ge(s_x[g // 2], 16)
                    core.stats_of_group(g)
                dve.wait_ge(s_exp, 1)
                V.link(nc.vector.tensor_scalar(coe[:, :], coe[:, :], 1.0, None, ALU.add))
                V.link(nc.vector.reciprocal(coe[:, :], coe[:, :]))
                V.link(nc.vector.tensor_scalar(om[:, :], coe[:, :], -1.0, 1.0, ALU.mult, ALU.add))
                V.tick(nc.vector.tensor_tensor(cf[:, 0:1], om[:, 1:2], coe[:, 0:1], ALU.mult))
                V.link(nc.vector.tensor_tensor(cf[:, 1:2], om[:, 1:2], om[:, 0:1], ALU.mult))
                dve.sem_inc(s_cf, 1)
                core.rstd_vector(1.0)
                for g in range(NG):
                    core.normalise_group(xn, g).then_inc(s_xn, 1)
                dve.wait_ge(s_fs, NG)
                fb = bank[TPG][:, 0:2 * NT].rearrange("p (t c) -> p t c", c=2)
                V.tick(nc.vector.tensor_copy(f1[:, :], fb[:, :, 0]))
                V.link(nc.vector.tensor_copy(f2[:, :], fb[:, :, 1]))
                dve.sem_inc(s_f1, 1)
                nc.vector.tensor_reduce(fmax[:, :], f2[:, :], AX, ALU.max).then_inc(s_fmax, 1)
                V.tick(nc.vector.tensor_scalar(steep[:, :], f2[:, :], STEEP, None, ALU.mult))
                dve.wait_ge(s_f1T, 1)
                nc.vector.tensor_copy(f1t, bank[0][0:NT, 0:P]).then_inc(s_f1s, 1)
                dve.wait_ge(s_fall, 1)
                V.tick(nc.vector.tensor_scalar(nfall[:, 0:1], fall[:, :], -1.0, None, ALU.mult))
                V.tick(nc.vector.tensor_scalar(nfall[:, 1:2], fall[:, :], -ALPHA, None, ALU.mult))
                V.link(nc.vector.tensor_scalar(z[:, :], f1[:, :], fall[:, 0:1], None, ALU.add))
                V.link(nc.vector.scalar_tensor_tensor(out=kx[:, :], in0=z[:, :], scalar=ALPHA, in1=z[:, :],
                                                      op0=ALU.mult, op1=ALU.max))
                V.tick(nc.vector.tensor_tensor(ca[:, :], z[:, :], kx[:, :], ALU.subtract))
                V.link(nc.vector.scalar_tensor_tensor(out=cc[:, :], in0=z[:, :], scalar=ALPHA, in1=kx[:, :],
                                                      op0=ALU.mult, op1=ALU.subtract))
                dve.sem_inc(s_z, 1)
                dve.wait_ge(s_exp, 5)
                V.tick(nc.vector.scalar_tensor_tensor(out=wb2[:, :], in0=wb[:, :], scalar=SC, in1=wb[:, :], op0=ALU.mult, op1=ALU.mult))
                V.link(nc.vector.scalar_tensor_tensor(out=wd2[:, :], in0=wd[:, :], scalar=SC, in1=wd[:, :], op0=ALU.mult, op1=ALU.mult))
                V.tick(nc.vector.tensor_scalar(wb[:, :], wb[:, :], SC, None, ALU.mult))
                V.link(nc.vector.tensor_scalar(wd[:, :], wd[:, :], SC, None, ALU.mult))
                dve.sem_inc(s_w, 1)
                for r, w, w2 in ((rb[0], wb, wb2), (rd[0], wd, wd2)):
                    V.tick(nc.vector.tensor_copy(r[:, :, 0, P], w[:, :]))
                    V.link(nc.vector.tensor_copy(r[:, :, 0, P + 1], w2[:, :]))
                    V.tick(nc.vector.tensor_tensor(r[:, :, 1, P], w[:, :], r[:, :, 0, P], ALU.subtract))
                    V.link(nc.vector.tensor_tensor(r[:, :, 1, P + 1], w2[:, :], r[:, :, 0, P + 1], ALU.subtract))
                dve.sem_inc(s_rb, 1)

                def lo_rows(k, g, vd, vb):
                    for v, r, s_v, s_hi, s_r in ((vd, rd, s_vd, s_hd, s_rd), (vb, rb, s_vb, s_hb, s_rb)):
                        dve.wait_ge(s_v, g + (k * NG + 1))
                        dve.wait_ge(s_hi, g + (k * NG + 1))
                        r = tiles(r[k], g)
                        nc.vector.tensor_tensor(r[:, :, 1, 0:P], v, r[:, :, 0, 0:P], ALU.subtract).then_inc(s_r, 1)

                def first_rows(g):
                    if g >= 2:
                        dve.wait_ge(s_rb, g)
                    nc.vector.tensor_tensor(vbs[g % 2], tiles(xn, g), over_columns(tiles(wb, g), P), ALU.mult).then_inc(s_vb, 1)

                def edges(g, q):
                    dve.wait_ge(s_adj[q % 2], g * (NQ // 2 * 16) + (q // 2 + 1) * 16)
                    dve.wait_ge(s_m2p, g * NQ + (M_START + q + 1 - RING))
                    dve.wait_ge(s_m2v, g * vector_tiles(NQ) + (2 * vector_tiles(NQ) + vector_tiles(q + 1 - RING)))
                    nc.vector.tensor_scalar(edge[:, q % RING], adj[:, q % 2], 0.0, None, ALU.is_gt).then_inc(s_edge, 1)

                def masks(g, q0, q1, more=True):
                    for q in range(q0, q1):
                        if q + 1 < NQ:
                            edges(g, q + 1)
                        elif more:
                            edges(g + 1, 0)
                        n = g * NQ + (q + 1)
                        dve.wait_ge(s_edge, n + 2)
                        dve.wait_ge(s_pos, n)
                        dve.wait_ge(s_pe, n)
                        r = q % RING
                        nc.vector.tensor_tensor(m1[:, r], edge[:, r], pos[:, q % 2], ALU.mult).then_inc(s_m1, 1)
                        if r == 0:
                            continue
                        dve.wait_ge(s_m1, n + M_START)
                        nc.vector.tensor_tensor(m2[:, r, 0, :], edge[:, r, 0, :], m1[:, r, 0, :], ALU.subtract).then_inc(s_m2v, 1)

                def sums(k, g):
                    w = W[k]
                    dve.wait_ge(s_pe, g * NQ + (k * NC + RING + NQ))
                    if k == 0:
                        s, d = tiles(sq, g), tiles(den, g)
                        for t in range(TPG):
                            ins = nc.vector.tensor_copy(sqd[:, t, :], banks[:, t, 1, w - 1:2 * w:w])
                        V.link(ins)
                        V.link(nc.vector.tensor_tensor(d, sqd[:, :, 0], sqd[:, :, 1], ALU.add))
                    for t in range(TPG):
                        dve.wait_ge(s_ea, g * TPG + (k * NT + TPG + t + 1))
                        nc.vector.scalar_tensor_tensor(out=acc_c[:, t, 0:2 * w], in0=bank[2 * t + 1][:, 0:2 * w],
                                                       scalar=cc[:, bass.ds(g * TPG + t, 1)], in1=acc_a[:, t, 0:2 * w],
                                                       op0=ALU.mult, op1=ALU.add).then_inc(s_ec, 1)
                    if k == 0:
                        V.tick(nc.vector.tensor_tensor(s, acc_a[:, :, w - 1], acc_a[:, :, 2 * w - 1], ALU.add))
                        V.link(nc.vector.tensor_tensor(d, d, tiles(cc, g), ALU.mult))
                        V.tick(nc.vector.tensor_tensor(s, s, tiles(ca, g), ALU.mult))
                        V.link(nc.vector.tensor_tensor(d, d, tiles(cc, g), ALU.mult))
                        V.tick(nc.vector.tensor_tensor(s, s, d, ALU.add))
                    dve.wait_ge(s_ec, g * TPG + (k * NT + 2 * TPG))
                    V.link(nc.vector.tensor_tensor(num[:, :, 0:w], acc_c[:, :, 0:w], acc_c[:, :, w:2 * w], ALU.add))

                def rowsums(g):
                    V.link(nc.vector.reciprocal(tiles(rden, g), num[:, :, P]))
                    V.link(nc.vector.tensor_tensor(tiles(den, g), tiles(rden, g), tiles(rden, g), ALU.mult))
                    V.link(nc.vector.scalar_tensor_tensor(out=tiles(rows, g), in0=tiles(den, g), scalar=0.5 * SC,
                                                          in1=tiles(sq, g), op0=ALU.mult, op1=ALU.mult))
                    V.link(nc.vector.tensor_scalar(tiles(kx, g), tiles(rows, g), -1.0, om[:, 2:3], ALU.mult, ALU.add))
                    for k in range(TPG):
                        t = g * TPG + k
                        ins = nc.vector.tensor_scalar(feat[:, t, :], xn[:, t, :], kx[:, bass.ds(t, 1)], None, ALU.mult)
                    V.tick(ins)

                def thresholded(g):
                    V.wait()
                    for k in range(TPG):
                        t = g * TPG + k
                        ins = nc.vector.scalar_tensor_tensor(out=feat[:, t, :], in0=num[:, k, 0:P], scalar=rden[:, bass.ds(t, 1)],
                                                             in1=feat[:, t, :], op0=ALU.mult, op1=ALU.add)
                    V.link(ins)
                    dve.wait_ge(s_rb, g + (NG + 1))
                    V.link(nc.vector.tensor_scalar(vb[:, :, :], tiles(feat, g), THRESH, -THRESH, ALU.min, ALU.max))
                    nc.vector.tensor_tensor(tiles(feat, g), tiles(feat, g), vb[:, :, :], ALU.subtract).then_inc(s_feat, 1)

                def add_pu(g):
                    for k in range(TPG):
                        t = g * TPG + k
                        ins = nc.vector.scalar_tensor_tensor(out=x[:, t, :], in0=num[:, k, 0:P], scalar=kp[:, bass.ds(t, 1)],
                                                             in1=x[:, t, :], op0=ALU.mult, op1=ALU.add)
                    ins.then_inc(s_feat, 1)

                def add_feat(g):
                    dve.wait_ge(s_feat, g + (NG + 2))
                    for k in range(TPG):
                        t = g * TPG + k
                        ins = nc.vector.scalar_tensor_tensor(out=x[:, t, :], in0=feat[:, t, :], scalar=kf[:, bass.ds(t, 1)],
                                                             in1=x[:, t, :], op0=ALU.mult, op1=ALU.add)
                    V.link(ins)
                    core.stats_of_group(g)

                FIRST_TICKS, SECOND_TICKS = 15, 3
                first_rows(0)
                edges(0, 0)
                for g in range(NG):
                    if g + 1 < NG:
                        first_rows(g + 1)
                    lo_rows(0, g, vds[g % 2], vbs[g % 2])
                    masks(0, g, g + 1)
                dve.wait_ge(s_res, NG)
                masks(1, 0, AHEAD)
                with dve.Fori(0, NG // 2) as g2:
                    V.loop(g2, 2 * FIRST_TICKS)
                    for b in range(2):
                        g = g2 * 2 + b
                        sums(0, g)
                        masks(g + 1, AHEAD, AHEAD + 1)
                        rowsums(g)
                        masks(g + 1, AHEAD + 1, AHEAD + 2)
                        thresholded(g)
                        masks(g + 1, AHEAD + 2, AHEAD + 4)
                        lo_rows(1, g, vd[:, :, :], vb[:, :, :])
                        masks(g + 1, AHEAD + 4, NQ)
                        masks(g + 2, 0, AHEAD)
                V.end(NG // 2)
                V.link(nc.vector.tensor_scalar(kf[:, :], rows[:, :], coe[:, 1:2], cf[:, 0:1], ALU.mult, ALU.add))
                V.link(nc.vector.tensor_scalar(kp[:, :], kf[:, :], coe[:, 3:4], None, ALU.mult))
                V.link(nc.vector.tensor_scalar(kp[:, :], kp[:, :], -1.0, coe[:, 1:2], ALU.mult, ALU.add))
                V.link(nc.vector.tensor_tensor(kp[:, :], kp[:, :], rden[:, :], ALU.mult))
                with dve.Fori(0, NG // 2 - 1) as g2:
                    V.loop(g2, 2 * SECOND_TICKS)
                    for b in range(2):
                        g = g2 * 2 + b
                        sums(1, g)
                        masks(g + (NG + 1), AHEAD, AHEAD + 1)
                        add_pu(g)
                        masks(g + (NG + 1), AHEAD + 1, AHEAD + 2)
                        add_feat(g)
                        masks(g + (NG + 1), AHEAD + 2, NQ)
                        masks(g + (NG + 2), 0, AHEAD)
                V.end(NG // 2 - 1)
                sums(1, NG - 2)
                masks(2 * NG - 1, AHEAD, AHEAD + 1)
                add_pu(NG - 2)
                masks(2 * NG - 1, AHEAD + 1, AHEAD + 2)
                add_feat(NG - 2)
                masks(2 * NG - 1, AHEAD + 2, NQ, more=False)
                sums(1, NG - 1)
                add_pu(NG - 1)
                add_feat(NG - 1)
                V.wait()


def split_tensors(core, c, tag):
    xs = core.sb(c, f"xs{tag}", [P, NT, P], F32)
    xh = core.sb(c, f"xh{tag}", [P, NT, 2, P], F16)
    xt = core.sb(c, f"xt{tag}", [P, 2, N], F16)
    turn = core.ps(c, f"turn{tag}", [P, 2, GW], F16)
    sems = [core.sem(f"{n}{tag}") for n in ("xs_ready", "xs_hi_ready", "xs_lo_ready", "xs_turned", "xt_ready")]
    return xs, xh, xt, turn, sems


def split_vector(core, s, small, then=None):
    xs, xh, xt, turn, (s_n, s_h, s_l, s_t, s_c) = s
    nc = core.nc
    core.rstd_vector(SC)
    core.normalise_group(xs, 0).then_inc(s_n, 1)
    small()
    for g in range(NG):
        if g + 1 < NG:
            core.normalise_group(xs, g + 1).then_inc(s_n, 1)
        nc.vector.wait_ge(s_n, g + 1)
        nc.vector.wait_ge(s_h, g + 1)
        nc.vector.tensor_tensor(tiles(xh, g)[:, :, 1, :], tiles(xs, g), tiles(xh, g)[:, :, 0, :], ALU.subtract).then_inc(s_l, 1)
        if then and g >= 3:
            then(g - 3)
    if then:
        for g in range(NG - 3, NG):
            then(g)


def split_scalar(core, s, n, spare, then=None):
    xs, xh, xt, turn, (s_n, s_h, s_l, s_t, s_c) = s
    nc = core.nc
    core.rstd_scalar(n)

    def hi(g):
        nc.scalar.wait_ge(s_n, g + 1)
        nc.scalar.activation(tiles(xh, g)[:, :, 0, :], tiles(xs, g), ACT.Copy).then_inc(s_h, 1)

    hi(0)
    for g in range(NG):
        if g + 1 < NG:
            hi(g + 1)
        for h in range(2):
            nc.scalar.wait_ge(s_t, 2 * g + h + 1)
            nc.scalar.activation(xt[:, h, g * GW:(g + 1) * GW], (turn[:, 0, :], spare)[h], ACT.Copy).then_inc(s_c, 1)
        if then and g >= 2:
            then(g - 2)
    if then:
        for g in range(NG - 2, NG):
            then(g)


def split_tensor(core, s, spare, then):
    xs, xh, xt, turn, (s_n, s_h, s_l, s_t, s_c) = s
    nc = core.nc

    def turn_group(g):
        for h in range(2):
            nc.tensor.wait_ge((s_h, s_l)[h], g + 1)
            if g:
                nc.tensor.wait_ge(s_c, 2 * g - 1 + h)
            for k in range(TPG):
                mm = nc.tensor.transpose((turn[:, 0, :], spare)[h][:, k * P:(k + 1) * P], xh[:, g * TPG + k, h, :], core.id16[:, :])
            mm.then_inc(s_t, 1)

    turn_group(0)
    for g in range(NG):
        if g + 1 < NG:
            turn_group(g + 1)
        nc.tensor.wait_ge(s_c, 2 * g + 2)
        then(g)


def experts(core, tag, S, wg_d, bg_d, w1_d, b1_d, w2_d, b2_d, x_rows, y_rows, out_d):
    nc, x, V, G, sem = core.nc, core.x, core.V, core.G, core.sem
    E = S + R
    norm = core.norms + 1
    CP = HC // 2
    PPU = HC // CP
    UPG = TPG // UT
    PPG = UPG * PPU
    RING = PPG
    LA = PPU
    DP, DG = S * NG * PPG, S * NG
    SG = HALVES * SNG
    with ExitStack() as c:
        def sb(name, shape, dt=F32):
            return core.sb(c, f"{name}{tag}", shape, dt)

        s = split_tensors(core, c, tag)
        xs, xh, xt, turn, (s_n, s_h, s_l, s_t, s_c) = s
        wg = sb("wg", [P, R])
        wgs = sb("wgs", [P, 2, R], F16)
        bg = sb("bg", [P, R])
        wf = sb("wf", [P, 2, 2, HC * P])
        w1 = sb("w1", [P, 2, E, HC, P], F16)
        w2 = sb("w2", [P, 2, E, HC, P], F16)
        b1 = sb("b1", [P, E, HC])
        b2f = sb("b2f", [2, E, P])
        b2h = sb("b2h", [2, E, P], F16)
        b2s = sb("b2s", [2, E, P], F16)
        pick2 = sb("pick2", [2, P], F16)
        low2 = sb("low2", [2, 1])
        lg = sb("lg", [P, NT, R])
        t1 = sb("t1", [P, NT, R])
        oh = sb("oh", [P, 2, NT, R])
        both = sb("both", [P, NT, R], F16)
        best = sb("best", [P, 2, NT])
        pick = sb("pick", [P, NT])
        ex = sb("ex", [P, NT])
        wt = sb("wt", [P, 2, NT])
        order = sb("order", [P, R])
        below = sb("below", [P, P], F16)
        ones = sb("ones", [P, P], F16)
        before = sb("before", [P, R, R])
        countn = sb("countn", [P, SNU], mybir.dt.int32)
        count = sb("count", [P, SNU])
        run = [sb(f"run{k}", [P, HALVES, HNT, R]) for k in range(2)]
        cnt = sb("cnt", [P, HALVES, HNT, R])
        tot = sb("tot", [P, HALVES, R])
        more = sb("more", [P, HALVES, R, HNT // UT])
        nt = sb("nt", [P, HALVES, R])
        prod = sb("prod", [P, HALVES, R, R])
        off = sb("off", [P, HALVES, R])
        base = sb("base", [P, HALVES, R])
        past = sb("past", [P, HALVES, SNU, R])
        owner = sb("owner", [P, HALVES, SNU])
        own = sb("own", [P, HALVES * SNU], mybir.dt.int32)
        slotf = sb("slotf", [P, 2, NT])
        slot = sb("slot", [P, 2, NT], mybir.dt.uint32)
        xg = sb("xg", [P, 2, TPG, 2 * P], F16)
        xgt = sb("xgt", [P, 2, 2, GW], F16)
        h32 = sb("h32", [P, RING, GW])
        hh = sb("hh", [P, RING, GW], F16)
        hl = sb("hl", [P, RING, GW], F16)
        yo = sb("yo", [P, 2, TPG, P])
        got = sb("got", [P, NT, 2, P])
        hbank = [core.ps(c, f"hid{tag}_{k}", [P, GW], F32) for k in range(RING)]
        ybank = [core.ps(c, f"y{tag}_{k}", [P, TPG, P], F32) for k in range(2)]
        lbank = core.ps(c, f"logits{tag}", [P, 2, NT * R], F32)
        spare = hbank[RING - 1][:, :].bitcast(F16)[:, 0:GW]

        s_wg = sem(f"gate_loaded{tag}")
        s_b = sem(f"biases_loaded{tag}")
        s_w = [sem(f"weights_loaded{tag}{b}") for b in range(2)]
        s_wh = sem(f"weights_hi{tag}")
        s_ws = sem(f"weights_split{tag}")
        s_small = sem(f"small_split{tag}")
        s_lg = sem(f"logits_summed{tag}")
        s_const = sem(f"constants_ready{tag}")
        s_ex = sem(f"gap_exp{tag}")
        s_both, s_rank = sem(f"choices_ready{tag}"), sem(f"ranks_summed{tag}")
        s_slot = sem(f"slots_ready{tag}")
        s_sc = [sem(f"half_scattered{tag}{h}") for h in range(HALVES)]
        s_xg = [sem(f"slot_rows_loaded{tag}{b}") for b in range(2)]
        s_xgt = sem(f"slot_rows_turned{tag}")
        s_xgc = sem(f"turned_copied{tag}")
        s_h1 = sem(f"hidden_summed{tag}")
        s_ge = sem(f"gelu_done{tag}")
        s_hh, s_hl = sem(f"hidden_hi{tag}"), sem(f"hidden_lo{tag}")
        s_y = sem(f"unit_done{tag}")
        s_add = sem(f"dense_added{tag}")
        s_yo = sem(f"y_copied{tag}")
        s_st = [sem(f"y_stored{tag}{b}") for b in range(2)]
        s_got = [sem(f"y_gathered{tag}{i}") for i in range(NG // 2 + 1)]
        s_res = sem(f"group_done{tag}")
        s_out = sem(f"stored{tag}")

        def got_by(g):
            return NG // 2 if g == NG - 1 else g // 2

        def load_owners(engine, u, n):
            return nc.values_load_multi_w_load_instructions(
                own[0:1, bass.ds(u, n)], engines=(engine,), min_val=S, max_val=E - 1,
                skip_runtime_bounds_check_because="the number of an expert")[1]

        with nc.Block() as block:

            @block.sync
            def _(sp):
                sp.sem_inc(s_st[0], 16)
                sp.sem_inc(s_st[1], 16)
                sp.dma_start(wg[:, :], wg_d).then_inc(s_wg, 16)
                if bg_d is not None:
                    sp.dma_start(bg[:, :], bg_d.partition_broadcast(P)).then_inc(s_wg, 16)
                sp.dma_start(b1[:, :, :], b1_d).then_inc(s_b, 16)
                for h in range(2):
                    sp.dma_start(b2f[h:h + 1, :, :], b2_d[None, :, :]).then_inc(s_b, 16)
                for e in range(E):
                    sp.wait_ge(s_ws, 2 * (e + 1))
                    sp.dma_start(wf[:, e % 2, 0, :], w1_d[e]).then_inc(s_w[e % 2], 16)
                    sp.dma_start(wf[:, e % 2, 1, :], w2_d[e]).then_inc(s_w[e % 2], 16)

                def of_group(rows, g):
                    return rows.rearrange("(g t p) f -> g p t f", p=P, t=TPG)[bass.ds(g, 1)].squeeze(0)

                def load(h, g, b):
                    sp.wait_ge(s_xgt, g + (h * SNG + 1))
                    sp.dma_start(xg[:, b, :, :], of_group(x_rows[h], g)).then_inc(s_xg[b], 16)

                def store(h, g, b):
                    sp.wait_ge(s_yo, g + (h * SNG + 3))
                    sp.dma_start(of_group(y_rows[h], g), yo[:, b, :, :]).then_inc(s_st[b], 16)

                for h in range(HALVES):
                    sp.wait_ge(s_sc[h], 2 * HNT * 16)
                    load(h, 0, 0)
                    load(h, 1, 1)
                    if h:
                        store(h - 1, SNG - 2, 0)
                        store(h - 1, SNG - 1, 1)
                    with sp.Fori(0, SNG // 2 - 1) as g2:
                        for b in range(2):
                            load(h, g2 * 2 + (b + 2), b)
                            store(h, g2 * 2 + b, b)
                store(HALVES - 1, SNG - 2, 0)
                store(HALVES - 1, SNG - 1, 1)
                if out_d is not None:
                    for g in range(NG):
                        sp.wait_ge(s_res, g + 1)
                        sp.dma_start(tiles(out_d, g), tiles(x, g)).then_inc(s_out, 16)
                    sp.wait_ge(s_out, 16 * NG)

            @block.gpsimd
            def _(pool):
                for k in range(R):
                    nc.gpsimd.memset(order[:, k:k + 1], float(R - k))
                G.link(nc.gpsimd.memset(ones[:, :], 1.0))
                nc.gpsimd.affine_select(out=below[:, :], in_=ones[:, :], compare_op=ALU.is_gt, fill=0.0, base=0,
                                        pattern=[[1, P]], channel_multiplier=-1)
                G.link(nc.gpsimd.memset(before[:, :, :], 1.0))
                nc.gpsimd.affine_select(out=before[:, :, :], in_=before[:, :, :], compare_op=ALU.is_gt, fill=0.0, base=0,
                                        pattern=[[1, R], [-1, R]], channel_multiplier=0)
                G.link(nc.gpsimd.iota(countn[:, :], [[1, SNU]], base=0, channel_multiplier=0))
                nc.gpsimd.tensor_copy(count[:, :], countn[:, :]).then_inc(s_const, 1)
                G.tick(nc.gpsimd.memset(pick2[:, :], HS))
                G.link(nc.gpsimd.memset(low2[:, :], 1.0))
                nc.gpsimd.affine_select(out=low2[:, :], in_=low2[:, :], compare_op=ALU.is_ge, fill=0.0, base=-1,
                                        pattern=[[0, 1]], channel_multiplier=1).then_inc(s_const, 1)
                pool.wait_ge(s_b, 48)
                pool.wait_ge(s_const, 2)
                G.link(nc.gpsimd.tensor_scalar(b2f[:, :, :], b2f[:, :, :], SC, None, ALU.mult))
                G.link(nc.gpsimd.tensor_copy(b2h[:, :, :], b2f[:, :, :]))
                G.link(nc.gpsimd.tensor_scalar(b2h[:, :, :], b2h[:, :, :], low2[:, 0:1], None, ALU.mult))
                pool.wait_ge(s_small, 1)
                nc.gpsimd.tensor_tensor(b2s[:, :, :], b2f[:, :, :], b2h[:, :, :], ALU.subtract).then_inc(s_small, 1)
                pool.wait_ge(core.s_zero, 16 * HALVES)
                pool.wait_ge(s_l, NG)
                pool.wait_ge(s_slot, 1)
                for h in range(HALVES):
                    for t in range(h * HNT, (h + 1) * HNT):
                        for k in range(2):
                            nc.gpsimd.indirect_dma_start(
                                x_rows[h], bass.IndirectOffsetOnAxis(slot[:, k, t:t + 1], 0),
                                xh[:, t, :, :].rearrange("p h f -> p (h f)"), None).then_inc(s_sc[h], 16)
                for h in range(HALVES):
                    for b in range(2):
                        pool.wait_ge(s_st[b], 16 + (h + 1) * (SNG // 2 * 16))
                    for t in range(h * HNT, (h + 1) * HNT):
                        for k in range(2):
                            nc.gpsimd.indirect_dma_start(
                                got[:, t, k, :], None, y_rows[h],
                                bass.IndirectOffsetOnAxis(slot[:, k, t:t + 1], 0)).then_inc(s_got[got_by(t // TPG)], 16)

            @block.scalar
            def _(act):
                act.sem_inc(s_ge, RING)
                act.sem_inc(s_yo, 2)
                split_scalar(core, s, norm, spare)

                def weights_hi(e, m):
                    act.wait_ge(s_w[e % 2], (e // 2 + 1) * 32)
                    nc.scalar.activation((w1, w2)[m][:, 0, e].rearrange("p c n -> p (c n)"), wf[:, e % 2, m, :], ACT.Copy,
                                         scale=SC).then_inc(s_wh, 1)

                for e in range(2):
                    for m in range(2):
                        weights_hi(e, m)
                act.wait_ge(s_both, 1)
                nc.scalar.activation(ex[:, :], ex[:, :], ACT.Exp).then_inc(s_ex, 1)

                def gelu(v, r, e):
                    act.wait_ge(s_h1, v + 1)
                    act.wait_ge(s_hl, v + 1)
                    for k in range(CP):
                        c = r % PPU * CP + k
                        ins = nc.scalar.activation(h32[:, r, k * UW:(k + 1) * UW], hbank[r][:, k * UW:(k + 1) * UW], ACT.Gelu,
                                                   bias=b1[:, e, c:c + 1], scale=1.0 / (SC * SC))
                    ins.then_inc(s_ge, 1)

                def copy_y(g, b):
                    act.wait_ge(s_y, g * PPG + (DP + RING + PPG))
                    act.wait_ge(s_st[b], (g + (2 - b)) * 8)
                    nc.scalar.copy(yo[:, b, :, :], ybank[b][:, :, :]).then_inc(s_yo, 1)

                act.wait_ge(s_b, 48)
                if S:
                    for g in range(DG):
                        for r in range(PPG):
                            gelu(g * PPG + r, r, 0)
                            if r == 1 and g:
                                weights_hi(g + 1, 1)
                            if r == PPG - 1 and g + 2 < E:
                                weights_hi(g + 2, 0)
                else:
                    for e in range(2, E):
                        for m in range(2):
                            weights_hi(e, m)
                act.wait_ge(s_slot, 2)
                e = load_owners(mybir.EngineType.Activation, 0, 1)
                for r in range(LA):
                    gelu(DP + r, r, e[0])
                with act.Fori(0, SG // 2 - 1) as g2:
                    e = load_owners(mybir.EngineType.Activation, g2 * (2 * UPG), 2 * UPG + 1)
                    for b in range(2):
                        for i in range(PPG):
                            n = b * PPG + i + LA
                            gelu(g2 * (2 * PPG) + (DP + n), n % RING, e[n // PPU])
                        copy_y(g2 * 2 + b, b)
                e = load_owners(mybir.EngineType.Activation, (SG - 2) * UPG, 2 * UPG)
                for n in range(LA, 2 * PPG):
                    gelu(DP + (SG - 2) * PPG + n, n % RING, e[n // PPU])
                    if n == PPG + LA - 1:
                        copy_y(SG - 2, 0)
                copy_y(SG - 1, 1)

            @block.vector
            def _(dve):
                dve.sem_inc(s_hl, RING)
                dve.sem_inc(s_add, 2)
                dve.sem_inc(s_xgc, 1)
                dve.sem_inc(s_ws, 4)

                def split_gate():
                    dve.wait_ge(s_wg, 16 if bg_d is None else 32)
                    V.link(nc.vector.tensor_scalar(wgs[:, 0, :], wg[:, :], SC, None, ALU.mult))
                    nc.vector.scalar_tensor_tensor(out=wgs[:, 1, :], in0=wg[:, :], scalar=SC, in1=wgs[:, 0, :],
                                                   op0=ALU.mult, op1=ALU.subtract).then_inc(s_small, 1)

                split_vector(core, s, split_gate)
                dve.wait_ge(s_const, 2)

                def weights_lo(e, m):
                    dve.wait_ge(s_wh, 2 * e + m + 1)
                    hi, lo = ((w1, w2)[m][:, h, e].rearrange("p c n -> p (c n)") for h in range(2))
                    nc.vector.scalar_tensor_tensor(out=lo, in0=wf[:, e % 2, m, :], scalar=SC, in1=hi,
                                                   op0=ALU.mult, op1=ALU.subtract).then_inc(s_ws, 1)

                for e in range(S):
                    for m in range(2):
                        weights_lo(e, m)
                dve.wait_ge(s_lg, NG)
                lview = lbank[:, 0, :].rearrange("p (t r) -> p t r", r=R)
                V.link(nc.vector.tensor_scalar(lg[:, :, :], lview, 1.0 / (SC * SC), None, ALU.mult))
                if bg_d is not None:
                    V.link(nc.vector.tensor_tensor(lg[:, :, :], lg[:, :, :], bg[:, None, :].to_broadcast([P, NT, R]), ALU.add))
                obc = order[:, None, :].to_broadcast([P, NT, R])
                for k in range(2):
                    V.link(nc.vector.tensor_reduce(best[:, k, :], lg[:, :, :], AX, ALU.max))
                    V.link(nc.vector.tensor_tensor(t1[:, :, :], lg[:, :, :], over_columns(best[:, k, :], R), ALU.is_equal))
                    V.link(nc.vector.tensor_tensor(t1[:, :, :], t1[:, :, :], obc, ALU.mult))
                    V.link(nc.vector.tensor_reduce(pick[:, :], t1[:, :, :], AX, ALU.max))
                    V.link(nc.vector.tensor_tensor(oh[:, k], obc, over_columns(pick[:, :], R), ALU.is_equal))
                    if k == 0:
                        V.link(nc.vector.scalar_tensor_tensor(out=lg[:, :, :], in0=oh[:, 0], scalar=-BIG, in1=lg[:, :, :],
                                                              op0=ALU.mult, op1=ALU.add))
                nc.vector.tensor_tensor(ex[:, :], best[:, 1, :], best[:, 0, :], ALU.subtract).then_inc(s_both, 1)
                nc.vector.tensor_tensor(both[:, :, :], oh[:, 0], oh[:, 1], ALU.add).then_inc(s_both, 1)
                dve.wait_ge(s_rank, 1)
                rank = lbank[:, 0, :].rearrange("p (h t r) -> p h t r", h=HALVES, r=R)
                V.link(nc.vector.tensor_copy(cnt[:, :, :, :], lbank[:, 1, :].rearrange("p (h t r) -> p h t r", h=HALVES, r=R)))
                a, step, k = cnt, 1, 0
                while step < HNT:
                    V.tick(nc.vector.tensor_copy(run[k][:, :, 0:step, :], a[:, :, 0:step, :]))
                    V.link(nc.vector.tensor_tensor(run[k][:, :, step:, :], a[:, :, step:, :], a[:, :, 0:HNT - step, :], ALU.add))
                    a, step, k = run[k], 2 * step, 1 - k
                V.tick(nc.vector.tensor_tensor(cnt[:, :, :, :], a[:, :, :, :], cnt[:, :, :, :], ALU.subtract))
                V.link(nc.vector.tensor_scalar(tot[:, :, :], a[:, :, HNT - 1, :], 1.0 / UW, None, ALU.mult))
                V.link(nc.vector.tensor_tensor(more[:, :, :, :], tot[:, :, :].unsqueeze(3).to_broadcast([P, HALVES, R, HNT // UT]),
                                               count[:, None, None, 0:HNT // UT].to_broadcast([P, HALVES, R, HNT // UT]), ALU.is_gt))
                V.link(nc.vector.tensor_reduce(nt[:, :, :], more[:, :, :, :], AX, ALU.add))
                V.link(nc.vector.tensor_tensor(prod[:, :, :, :], nt[:, :, None, :].to_broadcast([P, HALVES, R, R]),
                                               before[:, None, :, :].to_broadcast([P, HALVES, R, R]), ALU.mult))
                V.link(nc.vector.tensor_reduce(off[:, :, :], prod[:, :, :, :], AX, ALU.add))
                V.tick(nc.vector.tensor_scalar(base[:, :, :], off[:, :, :], float(UW), None, ALU.mult))
                V.link(nc.vector.tensor_tensor(cnt[:, :, :, :], cnt[:, :, :, :], rank, ALU.add))
                V.link(nc.vector.tensor_tensor(cnt[:, :, :, :], cnt[:, :, :, :],
                                               base[:, :, None, :].to_broadcast([P, HALVES, HNT, R]), ALU.add))
                for k in range(2):
                    V.link(nc.vector.tensor_tensor(t1[:, :, :], oh[:, k], cnt[:, :, :, :].rearrange("p h t r -> p (h t) r"), ALU.mult))
                    V.link(nc.vector.tensor_reduce(slotf[:, k, :], t1[:, :, :], AX, ALU.add))
                nc.vector.tensor_copy(slot[:, :, :], slotf[:, :, :]).then_inc(s_slot, 1)
                V.link(nc.vector.tensor_tensor(off[:, :, :], off[:, :, :], nt[:, :, :], ALU.add))
                V.link(nc.vector.tensor_tensor(past[:, :, :, :], off[:, :, None, :].to_broadcast([P, HALVES, SNU, R]),
                                               count[:, None, :, None].to_broadcast([P, HALVES, SNU, R]), ALU.is_le))
                V.link(nc.vector.tensor_reduce(owner[:, :, :], past[:, :, :, :], AX, ALU.add))
                V.link(nc.vector.tensor_scalar(owner[:, :, :], owner[:, :, :], float(R - 1), float(S), ALU.min, ALU.add))
                nc.vector.tensor_copy(own[:, :], owner[:, :, :].rearrange("p h s -> p (h s)")).then_inc(s_slot, 1)

                def parts(v, r):
                    dve.wait_ge(s_ge, v + (RING + 1))
                    dve.wait_ge(s_y, v + 1)
                    nc.vector.tensor_scalar(hh[:, r, :], h32[:, r, :], HS, None, ALU.mult).then_inc(s_hh, 1)
                    dve.wait_ge(s_hh, v + 1)
                    nc.vector.scalar_tensor_tensor(out=hl[:, r, :], in0=h32[:, r, :], scalar=HS, in1=hh[:, r, :],
                                                   op0=ALU.mult, op1=ALU.subtract).then_inc(s_hl, 1)

                def copy_turned(g, b):
                    dve.wait_ge(s_xgt, g + 3)
                    nc.vector.tensor_copy(xgt[:, b, :, :], turn[:, :, :]).then_inc(s_xgc, 1)

                def add_dense(g, b):
                    dve.wait_ge(s_y, g * PPG + (RING + PPG))
                    nc.vector.scalar_tensor_tensor(out=tiles(x, g), in0=ybank[b][:, :, :], scalar=1.0 / (SC * HS),
                                                   in1=tiles(x, g), op0=ALU.mult, op1=ALU.add).then_inc(s_add, 1)

                if S:
                    for n in range(LA):
                        parts(n, n)
                    for g in range(DG):
                        for n in range(g * PPG + LA, (g + 1) * PPG + LA):
                            if n < DP:
                                parts(n, n % RING)
                            if g + S < E and n % 2:
                                weights_lo(g + S, (n - LA) % PPG // 2)
                        add_dense(g, g % 2)
                else:
                    for e in range(E):
                        for m in range(2):
                            weights_lo(e, m)
                copy_turned(0, 0)
                parts(DP, 0)
                with dve.Fori(0, SG // 2 - 1) as g2:
                    for b in range(2):
                        v = g2 * (2 * PPG) + (DP + b * PPG)
                        parts(v + 1, 1)
                        copy_turned(g2 * 2 + (b + 1), 1 - b)
                        for n in range(2, PPG + 1):
                            parts(v + n, n % RING)
                v = DP + (SG - 2) * PPG
                parts(v + 1, 1)
                copy_turned(SG - 1, 1)
                for n in range(2, 2 * PPG):
                    parts(v + n, n % RING)
                dve.wait_ge(s_ex, 1)
                V.link(nc.vector.tensor_scalar(wt[:, 0, :], ex[:, :], 1.0, None, ALU.add))
                V.link(nc.vector.reciprocal(wt[:, 0, :], wt[:, 0, :]))
                V.link(nc.vector.tensor_scalar(wt[:, 0, :], wt[:, 0, :], 1.0 / (SC * HS), None, ALU.mult))
                V.link(nc.vector.tensor_tensor(wt[:, 1, :], wt[:, 0, :], ex[:, :], ALU.mult))
                dve.wait_ge(s_add, 2 + DG)
                for g in range(NG):
                    if got_by(g) != got_by(g - 1):
                        dve.wait_ge(s_got[got_by(g)], (2 if g >= NG - 2 else 4) * TPG * 16)
                    for k in range(2):
                        for t in range(g * TPG, (g + 1) * TPG):
                            ins = nc.vector.scalar_tensor_tensor(out=x[:, t, :], in0=got[:, t, k, :], scalar=wt[:, k, t:t + 1],
                                                                 in1=x[:, t, :], op0=ALU.mult, op1=ALU.add)
                        if k == 0 or out_d is None:
                            V.link(ins)
                        else:
                            ins.then_inc(s_res, 1)
                    if out_d is None:
                        core.stats_of_group(g)
                V.wait()

            @block.tensor
            def _(pe):
                pe.sem_inc(s_y, RING)
                pe.sem_inc(s_xgt, 2)

                def logits(g):
                    if g == 0:
                        pe.wait_ge(s_small, 1)
                    for t in range(g * TPG, (g + 1) * TPG):
                        for n, (h, w) in enumerate(((0, 0), (0, 1), (1, 0))):
                            mm = nc.tensor.matmul(lbank[:, 0, t * R:(t + 1) * R], xt[:, h, t * P:(t + 1) * P], wgs[:, w, :],
                                                  start=(n == 0), stop=(n == 2))
                    mm.then_inc(s_lg, 1)

                split_tensor(core, s, spare, logits)
                pe.wait_ge(s_both, 2)
                pe.wait_ge(s_const, 1)
                for i, m in enumerate((below, ones)):
                    mm = nc.tensor.matmul(lbank[:, i, :], m[:, :], both[:, :, :].rearrange("p t r -> p (t r)"), start=True, stop=True)
                mm.then_inc(s_rank, 1)

                def first(v, r, rows, e):
                    pe.wait_ge(s_ge, v + 1)
                    for k in range(CP):
                        for n, (h, w) in enumerate(((0, 0), (1, 0), (0, 1))):
                            mm = nc.tensor.matmul(hbank[r][:, k * UW:(k + 1) * UW],
                                                  w1[:, w, bass.ds(e, 1), r % PPU * CP + k, :].squeeze(1), rows[h],
                                                  start=(n == 0), stop=(n == 2))
                    mm.then_inc(s_h1, 1)

                def second(v, i, e, b):
                    pe.wait_ge(s_hl, v + (RING + 1))
                    at = [(i // PPU * UT + t, t * P) for t in range(UT)]
                    if i % PPU == 0:
                        for j, _ in at:
                            nc.tensor.matmul(ybank[b][:, j, :], pick2[:, :], b2s[:, bass.ds(e, 1), :].squeeze(1),
                                             start=(j == 0), stop=False, skip_group_check=True)
                    for k in range(CP):
                        for w, h in ((0, hh), (0, hl), (1, hh)):
                            for j, c0 in at:
                                mm = nc.tensor.matmul(ybank[b][:, j, :], h[:, i, k * UW + c0:k * UW + c0 + P],
                                                      w2[:, w, bass.ds(e, 1), i % PPU * CP + k, :].squeeze(1),
                                                      start=False, stop=(i == PPG - 1 and k == CP - 1 and w == 1 and j == TPG - 1),
                                                      skip_group_check=True)
                    mm.then_inc(s_y, 1)

                def transpose_rows(g, b):
                    pe.wait_ge(s_xg[b], (g + (2 - b)) * 8)
                    pe.wait_ge(s_xgc, g + 1)
                    for h in range(2):
                        for j in range(TPG):
                            mm = nc.tensor.transpose(turn[:, h, j * P:(j + 1) * P], xg[:, b, j, h * P:(h + 1) * P], core.id16[:, :])
                    mm.then_inc(s_xgt, 1)

                pe.wait_ge(s_small, 2)
                if S:
                    pe.wait_ge(s_ws, 4 + 2 * S)

                    def dense_rows(u):
                        return [xt[:, h, bass.ds(u * UW, UW)] for h in range(2)]

                    def dense_pair(g2, last):
                        for b in range(2):
                            for i in range(PPG):
                                n = b * PPG + i
                                v = g2 * (2 * PPG) + n
                                if n + LA < 2 * PPG or not last:
                                    first(v + LA, (n + LA) % RING, dense_rows(g2 * (2 * UPG) + (n + LA) // PPU), 0)
                                if i == 0:
                                    pe.wait_ge(s_add, g2 * 2 + (b + 1))
                                second(v, i, 0, b)

                    for v in range(LA):
                        first(v, v, dense_rows(0), 0)
                    with pe.Fori(0, DG // 2 - 1) as g2:
                        dense_pair(g2, False)
                    dense_pair(DG // 2 - 1, True)
                    pe.wait_ge(s_add, 2 + DG)

                def slot_rows(b, u):
                    return [xgt[:, b, h, u * UW:(u + 1) * UW] for h in range(2)]

                def slot_pair(g2, e, last):
                    for b in range(2):
                        for i in range(PPG):
                            n = b * PPG + i
                            v = g2 * (2 * PPG) + (DP + n)
                            if i == 0 and not (last and b):
                                transpose_rows(g2 * 2 + (b + 1), 1 - b)
                            if n + LA < 2 * PPG or not last:
                                if i + LA == PPG:
                                    pe.wait_ge(s_xgc, g2 * 2 + (b + 3))
                                u = (n + LA) // PPU
                                first(v + LA, (n + LA) % RING, slot_rows(u // UPG % 2, u % UPG), e[u])
                            if i == 0:
                                pe.wait_ge(s_yo, g2 * 2 + (b + 1))
                            second(v, i, e[n // PPU], b)

                transpose_rows(0, 0)
                pe.wait_ge(s_ws, 4 + 2 * E)
                pe.wait_ge(s_slot, 2)
                pe.wait_ge(s_xgc, 2)
                e = load_owners(mybir.EngineType.PE, 0, 1)
                for v in range(LA):
                    first(DP + v, v, slot_rows(0, 0), e[0])
                with pe.Fori(0, SG // 2 - 1) as g2:
                    slot_pair(g2, load_owners(mybir.EngineType.PE, g2 * (2 * UPG), 2 * UPG + 1), False)
                slot_pair(SG // 2 - 1, load_owners(mybir.EngineType.PE, (SG - 2) * UPG, 2 * UPG), True)


def aggregate(core, io):
    nc, x, V, sem = core.nc, core.x, core.V, core.sem
    W = P + 1
    norm = core.norms + 1
    RING = 4
    CV = CJ - 1
    AHEAD = RING - 1
    with ExitStack() as c:
        def sb(name, shape, dt=F32):
            return core.sb(c, name, shape, dt)

        s = split_tensors(core, c, "g")
        xs, xh, xt, turn, (s_n, s_h, s_l, s_t, s_c) = s
        kf = sb("kernf", [P, P])
        ks = sb("kerns", [P, 2, P], F16)
        ys = sb("ys", [P, NT, P])
        ry = sb("ry", [P, NT, 2, W], F16)
        bias = sb("bias", [P, P])
        beta = sb("beta", [P, NT])
        adj = sb("adjg", [P, NQ, CJ, GW])
        ah = sb("ah", [P, RING, CJ, GW], F16)
        al = sb("al", [P, RING, CJ, GW], F16)
        acc = sb("accg", [P, TPG, 2 * W])
        num = sb("numg", [P, TPG, W])
        sc = sb("scg", [P, TPG])
        bank = [core.ps(c, f"agg{b}", [P, 512], F32) for b in range(TPG + 1)]
        spare = bank[TPG][:, :].bitcast(F16)[:, 0:GW]
        s_par = sem("kernel_loaded")
        s_ks = sem("kernel_split")
        s_one = sem("ones_ready")
        s_xb = sem("bias_added")
        s_y = sem("y_summed")
        s_yc = sem("y_copied")
        s_yh, s_yl = sem("y_hi"), sem("y_lo")
        s_adj = [sem(f"adjg_loaded{q}") for q in range(NQ)]
        s_ah = sem("adj_hi")
        s_al, s_alp = sem("adj_lo_by_vector"), sem("adj_lo_by_gpsimd")
        s_pe = sem("adj_parts_used")
        s_acc = sem("sums_copied")
        s_done = sem("group_done")
        with nc.Block() as block:

            @block.sync
            def _(sp):
                sp.dma_start(kf[:, :], io["L1_gnn_kernel"]).then_inc(s_par, 16)
                sp.dma_start(bias[:, :], io["L1_gnn_bias"].partition_broadcast(P)).then_inc(s_par, 16)
                sp.dma_start(beta[:, :], io["L1_gnn_beta"]).then_inc(s_par, 16)
                with sp.Fori(0, NG) as g:
                    for q in range(NQ):
                        n = g * NQ + q
                        sp.wait_ge(s_al, n + 1)
                        sp.wait_ge(s_alp, n + 1)
                        sp.dma_start(adj[:, q, :, :], io["adj"][bass.ds(n, 1)].squeeze(0)).then_inc(s_adj[q], 16)

            @block.gpsimd
            def _(pool):
                pool.sem_inc(s_alp, NQ)
                nc.gpsimd.memset(ry[:, :, 0, P:W], 1.0)
                nc.gpsimd.memset(ry[:, :, 1, P:W], 0.0).then_inc(s_one, 1)
                pool.wait_ge(s_par, 48)
                pool.wait_ge(s_n, NG)
                for g in range(NG):
                    nc.gpsimd.tensor_tensor(tiles(x, g), tiles(x, g), bias[:, None, :].to_broadcast([P, TPG, P]),
                                            ALU.add).then_inc(s_xb, 1)
                with pool.Fori(0, NG) as g:
                    for q in range(NQ):
                        pool.wait_ge(s_ah, g * NQ + (q + 1))
                        nc.gpsimd.tensor_tensor(al[:, q % RING, CV:CJ], adj[:, q, CV:CJ], ah[:, q % RING, CV:CJ],
                                                ALU.subtract).then_inc(s_alp, 1)

            @block.scalar
            def _(act):

                def copy_y(g):
                    act.wait_ge(s_y, g + 1)
                    yb = bank[g % 4][:, :].rearrange("p (t f) -> p t f", f=P)
                    nc.scalar.activation(tiles(ry, g)[:, :, 0, 0:P], yb, ACT.Copy, scale=1.0 / SC).then_inc(s_yh, 1)
                    nc.scalar.activation(tiles(ys, g), yb, ACT.Copy, scale=1.0 / SC).then_inc(s_yc, 1)

                act.sem_inc(s_acc, 1)
                split_scalar(core, s, norm, spare, copy_y)

                def parts(g, q0, q1):
                    for q in range(q0, q1):
                        act.wait_ge(s_adj[q], g * 16 + 16)
                        act.wait_ge(s_pe, g * NQ + (q + 1))
                        nc.scalar.activation(ah[:, q % RING], adj[:, q], ACT.Copy).then_inc(s_ah, 1)

                def copy_out(g):
                    act.wait_ge(s_pe, g * NQ + (RING + NQ))
                    act.wait_ge(s_done, g + 1)
                    for t in range(TPG):
                        ins = nc.scalar.activation(acc[:, t, :], bank[t][:, 0:2 * W], ACT.Copy)
                    ins.then_inc(s_acc, 1)

                parts(0, 0, AHEAD)
                with act.Fori(0, NG - 1) as g:
                    parts(g, AHEAD, NQ)
                    parts(g + 1, 0, AHEAD)
                    copy_out(g)
                parts(NG - 1, AHEAD, NQ)
                copy_out(NG - 1)

            @block.vector
            def _(dve):
                dve.sem_inc(s_al, NQ)
                dve.sem_inc(s_done, 1)

                def split_kernel():
                    dve.wait_ge(s_par, 48)
                    V.link(nc.vector.tensor_scalar(ks[:, 0, :], kf[:, :], SC, None, ALU.mult))
                    nc.vector.scalar_tensor_tensor(out=ks[:, 1, :], in0=kf[:, :], scalar=SC, in1=ks[:, 0, :],
                                                   op0=ALU.mult, op1=ALU.subtract).then_inc(s_ks, 1)

                def lo_y(g):
                    dve.wait_ge(s_yh, g + 1)
                    dve.wait_ge(s_yc, g + 1)
                    r = tiles(ry, g)
                    nc.vector.tensor_tensor(r[:, :, 1, 0:P], tiles(ys, g), r[:, :, 0, 0:P], ALU.subtract).then_inc(s_yl, 1)

                split_vector(core, s, split_kernel, lo_y)

                def parts(g, q0, q1):
                    for q in range(q0, q1):
                        dve.wait_ge(s_ah, g * NQ + (q + 1))
                        nc.vector.tensor_tensor(al[:, q % RING, 0:CV], adj[:, q, 0:CV], ah[:, q % RING, 0:CV], ALU.subtract).then_inc(s_al, 1)

                def post(g):
                    dve.wait_ge(s_acc, g + 2)
                    V.link(nc.vector.tensor_tensor(num[:, :, :], acc[:, :, 0:W], acc[:, :, W:2 * W], ALU.add))
                    V.link(nc.vector.tensor_tensor(sc[:, :], num[:, :, P], tiles(beta, g), ALU.add))
                    V.link(nc.vector.reciprocal(sc[:, :], sc[:, :]))
                    V.tick(nc.vector.tensor_scalar(sc[:, :], sc[:, :], 1.0 / SC, None, ALU.mult))
                    for k in range(TPG):
                        t = g * TPG + k
                        ins = nc.vector.scalar_tensor_tensor(out=num[:, k, 0:P], in0=ys[:, t, :], scalar=beta[:, bass.ds(t, 1)],
                                                             in1=num[:, k, 0:P], op0=ALU.mult, op1=ALU.add)
                    V.link(ins)
                    for k in range(TPG):
                        t = g * TPG + k
                        ins = nc.vector.scalar_tensor_tensor(out=x[:, t, :], in0=num[:, k, 0:P], scalar=sc[:, k:k + 1],
                                                             in1=x[:, t, :], op0=ALU.mult, op1=ALU.add)
                    V.link(ins)
                    core.stats_of_group(g)

                parts(0, 0, AHEAD)
                dve.wait_ge(s_xb, NG)
                with dve.Fori(0, NG - 1) as g:
                    V.loop(g, 7)
                    parts(g, AHEAD, NQ)
                    parts(g + 1, 0, AHEAD)
                    post(g)
                    dve.sem_inc(s_done, 1)
                V.end(NG - 1)
                parts(NG - 1, AHEAD, NQ)
                post(NG - 1)
                V.wait()

            @block.tensor
            def _(pe):
                pe.sem_inc(s_pe, RING)

                def sums_y(g):
                    if g == 0:
                        pe.wait_ge(s_ks, 1)
                    if g >= 4:
                        pe.wait_ge(s_yc, g - 3)
                    for k in range(TPG):
                        for i, (h, w) in enumerate(((0, 0), (0, 1), (1, 0))):
                            mm = nc.tensor.matmul(bank[g % 4][:, k * P:(k + 1) * P], xt[:, h, g * GW + k * P:g * GW + (k + 1) * P],
                                                  ks[:, w, :], start=(i == 0), stop=(i == 2))
                    mm.then_inc(s_y, 1)

                split_tensor(core, s, spare, sums_y)
                pe.wait_ge(s_yl, NG)
                pe.wait_ge(s_one, 1)
                with pe.Fori(0, NG) as g:
                    pe.wait_ge(s_acc, g + 1)
                    for jt in range(NT):
                        q = jt // CJ
                        if jt % CJ == 0:
                            pe.wait_ge(s_al, g * NQ + (q + 1 + NQ))
                            pe.wait_ge(s_alp, g * NQ + (q + 1 + NQ))
                        for t in range(TPG):
                            for part in range(2):
                                mm = nc.tensor.matmul(
                                    bank[t][:, 0:W if part else 2 * W],
                                    (ah, al)[part][:, q % RING, jt % CJ, t * P:(t + 1) * P],
                                    ry[:, jt, 0, :] if part else ry[:, jt, :, :].rearrange("p h w -> p (h w)"),
                                    start=(jt == 0 and part == 0), stop=(jt == NT - 1 and part == 1), skip_group_check=True)
                        if jt % CJ == CJ - 1:
                            mm.then_inc(s_pe, 1)


NAMES = ["x", "adj", "L0_gnn_h0", "L0_gnn_a", "L0_gnn_temp", "L0_ffn_Wg", "L0_ffn_bg", "L0_ffn_W1", "L0_ffn_b1",
         "L0_ffn_W2", "L0_ffn_b2", "L1_gnn_kernel", "L1_gnn_bias", "L1_gnn_beta", "L1_ffn_Wr", "L1_ffn_W1", "L1_ffn_b1",
         "L1_ffn_W2", "L1_ffn_b2"]


def build(nc, io, out):
    f1_row = nc.dram_tensor("f1_row", [NG, GW], F32).ap()
    x_rows = [nc.dram_tensor(f"x_rows{h}", [SLOTS, 2 * P], F16).ap() for h in range(HALVES)]
    y_rows = [nc.dram_tensor(f"y_rows{h}", [SLOTS, P], F32).ap() for h in range(HALVES)]
    with ExitStack() as ctx:
        core = Core(nc, ctx)
        attention(core, io, f1_row, x_rows)
        experts(core, "a", 0, io["L0_ffn_Wg"], io["L0_ffn_bg"], io["L0_ffn_W1"], io["L0_ffn_b1"],
                io["L0_ffn_W2"], io["L0_ffn_b2"], x_rows, y_rows, None)
        aggregate(core, io)
        experts(core, "b", 1, io["L1_ffn_Wr"], None, io["L1_ffn_W1"], io["L1_ffn_b1"],
                io["L1_ffn_W2"], io["L1_ffn_b2"], x_rows, y_rows, out)


def kernel(**inputs):
    import numpy as np
    import concourse.bacc as bacc
    from concourse import mybir as mb
    from concourse.bass_utils import run_bass_kernel_spmd

    v = {n: np.asarray(a) for n, a in inputs.items()}

    def by_tile(a):
        return a.reshape(NT, P, P).transpose(1, 0, 2)

    def hidden_bias(a):
        return a.reshape(-1, HC, P).transpose(2, 0, 1)

    def second_weight(a):
        return a.reshape(-1, HC, P, P).transpose(0, 2, 1, 3).reshape(-1, P, HC * P)

    laid = {
        "x": by_tile(v["x"]),
        "adj": v["adj"].reshape(NG, GW, NQ, CJ, P).transpose(0, 2, 4, 3, 1).reshape(NC, P, CJ, GW),
        "L0_gnn_h0": by_tile(v["L0_gnn_h0"]),
        "L0_gnn_a": v["L0_gnn_a"].reshape(2, P).T,
        "L0_gnn_temp": v["L0_gnn_temp"],
        "L0_ffn_Wg": v["L0_ffn_Wg"], "L0_ffn_bg": v["L0_ffn_bg"],
        "L0_ffn_W1": v["L0_ffn_W1"], "L0_ffn_b1": hidden_bias(v["L0_ffn_b1"]),
        "L0_ffn_W2": second_weight(v["L0_ffn_W2"]), "L0_ffn_b2": v["L0_ffn_b2"],
        "L1_gnn_kernel": v["L1_gnn_kernel"], "L1_gnn_bias": v["L1_gnn_bias"],
        "L1_gnn_beta": v["L1_gnn_beta"].reshape(NT, P).T,
        "L1_ffn_Wr": v["L1_ffn_Wr"],
        "L1_ffn_W1": np.concatenate([v["L1_ffn_W1s"][None], v["L1_ffn_W1p"]]),
        "L1_ffn_b1": hidden_bias(np.concatenate([v["L1_ffn_b1s"][None], v["L1_ffn_b1p"]])),
        "L1_ffn_W2": second_weight(np.concatenate([v["L1_ffn_W2s"][None], v["L1_ffn_W2p"]])),
        "L1_ffn_b2": np.concatenate([v["L1_ffn_b2s"][None], v["L1_ffn_b2p"]]),
    }
    nc = bacc.Bacc("TRN2", target_bir_lowering=False, num_devices=1)
    arrays, io = {}, {}
    for name in NAMES:
        a = np.ascontiguousarray(laid[name])
        arrays[f"in_{name}"] = a
        io[name] = nc.dram_tensor(f"in_{name}", a.shape, mb.dt.from_np(a.dtype), kind="ExternalInput").ap()
    out = nc.dram_tensor("out_0", (P, NT, P), mb.dt.float32, kind="ExternalOutput").ap()
    build(nc, io, out)
    r = run_bass_kernel_spmd(nc, [arrays], core_ids=[0])
    return np.ascontiguousarray(r.results[0]["out_0"].transpose(1, 0, 2)).reshape(N, P)
```
